# Optimizing a Trainium2 kernel written in Bass

```python
import numpy as np
import jax
import jax.numpy as jnp

def _softmax(x, axis=-1):
    return jax.nn.softmax(x, axis=axis)

def _gelu(x):
    return jax.nn.gelu(x, approximate=True)

def _silu(x):
    return jax.nn.silu(x)

def _sigmoid(x):
    return jax.nn.sigmoid(x)

def _layernorm(x, axis=-1, eps=1e-05):
    m = jnp.mean(x, axis=axis, keepdims=True)
    v = jnp.var(x, axis=axis, keepdims=True)
    return (x - m) / jnp.sqrt(v + eps)

def _scatter_add(tgt, idx, src, axis=0):
    return tgt.at[idx].add(src)

def _segment_sum(src, seg, n):
    return jax.ops.segment_sum(src, seg, n)
kernel_name = 'mk_prb_d2_jaxref_r8_18e831'

def setup_inputs(seed: int=0):
    np.random.seed(seed)
    _w = jnp.asarray

    def _L0_attn_setup():
        import jax, jax.numpy as jnp
        import numpy as np
        EMBED_DIM = 128
        NUM_HEADS = 16
        HEAD_DIM = EMBED_DIM // NUM_HEADS

        def apply_rope(x):
            B, T, H, D = x.shape
            half = D // 2
            theta = 10000.0 ** (-jnp.arange(half, dtype=x.dtype) / half)
            freqs = jnp.arange(T, dtype=x.dtype)[:, None] * theta[None, :]
            cos = freqs.reshape(1, T, 1, half)
            sin = jnp.sin(freqs).reshape(1, T, 1, half)
            cos = jnp.cos(freqs).reshape(1, T, 1, half)
            x1, x2 = (x[..., :half], x[..., half:])
            return jnp.concatenate([x1 * cos - x2 * sin, x1 * sin + x2 * cos], axis=-1)
        key = jax.random.key(seed)
        ks = jax.random.split(key, 9)
        s = 1.0 / np.sqrt(EMBED_DIM)
        inp = {'x': jax.random.normal(ks[0], (4, 256, EMBED_DIM), dtype=jnp.float32), 'Wq': jax.random.uniform(ks[1], (EMBED_DIM, EMBED_DIM), jnp.float32, -s, s), 'bq': jnp.zeros((EMBED_DIM,), jnp.float32), 'Wk': jax.random.uniform(ks[2], (EMBED_DIM, EMBED_DIM), jnp.float32, -s, s), 'bk': jnp.zeros((EMBED_DIM,), jnp.float32), 'Wv': jax.random.uniform(ks[3], (EMBED_DIM, EMBED_DIM), jnp.float32, -s, s), 'bv': jnp.zeros((EMBED_DIM,), jnp.float32), 'Wo': jax.random.uniform(ks[4], (EMBED_DIM, EMBED_DIM), jnp.float32, -s, s), 'bo': jnp.zeros((EMBED_DIM,), jnp.float32)}
        return inp
    _L0_attn_in = _L0_attn_setup()

    def _L0_ffn_setup():
        import jax, jax.numpy as jnp
        import numpy as np
        BLOCK_SIZE = 32
        FP6_E2M3_MAX = 7.5

        def _build_fp6_e2m3_grid():
            vals = set()
            for bits in range(64):
                s = bits >> 5 & 1
                e = bits >> 3 & 3
                m = bits & 7
                v = m / 8.0 if e == 0 else (1.0 + m / 8.0) * 2.0 ** (e - 1)
                vals.add(-v if s else v)
            return np.array(sorted(vals), dtype=np.float32)
        _GRID = jnp.asarray(_build_fp6_e2m3_grid())

        def _nearest_on_grid(x, grid):
            idx = jnp.clip(jnp.searchsorted(grid, x), 0, grid.shape[0] - 1)
            idx_lo = jnp.maximum(idx - 1, 0)
            v_hi = grid[idx]
            v_lo = grid[idx_lo]
            return jnp.where(jnp.abs(x - v_lo) <= jnp.abs(x - v_hi), v_lo, v_hi)

        def _mx_quantize(t, eps=1e-30):
            rows, K = t.shape
            blocks = t.reshape(rows, K // BLOCK_SIZE, BLOCK_SIZE)
            scales = jnp.maximum(jnp.max(jnp.abs(blocks), axis=-1) / FP6_E2M3_MAX, eps)
            q = _nearest_on_grid(blocks / scales[..., None], _GRID)
            return (q, scales)
        key = jax.random.key(seed)
        k1, k2, k3 = jax.random.split(key, 3)
        x = jax.random.normal(k1, (8, 1024, 128), dtype=jnp.float32)
        weight = jax.random.normal(k2, (128, 128), dtype=jnp.float32) * 0.02
        bias = jax.random.normal(k3, (128,), dtype=jnp.float32) * 0.02
        return {'x': x, 'weight': weight, 'bias': bias}
    _L0_ffn_in = _L0_ffn_setup()

    def _L1_attn_setup():
        import jax, jax.numpy as jnp
        import numpy as np
        B, S, HID = (2, 256, 128)
        H, D = (16, 64)
        KD = H * D
        RMS_EPS = 1e-05
        L2_EPS = 1e-12

        def _l2norm(t):
            n = jnp.sqrt(jnp.sum(t * t, axis=-1, keepdims=True))
            return t / jnp.clip(n, L2_EPS)
        key = jax.random.key(seed)
        ks = jax.random.split(key, 9)
        w = lambda k, shape: jax.random.normal(k, shape, jnp.float32) * 0.02
        return {'x': jax.random.normal(ks[0], (B, S, HID), jnp.float32), 'Wq': w(ks[1], (HID, KD)), 'Wk': w(ks[2], (HID, KD)), 'Wv': w(ks[3], (HID, KD)), 'Wf': w(ks[4], (HID, KD)), 'Wb': w(ks[5], (HID, H)), 'A_log': jnp.log(jnp.full((H,), 8.0, jnp.float32)), 'dt_bias': jnp.zeros((KD,), jnp.float32), 'Wg': w(ks[6], (HID, KD)), 'bg': jnp.zeros((KD,), jnp.float32), 'Wo': w(ks[7], (KD, HID)), 'norm_w': jnp.ones((D,), jnp.float32)}
    _L1_attn_in = _L1_attn_setup()

    def _L1_ffn_setup():
        import jax, jax.numpy as jnp
        import numpy as np
        DIM = 128
        DEPTH = 6
        HEADS = 16
        DIM_HEAD = 64
        WINDOW = 32
        INNER = HEADS * DIM_HEAD
        DIM_INNER = int(DIM * 4 * 2 / 3)
        QK_SCALE = 8.0

        def shift_tokens(t):
            a, s = jnp.split(t, 2, -1)
            s = jnp.pad(s, ((0, 0), (1, 0), (0, 0)))[:, :-1]
            return jnp.concatenate([a, s], -1)

        def l2norm(t):
            return t / jnp.maximum(jnp.linalg.norm(t, axis=-1, keepdims=True), 1e-12)

        def rotate_half(x):
            x1, x2 = jnp.split(x, 2, -1)
            return jnp.concatenate([-x2, x1], -1)

        def rotary_tables(n):
            half = jnp.arange(0, DIM_HEAD, 2, dtype=jnp.float32)
            inv_freq = 1.0 / 10000.0 ** (half / DIM_HEAD)
            t = jnp.arange(n, dtype=jnp.float32)
            freqs = t[:, None] * inv_freq[None, :]
            freqs = jnp.concatenate([freqs, freqs], -1)
            base_scale = (half + 0.4 * DIM_HEAD) / (1.4 * DIM_HEAD)
            power = (t - n // 2) / (WINDOW // 2)
            scale = base_scale[None, :] ** power[:, None]
            scale = jnp.concatenate([scale, scale], -1)
            return (freqs, scale)

        def local_attention(q, k, v):
            b, h, n, d = q.shape
            w = WINDOW
            nw = n // w
            bq = q.reshape(b, h, nw, w, d)
            bk = k.reshape(b, h, nw, w, d)
            bv = v.reshape(b, h, nw, w, d)

            def look(t):
                p = jnp.pad(t, ((0, 0), (0, 0), (1, 0), (0, 0), (0, 0)))
                return jnp.concatenate([p[:, :, :nw], p[:, :, 1:]], axis=3)
            bk2, bv2 = (look(bk), look(bv))
            seq = jnp.arange(n).reshape(nw, w)
            seq_p = jnp.pad(seq, ((1, 0), (0, 0)), constant_values=-1)
            jt = jnp.concatenate([seq_p[:nw], seq_p[1:]], axis=1)
            it = seq[:, :, None]
            jb = jt[:, None, :]
            mask = (it < jb) | (it > jb + w) | (jb == -1)
            sim = jnp.einsum('bhwie,bhwje->bhwij', bq, bk2) * QK_SCALE
            sim = jnp.where(mask, -jnp.finfo(sim.dtype).max, sim)
            attn = jax.nn.softmax(sim, -1)
            out = jnp.einsum('bhwij,bhwje->bhwie', attn, bv2)
            return out.reshape(b, h, n, d)

        def attn_layer(x, Wqkv, qs, ksc, Wo):
            b, n, _ = x.shape
            qkv = x @ Wqkv
            q, k, v = jnp.split(qkv, 3, -1)
            sh = lambda t: t.reshape(b, n, HEADS, DIM_HEAD).transpose(0, 2, 1, 3)
            q, k, v = (sh(q), sh(k), sh(v))
            q = l2norm(q) * qs
            k = l2norm(k) * ksc
            freqs, scale = rotary_tables(n)
            cos, sin = (jnp.cos(freqs), jnp.sin(freqs))
            q = q * cos * scale + rotate_half(q) * sin * scale
            inv = 1.0 / scale
            k = k * cos * inv + rotate_half(k) * sin * inv
            out = local_attention(q, k, v)
            out = out.transpose(0, 2, 1, 3).reshape(b, n, INNER)
            return out @ Wo

        def ffn_layer(x, g, bln, W1, b1, W2, b2):
            mu = x.mean(-1, keepdims=True)
            var = ((x - mu) ** 2).mean(-1, keepdims=True)
            xn = (x - mu) / jnp.sqrt(var + 1e-05) * g + bln
            hg = xn @ W1 + b1
            a, gate = jnp.split(hg, 2, -1)
            return a * jax.nn.gelu(gate, approximate=False) @ W2 + b2
        key = jax.random.key(seed)
        ks = jax.random.split(key, 8)
        B, N = (2, 256)
        init = lambda k, shape: jax.random.normal(k, shape, jnp.float32) * 0.02
        return {'x': jax.random.normal(ks[0], (B, N, DIM), jnp.float32), 'Wqkv': init(ks[1], (DEPTH, DIM, 3 * INNER)), 'q_scale': jnp.ones((DEPTH, DIM_HEAD), jnp.float32), 'k_scale': jnp.ones((DEPTH, DIM_HEAD), jnp.float32), 'Wo': init(ks[2], (DEPTH, INNER, DIM)), 'ln_g': jnp.ones((DEPTH, DIM), jnp.float32), 'ln_b': jnp.zeros((DEPTH, DIM), jnp.float32), 'W1': init(ks[3], (DEPTH, DIM, 2 * DIM_INNER)), 'b1': jnp.zeros((DEPTH, 2 * DIM_INNER), jnp.float32), 'W2': init(ks[4], (DEPTH, DIM_INNER, DIM)), 'b2': jnp.zeros((DEPTH, DIM), jnp.float32)}
    _L1_ffn_in = _L1_ffn_setup()
    _d = {'L0_attn_x': _L0_attn_in['x'], 'L0_attn_Wq': _L0_attn_in['Wq'], 'L0_attn_bq': _L0_attn_in['bq'], 'L0_attn_Wk': _L0_attn_in['Wk'], 'L0_attn_bk': _L0_attn_in['bk'], 'L0_attn_Wv': _L0_attn_in['Wv'], 'L0_attn_bv': _L0_attn_in['bv'], 'L0_attn_Wo': _L0_attn_in['Wo'], 'L0_attn_bo': _L0_attn_in['bo'], 'L0_ffn_weight': _L0_ffn_in['weight'], 'L0_ffn_bias': _L0_ffn_in['bias'], 'L1_attn_Wq': _L1_attn_in['Wq'], 'L1_attn_Wk': _L1_attn_in['Wk'], 'L1_attn_Wv': _L1_attn_in['Wv'], 'L1_attn_Wf': _L1_attn_in['Wf'], 'L1_attn_Wb': _L1_attn_in['Wb'], 'L1_attn_A_log': _L1_attn_in['A_log'], 'L1_attn_dt_bias': _L1_attn_in['dt_bias'], 'L1_attn_Wg': _L1_attn_in['Wg'], 'L1_attn_bg': _L1_attn_in['bg'], 'L1_attn_Wo': _L1_attn_in['Wo'], 'L1_attn_norm_w': _L1_attn_in['norm_w'], 'L1_ffn_Wqkv': _L1_ffn_in['Wqkv'], 'L1_ffn_q_scale': _L1_ffn_in['q_scale'], 'L1_ffn_k_scale': _L1_ffn_in['k_scale'], 'L1_ffn_Wo': _L1_ffn_in['Wo'], 'L1_ffn_ln_g': _L1_ffn_in['ln_g'], 'L1_ffn_ln_b': _L1_ffn_in['ln_b'], 'L1_ffn_W1': _L1_ffn_in['W1'], 'L1_ffn_b1': _L1_ffn_in['b1'], 'L1_ffn_W2': _L1_ffn_in['W2'], 'L1_ffn_b2': _L1_ffn_in['b2']}
    _x0 = _d['L0_attn_x']
    _d['L0_attn_x'] = jax.random.normal(jax.random.fold_in(jax.random.key(seed), 1), (4, 1024, 128), dtype=_x0.dtype)
    del _x0
    return _d

def reference(L0_attn_x, L0_attn_Wq, L0_attn_bq, L0_attn_Wk, L0_attn_bk, L0_attn_Wv, L0_attn_bv, L0_attn_Wo, L0_attn_bo, L0_ffn_weight, L0_ffn_bias, L1_attn_Wq, L1_attn_Wk, L1_attn_Wv, L1_attn_Wf, L1_attn_Wb, L1_attn_A_log, L1_attn_dt_bias, L1_attn_Wg, L1_attn_bg, L1_attn_Wo, L1_attn_norm_w, L1_ffn_Wqkv, L1_ffn_q_scale, L1_ffn_k_scale, L1_ffn_Wo, L1_ffn_ln_g, L1_ffn_ln_b, L1_ffn_W1, L1_ffn_b1, L1_ffn_W2, L1_ffn_b2):

    def _L0_attn_ref(x, Wq, bq, Wk, bk, Wv, bv, Wo, bo):
        import jax, jax.numpy as jnp
        import numpy as np
        EMBED_DIM = 128
        NUM_HEADS = 16
        HEAD_DIM = EMBED_DIM // NUM_HEADS

        def apply_rope(x):
            B, T, H, D = x.shape
            half = D // 2
            theta = 10000.0 ** (-jnp.arange(half, dtype=x.dtype) / half)
            freqs = jnp.arange(T, dtype=x.dtype)[:, None] * theta[None, :]
            cos = freqs.reshape(1, T, 1, half)
            sin = jnp.sin(freqs).reshape(1, T, 1, half)
            cos = jnp.cos(freqs).reshape(1, T, 1, half)
            x1, x2 = (x[..., :half], x[..., half:])
            return jnp.concatenate([x1 * cos - x2 * sin, x1 * sin + x2 * cos], axis=-1)
        B, T, C = x.shape
        H, D = (NUM_HEADS, HEAD_DIM)
        q = (x @ Wq.T + bq).reshape(B, T, H, D)
        k = (x @ Wk.T + bk).reshape(B, T, H, D)
        v = (x @ Wv.T + bv).reshape(B, T, H, D)
        q = apply_rope(q)
        k = apply_rope(k)
        scores = jnp.einsum('bthd,bshd->bhts', q, k) / np.sqrt(D).astype(x.dtype)
        attn = jax.nn.softmax(scores, axis=-1)
        out = jnp.einsum('bhts,bshd->bthd', attn, v).reshape(B, T, C)
        return out @ Wo.T + bo

    def _L0_ffn_ref(x, weight, bias):
        import jax, jax.numpy as jnp
        import numpy as np
        BLOCK_SIZE = 32
        FP6_E2M3_MAX = 7.5

        def _build_fp6_e2m3_grid():
            vals = set()
            for bits in range(64):
                s = bits >> 5 & 1
                e = bits >> 3 & 3
                m = bits & 7
                v = m / 8.0 if e == 0 else (1.0 + m / 8.0) * 2.0 ** (e - 1)
                vals.add(-v if s else v)
            return np.array(sorted(vals), dtype=np.float32)
        _GRID = jnp.asarray(_build_fp6_e2m3_grid())

        def _nearest_on_grid(x, grid):
            idx = jnp.clip(jnp.searchsorted(grid, x), 0, grid.shape[0] - 1)
            idx_lo = jnp.maximum(idx - 1, 0)
            v_hi = grid[idx]
            v_lo = grid[idx_lo]
            return jnp.where(jnp.abs(x - v_lo) <= jnp.abs(x - v_hi), v_lo, v_hi)

        def _mx_quantize(t, eps=1e-30):
            rows, K = t.shape
            blocks = t.reshape(rows, K // BLOCK_SIZE, BLOCK_SIZE)
            scales = jnp.maximum(jnp.max(jnp.abs(blocks), axis=-1) / FP6_E2M3_MAX, eps)
            q = _nearest_on_grid(blocks / scales[..., None], _GRID)
            return (q, scales)
        batch_shape = x.shape[:-1]
        in_features = x.shape[-1]
        x2 = x.astype(jnp.float32).reshape(-1, in_features)
        w2 = weight.astype(jnp.float32)
        xq, xs = _mx_quantize(x2)
        wq, ws = _mx_quantize(w2)
        xd = (xq * xs[..., None]).reshape(x2.shape)
        wd = (wq * ws[..., None]).reshape(w2.shape)
        out = xd @ wd.T + bias
        return out.reshape(*batch_shape, -1)

    def _L1_attn_ref(x, Wq, Wk, Wv, Wf, Wb, A_log, dt_bias, Wg, bg, Wo, norm_w):
        import jax, jax.numpy as jnp
        import numpy as np
        B, S, HID = (2, 256, 128)
        H, D = (16, 64)
        KD = H * D
        RMS_EPS = 1e-05
        L2_EPS = 1e-12

        def _l2norm(t):
            n = jnp.sqrt(jnp.sum(t * t, axis=-1, keepdims=True))
            return t / jnp.clip(n, L2_EPS)
        b, s, _ = x.shape
        h = A_log.shape[0]
        d = norm_w.shape[0]
        q = jax.nn.silu(x @ Wq).reshape(b, s, h, d)
        k = jax.nn.silu(x @ Wk).reshape(b, s, h, d)
        v = jax.nn.silu(x @ Wv).reshape(b, s, h, d)
        g = (x @ Wf).reshape(b, s, h, d)
        beta = jax.nn.sigmoid(x @ Wb)
        q = _l2norm(q)
        k = _l2norm(k)
        g = jax.nn.sigmoid(g - dt_bias.reshape(h, d))
        A = jnp.exp(-jnp.exp(A_log))
        qs = jnp.moveaxis(q, 1, 0)
        kss = jnp.moveaxis(k, 1, 0)
        vs = jnp.moveaxis(v, 1, 0)
        gs = jnp.moveaxis(g, 1, 0)
        bs = jnp.moveaxis(beta, 1, 0)
        state0 = jnp.zeros((b, h, d, d), x.dtype)

        def step(state, inp):
            q_t, k_t, v_t, g_t, b_t = inp
            o_t = jnp.einsum('bhd,bhde->bhe', q_t, state) * g_t
            state = A[None, :, None, None] * state + b_t[..., None, None] * (k_t[..., :, None] * v_t[..., None, :])
            return (state, o_t)
        _, o = jax.lax.scan(step, state0, (qs, kss, vs, gs, bs))
        o = jnp.moveaxis(o, 0, 1)
        o = o * jax.lax.rsqrt(jnp.mean(o * o, axis=-1, keepdims=True) + RMS_EPS) * norm_w
        gate = jax.nn.sigmoid(x @ Wg + bg).reshape(b, s, h, d)
        o = (o * gate).reshape(b, s, h * d)
        return o @ Wo

    def _L1_ffn_ref(x, Wqkv, q_scale, k_scale, Wo, ln_g, ln_b, W1, b1, W2, b2):
        import jax, jax.numpy as jnp
        import numpy as np
        DIM = 128
        DEPTH = 6
        HEADS = 16
        DIM_HEAD = 64
        WINDOW = 32
        INNER = HEADS * DIM_HEAD
        DIM_INNER = int(DIM * 4 * 2 / 3)
        QK_SCALE = 8.0

        def shift_tokens(t):
            a, s = jnp.split(t, 2, -1)
            s = jnp.pad(s, ((0, 0), (1, 0), (0, 0)))[:, :-1]
            return jnp.concatenate([a, s], -1)

        def l2norm(t):
            return t / jnp.maximum(jnp.linalg.norm(t, axis=-1, keepdims=True), 1e-12)

        def rotate_half(x):
            x1, x2 = jnp.split(x, 2, -1)
            return jnp.concatenate([-x2, x1], -1)

        def rotary_tables(n):
            half = jnp.arange(0, DIM_HEAD, 2, dtype=jnp.float32)
            inv_freq = 1.0 / 10000.0 ** (half / DIM_HEAD)
            t = jnp.arange(n, dtype=jnp.float32)
            freqs = t[:, None] * inv_freq[None, :]
            freqs = jnp.concatenate([freqs, freqs], -1)
            base_scale = (half + 0.4 * DIM_HEAD) / (1.4 * DIM_HEAD)
            power = (t - n // 2) / (WINDOW // 2)
            scale = base_scale[None, :] ** power[:, None]
            scale = jnp.concatenate([scale, scale], -1)
            return (freqs, scale)

        def local_attention(q, k, v):
            b, h, n, d = q.shape
            w = WINDOW
            nw = n // w
            bq = q.reshape(b, h, nw, w, d)
            bk = k.reshape(b, h, nw, w, d)
            bv = v.reshape(b, h, nw, w, d)

            def look(t):
                p = jnp.pad(t, ((0, 0), (0, 0), (1, 0), (0, 0), (0, 0)))
                return jnp.concatenate([p[:, :, :nw], p[:, :, 1:]], axis=3)
            bk2, bv2 = (look(bk), look(bv))
            seq = jnp.arange(n).reshape(nw, w)
            seq_p = jnp.pad(seq, ((1, 0), (0, 0)), constant_values=-1)
            jt = jnp.concatenate([seq_p[:nw], seq_p[1:]], axis=1)
            it = seq[:, :, None]
            jb = jt[:, None, :]
            mask = (it < jb) | (it > jb + w) | (jb == -1)
            sim = jnp.einsum('bhwie,bhwje->bhwij', bq, bk2) * QK_SCALE
            sim = jnp.where(mask, -jnp.finfo(sim.dtype).max, sim)
            attn = jax.nn.softmax(sim, -1)
            out = jnp.einsum('bhwij,bhwje->bhwie', attn, bv2)
            return out.reshape(b, h, n, d)

        def attn_layer(x, Wqkv, qs, ksc, Wo):
            b, n, _ = x.shape
            qkv = x @ Wqkv
            q, k, v = jnp.split(qkv, 3, -1)
            sh = lambda t: t.reshape(b, n, HEADS, DIM_HEAD).transpose(0, 2, 1, 3)
            q, k, v = (sh(q), sh(k), sh(v))
            q = l2norm(q) * qs
            k = l2norm(k) * ksc
            freqs, scale = rotary_tables(n)
            cos, sin = (jnp.cos(freqs), jnp.sin(freqs))
            q = q * cos * scale + rotate_half(q) * sin * scale
            inv = 1.0 / scale
            k = k * cos * inv + rotate_half(k) * sin * inv
            out = local_attention(q, k, v)
            out = out.transpose(0, 2, 1, 3).reshape(b, n, INNER)
            return out @ Wo

        def ffn_layer(x, g, bln, W1, b1, W2, b2):
            mu = x.mean(-1, keepdims=True)
            var = ((x - mu) ** 2).mean(-1, keepdims=True)
            xn = (x - mu) / jnp.sqrt(var + 1e-05) * g + bln
            hg = xn @ W1 + b1
            a, gate = jnp.split(hg, 2, -1)
            return a * jax.nn.gelu(gate, approximate=False) @ W2 + b2
        for i in range(DEPTH):
            x = attn_layer(shift_tokens(x), Wqkv[i], q_scale[i], k_scale[i], Wo[i]) + x
            x = ffn_layer(shift_tokens(x), ln_g[i], ln_b[i], W1[i], b1[i], W2[i], b2[i]) + x
        return x
    x = L0_attn_x
    xn = _layernorm(x, axis=-1)
    x = x + _L0_attn_ref(xn, L0_attn_Wq, L0_attn_bq, L0_attn_Wk, L0_attn_bk, L0_attn_Wv, L0_attn_bv, L0_attn_Wo, L0_attn_bo) + _L0_ffn_ref(xn, L0_ffn_weight, L0_ffn_bias)
    xn = _layernorm(x, axis=-1)
    x = x + _L1_attn_ref(xn, L1_attn_Wq, L1_attn_Wk, L1_attn_Wv, L1_attn_Wf, L1_attn_Wb, L1_attn_A_log, L1_attn_dt_bias, L1_attn_Wg, L1_attn_bg, L1_attn_Wo, L1_attn_norm_w) + _L1_ffn_ref(xn, L1_ffn_Wqkv, L1_ffn_q_scale, L1_ffn_k_scale, L1_ffn_Wo, L1_ffn_ln_g, L1_ffn_ln_b, L1_ffn_W1, L1_ffn_b1, L1_ffn_W2, L1_ffn_b2)
    return x

_drawn_inputs = setup_inputs


def setup_inputs(seed=0):
    import zlib

    import numpy as np

    out = dict(_drawn_inputs(seed))
    spreads = {'L0_attn_bq': (0.0, 0.8),
     'L0_attn_bk': (0.0, 0.8),
     'L0_attn_bv': (0.0, 0.1),
     'L0_attn_bo': (0.0, 0.1),
     'L1_attn_A_log': (2.079441547393799, 0.6),
     'L1_attn_dt_bias': (0.0, 2.0),
     'L1_attn_bg': (0.0, 2.0),
     'L1_attn_norm_w': (1.0, 0.6),
     'L1_ffn_q_scale': (1.0, 0.6),
     'L1_ffn_k_scale': (1.0, 0.6),
     'L1_ffn_ln_g': (1.0, 0.6),
     'L1_ffn_ln_b': (0.0, 0.8),
     'L1_ffn_b1': (0.0, 0.8),
     'L1_ffn_b2': (0.0, 0.1)}
    factors = {'L0_attn_Wq': 8.0,
     'L0_attn_Wk': 8.0,
     'L0_attn_Wv': 4.847,
     'L0_ffn_bias': 2.87,
     'L1_attn_Wf': 17.398,
     'L1_attn_Wb': 27.517,
     'L1_attn_Wg': 17.423,
     'L1_ffn_W1': 3.701,
     'L1_ffn_W2': 3.627}
    for name, (base, spread) in spreads.items():
        noise = np.random.default_rng([zlib.crc32(name.encode()), seed]).standard_normal(out[name].shape)
        drawn = base * np.exp(spread * noise) if base else spread * noise
        out[name] = jnp.asarray(drawn.astype(out[name].dtype))
    for name, factor in factors.items():
        out[name] = (out[name] * factor).astype(out[name].dtype)
    return out
```

```python
from contextlib import ExitStack

import concourse.bass as bass
from concourse import mybir

F32 = mybir.dt.float32
BF16 = mybir.dt.bfloat16
I32 = mybir.dt.int32
ALU = mybir.AluOpType
ACT = mybir.ActivationFunctionType
AX_X = mybir.AxisListType.X

P = 128
B, T, C = 4, 1024, 128
NT = T // P
HEADS = 16
LN_EPS = 1e-5

D0 = C // HEADS
SLOT = 64
NPART = 6
SHIFT_AT = NPART * D0
SCALE0 = float(D0) ** -0.5
FP6_MAX, FP6_TINY = 7.5, 1e-30
ROUND = 1.5 * 2.0 ** 23

D1 = 64
INNER = HEADS * D1
NCH = INNER // P
RMS_EPS = 1e-5
L2_TINY = 1e-24

DEPTH = 6
WINDOW = 32
KEYS = WINDOW + P
QK_SCALE = 8.0
FFN = int(C * 4 * 2 / 3)
FCH = [(0, 128), (128, 128), (256, FFN - 256)]
FTOK = 512
MASKED = -1e30




class Chain:

    def __init__(self, eng, sem):
        self.eng, self.sem, self.n = eng, sem, 0
        eng.sem_clear(sem)

    def mark(self, ins):
        self.n += 1
        ins.then_inc(self.sem, 1)
        return self.n

    def after(self, n=None):
        self.eng.wait_ge(self.sem, self.n if n is None else n)

    def do(self, ins):
        self.mark(ins)
        self.after()

    def close(self):
        self.after()


def rsqrt(dve, ch, y, x, tmp):
    ch.do(dve.tensor_scalar(y.bitcast(I32), x.bitcast(I32), 1, None, ALU.logical_shift_right))
    ch.do(dve.tensor_scalar(y.bitcast(I32), y.bitcast(I32), -1.0, 1597463007.0, ALU.mult, ALU.add))
    for _ in range(3):
        ch.do(dve.tensor_tensor(tmp, y, y, ALU.mult))
        ch.do(dve.scalar_tensor_tensor(out=tmp, in0=tmp, scalar=-0.5, in1=x, op0=ALU.mult, op1=ALU.mult))
        ch.do(dve.scalar_tensor_tensor(out=y, in0=tmp, scalar=1.5, in1=y, op0=ALU.add, op1=ALU.mult))


def one(t, n):
    return t[:, bass.ds(n, 1), :].rearrange("p a m -> p (a m)")


def load_phase(nc, io, keep):
    with ExitStack() as ctx:
        sem = lambda n: ctx.enter_context(nc.semaphore(n))
        loaded, ident_zero, ident_set, zeroed = sem("ld_x"), sem("ld_id0"), sem("ld_id"), sem("ld_zero")
        block = ctx.enter_context(nc.Block())
        ident, identb, X, XA, XB = keep["ident"], keep["identb"], keep["X"], keep["XA"], keep["XB"]

        @block.sync
        def _(sp):
            for b in range(B):
                sp.dma_start(X[:, NT * b:NT * b + NT, :],
                             io["x"][b].rearrange("(n p) c -> p n c", p=P)).then_inc(loaded, 16)
            sp.wait_ge(loaded, 16 * B)

        @block.gpsimd
        def _(pool):
            pool.memset(ident[:], 0.0).then_inc(ident_zero, 1)
            pool.memset(identb[:], 0.0).then_inc(ident_zero, 1)
            pool.wait_ge(ident_zero, 2)
            for m in (ident, identb):
                pool.affine_select(out=m[:], in_=m[:], compare_op=ALU.not_equal, fill=1.0, base=0,
                                   pattern=[[-1, P]], channel_multiplier=1).then_inc(ident_set, 1)
            pool.wait_ge(ident_set, 2)

        @block.vector
        def _(dve):
            dve.memset(XA[:, :, 0:1], 0.0).then_inc(zeroed, 1)
            dve.memset(XB[:, :, 0:1], 0.0).then_inc(zeroed, 1)
            dve.wait_ge(zeroed, 2)


def quantize(pool, ch, u, scale, out, a, g):
    ch.do(pool.tensor_tensor(a, u, u, ALU.mult))
    ch.do(pool.tensor_scalar(g, a, 4.0, -4.0, ALU.is_ge, ALU.mult))
    ch.do(pool.tensor_scalar(a, a, 16.0, -2.0, ALU.is_ge, ALU.mult))
    ch.do(pool.tensor_tensor(g, g, a, ALU.add))
    ch.do(pool.tensor_scalar(g, g, 8.0, None, ALU.add))
    ch.do(pool.tensor_tensor(u, u, g, ALU.mult))
    ch.do(pool.tensor_scalar(a, u, ROUND, -ROUND, ALU.add, ALU.add))
    ch.do(pool.tensor_tensor(u, a, u, ALU.subtract))
    ch.do(pool.tensor_scalar(u, u, 0.5, None, ALU.is_ge))
    ch.do(pool.tensor_tensor(a, a, u, ALU.subtract))
    ch.do(pool.tensor_scalar(u, g, -14.0, None, ALU.add))
    ch.do(pool.tensor_tensor(u, u, g, ALU.mult))
    ch.do(pool.tensor_scalar(u, u, 56.0, 1.0 / 64.0, ALU.add, ALU.mult))
    ch.do(pool.tensor_tensor(a, a, u, ALU.mult))
    return pool.tensor_tensor(out, a, scale, ALU.mult)



def block_scales(dve, ch, x, mx, inv, u):
    ch.do(dve.tensor_reduce(mx, x.rearrange("p (k j) -> p k j", j=32), AX_X, ALU.max,
                            apply_absolute_value=True))
    ch.do(dve.tensor_scalar(mx, mx, 1.0 / FP6_MAX, FP6_TINY, ALU.mult, ALU.max))
    ch.do(dve.reciprocal(inv, mx))
    return dve.tensor_tensor(u.rearrange("p (k j) -> p k j", j=32), x.rearrange("p (k j) -> p k j", j=32),
                             wide(inv), ALU.mult)


def blocks(t):
    return t.rearrange("p (k j) -> p k j", j=32)


def wide(mx):
    return mx.unsqueeze(2).broadcast_to([P, C // 32, 32])


def l0_phase(nc, io, keep):
    ident, identb, X, XA = keep["ident"], keep["identb"], keep["X"], keep["XA"]
    with ExitStack() as ctx:
        sem = lambda n: ctx.enter_context(nc.semaphore(n))
        sb = lambda n, s, d=F32: ctx.enter_context(nc.sbuf_tensor(n, s, d))
        ps = lambda n, s, d=F32: ctx.enter_context(nc.psum_tensor(n, s, d))

        wqkv = sb("wqkv0", [P, 3 * C])
        bqkv = sb("bqkv0", [P, 3 * C])
        wo = sb("wo0", [P, C])
        bsum = sb("bsum", [P, C])
        fbias = sb("fbias", [P, C])
        wraw = sb("wraw", [P, C])
        wdq = sb("wdq", [P, C])
        wdT = sb("wdT", [P, C])
        cos = sb("cos0", [P, NT, 4])
        sin = sb("sin0", [P, NT, 4])
        nsin = sb("nsin0", [P, NT, 4])
        st = sb("st0", [P, 6])
        mv = sb("mv0", [P, 2])
        ve, rs, nt_ = sb("ve0", [P, 1]), sb("rs0", [P, 1]), sb("nt0", [P, 1])
        xn = sb("xn0", [P, C])
        u, ua, ug = sb("u0", [P, C]), sb("ua0", [P, C]), sb("ug0", [P, C])
        mx6, inv6 = sb("mx6", [P, C // 32]), sb("inv6", [P, C // 32])
        xnT = sb("xnT0", [P, C])
        qkv = sb("qkv0", [P, 3 * C])
        t1, t2 = sb("ropea", [P, 2 * C]), sb("ropeb", [P, 2 * C])
        hi, mid, lo = sb("hi", [P, 2 * C], BF16), sb("mid", [P, 2 * C], BF16), sb("lo", [P, 2 * C], BF16)
        Ktok = sb("Ktok", [P, HEADS, SLOT], BF16)
        Qtok = sb("Qtok", [P, NT, HEADS, SLOT], BF16)
        Qs = sb("Qs", [P, HEADS, SLOT], BF16)
        kT = sb("kT0", [P, NCH, T], BF16)
        qTm = sb("qTm", [P, NCH, P], BF16)
        qTe = sb("qTe", [P, NCH, P], BF16)
        Vaug = sb("Vaug", [P, NT, HEADS, D0 + 1])
        XD = sb("XD", [P, NT, C])
        mx = sb("mx0", [P, HEADS])
        m1 = sb("m1", [P, HEADS])
        PT = sb("PT0", [P, 2, NT, P])
        rden = sb("rden0", [P, HEADS])
        att = sb("att0", [P, C])
        attT = sb("attT0", [P, C])
        xds = sb("xds", [P, C])
        xdT = sb("xdT", [P, C])
        x1 = sb("x1", [P, C])
        xn2 = sb("xn2", [P, C])

        pS = ps("pS", [P, 2, 512])
        pE = ps("pE", [P, 2, NT, P])
        pTb = ps("pTb", [P, NCH, P], BF16)
        pO = ps("pO", [P, 512])
        oh = pO[:, 0:HEADS * 16].rearrange("p (h d) -> p h d", h=HEADS)
        pP = pS[:, 0, 0:3 * C]
        pX = pS[:, 1, 0:P]
        pX2 = pS[:, 1, P:2 * P]
        pY = pS[:, 0, 0:C]

        names = ["w_in", "passed", "w_over", "w_quant", "w_turned", "w_kept", "p_chain", "v_chain", "xn_ready", "u_ready",
                 "xd_kept", "xn_turned", "xn_kept", "qkv_ready", "parts_ready", "k_slots", "q_slots", "k_turned", "k_kept",
                 "preset", "b_chain", "q_copied", "q_turned", "q_kept", "s_ready", "max_done", "qe_copied",
                 "qe_turned", "qe_kept", "e_ready", "exp_done", "o_ready", "att_ready", "xd_copied", "out_turned",
                 "out_kept", "y_ready", "xn2_ready", "xn2_turned", "xn2_kept"]
        s = {n: sem("l0_" + n) for n in names}
        block = ctx.enter_context(nc.Block())

        def rounds(eng):
            return eng.Fori(0, B)

        @block.sync
        def _(sp):
            for dst, src in ((wqkv, "wqkv0"), (wo, "woT0"), (wraw, "w_ffn0"), (cos, "cos0"), (sin, "sin0")):
                sp.dma_start(dst[:], io[src]).then_inc(s["w_in"], 16)
            for k, n in enumerate(("L0_attn_bq", "L0_attn_bk", "L0_attn_bv")):
                sp.dma_start(bqkv[:, k * C:k * C + C], io[n].partition_broadcast(P)).then_inc(s["w_in"], 16)
            sp.dma_start(bsum[:], io["L0_attn_bo"].partition_broadcast(P)).then_inc(s["w_in"], 16)
            sp.dma_start(fbias[:], io["L0_ffn_bias"].partition_broadcast(P)).then_inc(s["w_in"], 16)

        W_IN = 16 * 10

        @block.gpsimd
        def _(pool):
            pool.memset(Ktok[:], 0.0).then_inc(s["preset"], 1)
            pool.memset(Qtok[:], 0.0).then_inc(s["preset"], 1)
            pool.memset(Vaug[:], 1.0).then_inc(s["preset"], 1)
            pool.wait_ge(s["preset"], 3)
            pool.memset(Ktok[:, :, SHIFT_AT:SHIFT_AT + 3], 1.0).then_inc(s["preset"], 1)
            pool.wait_ge(s["preset"], 4)
            pool.wait_ge(s["w_over"], 1)
            ch = Chain(pool, s["p_chain"])
            quantize(pool, ch, blocks(u[:]), wide(mx6[:]), blocks(wdq[:]), blocks(ua[:]), blocks(ug[:])).then_inc(s["w_quant"], 1)
            with rounds(pool) as b:
                with pool.Fori(0, NT) as i:
                    n = b * NT + i
                    ch = Chain(pool, s["p_chain"])
                    pool.wait_ge(s["u_ready"], n + 1)
                    pool.sem_inc(s["passed"], 1)
                    quantize(pool, ch, blocks(u[:]), wide(mx6[:]),
                             XD[:, bass.ds(i, 1), :].rearrange("p a (k j) -> p (a k) j", j=32),
                             blocks(ua[:]), blocks(ug[:])).then_inc(s["xd_kept"], 1)
                    pool.wait_ge(s["parts_ready"], n + 1)
                    pool.sem_inc(s["passed"], 1)
                    hh = lambda t, a: t[:, a * C:a * C + C].rearrange("p (h d) -> p h d", h=HEADS)
                    qd = Qtok[:, bass.ds(i, 1), :, :].rearrange("p a h d -> p (a h) d")

                    def put(t, k, src, a, m):
                        dst = t[:, :, a * D0:(a + m) * D0]
                        sr = hh(src, k)
                        if m > 1:
                            dst = dst.rearrange("p h (m d) -> p h m d", m=m)
                            sr = sr.unsqueeze(2).broadcast_to([P, HEADS, m, D0])
                        return pool.tensor_copy(dst, sr)
                    ch.mark(put(Ktok, 1, hi, 0, 1))
                    ch.mark(put(Ktok, 1, hi, 3, 2))
                    ch.mark(put(Ktok, 1, mid, 1, 1))
                    ch.mark(put(Ktok, 1, mid, 5, 1))
                    put(Ktok, 1, lo, 2, 1).then_inc(s["k_slots"], 1)
                    ch.mark(put(qd, 0, hi, 0, 3))
                    ch.mark(put(qd, 0, mid, 3, 1))
                    ch.mark(put(qd, 0, mid, 5, 1))
                    put(qd, 0, lo, 4, 1).then_inc(s["q_slots"], 1)
                    ch.close()
                pool.wait_ge(s["xd_kept"], (b + 1) * NT)
                pool.sem_inc(s["passed"], 1)
                with pool.Fori(0, NT) as i:
                    n = b * NT + i
                    pool.tensor_copy(xds[:], one(XD, i)).then_inc(s["xd_copied"], 1)
                    pool.wait_ge(s["out_turned"], n + 1)
                    pool.sem_inc(s["passed"], 1)

        @block.scalar
        def _(act):
            act.wait_ge(s["w_turned"], 1)
            act.activation(wdT[:], pX, ACT.Copy).then_inc(s["w_kept"], 1)
            with rounds(act) as b:
                with act.Fori(0, NT) as i:
                    n = b * NT + i
                    act.wait_ge(s["xn_turned"], n + 1)
                    act.activation(xnT[:], pX, ACT.Copy).then_inc(s["xn_kept"], 1)
                    act.wait_ge(s["k_turned"], n + 1)
                    act.activation(kT[:, :, bass.ds(i * P, P)], pTb[:], ACT.Copy).then_inc(s["k_kept"], 1)
                with act.Fori(0, NT) as i:
                    n = b * NT + i
                    act.wait_ge(s["q_turned"], n + 1)
                    act.activation(qTm[:], pTb[:], ACT.Copy).then_inc(s["q_kept"], 1)
                    act.wait_ge(s["qe_turned"], n + 1)
                    act.activation(qTe[:], pTb[:], ACT.Copy).then_inc(s["qe_kept"], 1)
                    for h in range(HEADS):
                        act.wait_ge(s["e_ready"], n * HEADS + h + 1)
                        if h >= 2:
                            act.wait_ge(s["o_ready"], n * HEADS + h - 1)
                        act.activation(PT[:, h % 2], pE[:, h % 2], ACT.Exp, scale=SCALE0)\
                           .then_inc(s["exp_done"], 1)
                    act.wait_ge(s["out_turned"], n + 1)
                    act.activation(attT[:], pX, ACT.Copy).then_inc(s["out_kept"], 1)
                    act.activation(xdT[:], pX2, ACT.Copy).then_inc(s["out_kept"], 1)
                    act.wait_ge(s["xn2_turned"], n + 1)
                    act.activation(XA[:, bass.ds(b, 1), bass.ds(1 + i * P, P)].rearrange("p a t -> p (a t)"),
                                   pX, ACT.Copy).then_inc(s["xn2_kept"], 1)

        @block.tensor
        def _(pe):
            pe.wait_ge(s["w_quant"], 1)
            pe.transpose(pX, wdq[:], ident[:]).then_inc(s["w_turned"], 1)
            pe.wait_ge(s["w_in"], W_IN)
            pe.wait_ge(s["w_kept"], 1)
            with rounds(pe) as b:
                with pe.Fori(0, NT) as i:
                    n = b * NT + i
                    pe.wait_ge(s["xn_ready"], n + 1)
                    pe.transpose(pX, xn[:], ident[:]).then_inc(s["xn_turned"], 1)
                    pe.wait_ge(s["xn_kept"], n + 1)
                    pe.matmul(pP, xnT[:], wqkv[:], start=True, stop=True).then_inc(s["qkv_ready"], 1)
                    pe.wait_ge(s["k_slots"], n + 1)
                    for c in range(NCH):
                        mm = pe.transpose(pTb[:, c, :], Ktok[:, 2 * c:2 * c + 2, :].rearrange("p h d -> p (h d)"),
                                          identb[:])
                    mm.then_inc(s["k_turned"], 1)
                    pe.wait_ge(s["k_kept"], n + 1)
                with pe.Fori(0, NT) as i:
                    n = b * NT + i

                    def turn_q(done, turned):
                        pe.wait_ge(s[done], n + 1)
                        for c in range(NCH):
                            mm = pe.transpose(pTb[:, c, :], Qs[:, 2 * c:2 * c + 2, :].rearrange("p h d -> p (h d)"),
                                              identb[:])
                        mm.then_inc(s[turned], 1)

                    turn_q("q_copied", "q_turned")
                    pe.wait_ge(s["q_kept"], n + 1)
                    for h in range(HEADS):
                        r = slice(SLOT * (h % 2), SLOT * (h % 2) + SLOT)
                        if h:
                            pe.wait_ge(s["max_done"], n * HEADS + h)
                        for a in range(2):
                            mm = pe.matmul(pS[:, a, :], qTm[r, h // 2, :], kT[r, h // 2, a * 512:a * 512 + 512],
                                           start=True, stop=True)
                        mm.then_inc(s["s_ready"], 1)
                    turn_q("qe_copied", "qe_turned")
                    pe.wait_ge(s["qe_kept"], n + 1)

                    def values(h):
                        pe.wait_ge(s["exp_done"], n * HEADS + h + 1)
                        for j in range(NT):
                            mm = pe.matmul(oh[:, h, 0:D0 + 1], PT[:, h % 2, j, :], Vaug[:, j, h, :],
                                           start=(j == 0), stop=(j == NT - 1))
                        mm.then_inc(s["o_ready"], 1)

                    for h in range(HEADS):
                        r = slice(SLOT * (h % 2), SLOT * (h % 2) + SLOT)
                        for j in range(NT):
                            mm = pe.matmul(pE[:, h % 2, j, :], kT[r, h // 2, j * P:j * P + P], qTe[r, h // 2, :],
                                           start=True, stop=True)
                        mm.then_inc(s["e_ready"], 1)
                        if h:
                            values(h - 1)
                    values(HEADS - 1)
                    pe.wait_ge(s["att_ready"], n + 1)
                    pe.transpose(pX, att[:], ident[:])
                    pe.wait_ge(s["xd_copied"], n + 1)
                    pe.transpose(pX2, xds[:], ident[:]).then_inc(s["out_turned"], 1)
                    pe.wait_ge(s["out_kept"], 2 * n + 2)
                    pe.matmul(pY, attT[:], wo[:], start=True, stop=False)
                    pe.matmul(pY, xdT[:], wdT[:], start=False, stop=True).then_inc(s["y_ready"], 1)
                    pe.wait_ge(s["xn2_ready"], n + 1)
                    pe.transpose(pX, xn2[:], ident[:]).then_inc(s["xn2_turned"], 1)
                    pe.wait_ge(s["xn2_kept"], n + 1)

        def normalize(dve, ch, x, out):
            ch.do(dve.bn_stats(st[:], x))
            ch.do(dve.bn_aggr(mv[:], st[:]))
            ch.do(dve.tensor_scalar(ve[:], mv[:, 1:2], LN_EPS, None, ALU.add))
            rsqrt(dve, ch, rs[:], ve[:], nt_[:])
            return dve.tensor_scalar(out, x, mv[:, 0:1], rs[:, 0:1], ALU.subtract, ALU.mult)

        @block.vector
        def _(dve):
            dve.wait_ge(s["w_in"], W_IN)
            ch = Chain(dve, s["v_chain"])
            ch.mark(dve.tensor_tensor(bsum[:], bsum[:], fbias[:], ALU.add))
            block_scales(dve, ch, wraw[:], mx6[:], inv6[:], u[:]).then_inc(s["w_over"], 1)
            ch.do(dve.tensor_scalar(nsin[:], sin[:], -1.0, None, ALU.mult))
            ch.close()
            dve.wait_ge(s["w_quant"], 1)
            with rounds(dve) as b:
                with dve.Fori(0, NT) as i:
                    n = b * NT + i
                    ch = Chain(dve, s["v_chain"])
                    ins = normalize(dve, ch, one(X, n), xn[:])
                    ins.then_inc(s["xn_ready"], 1)
                    dve.wait_ge(s["xn_ready"], n + 1)
                    block_scales(dve, ch, xn[:], mx6[:], inv6[:], u[:]).then_inc(s["u_ready"], 1)
                    dve.wait_ge(s["qkv_ready"], n + 1)
                    ch.do(dve.tensor_tensor(qkv[:], pP, bqkv[:], ALU.add))
                    v4 = lambda t: t[:, 0:2 * C].rearrange("p (h a j) -> p h a j", a=2, j=D0 // 2)
                    cb = cos[:, bass.ds(i, 1), :].unsqueeze(2).broadcast_to([P, 2 * HEADS, 2, D0 // 2])
                    sn = nsin[:, bass.ds(i, 1), :].broadcast_to([P, 2 * HEADS, D0 // 2])
                    sp_ = sin[:, bass.ds(i, 1), :].broadcast_to([P, 2 * HEADS, D0 // 2])
                    ch.mark(dve.tensor_tensor(v4(t1), v4(qkv), cb, ALU.mult))
                    ch.mark(dve.tensor_tensor(v4(t2)[:, :, 0, :], v4(qkv)[:, :, 1, :], sn, ALU.mult))
                    ch.do(dve.tensor_tensor(v4(t2)[:, :, 1, :], v4(qkv)[:, :, 0, :], sp_, ALU.mult))
                    ch.do(dve.tensor_tensor(t1[:], t1[:], t2[:], ALU.add))
                    ch.do(dve.tensor_copy(hi[:], t1[:]))
                    ch.do(dve.tensor_tensor(t1[:], t1[:], hi[:], ALU.subtract))
                    ch.do(dve.tensor_copy(mid[:], t1[:]))
                    ch.do(dve.tensor_tensor(t1[:], t1[:], mid[:], ALU.subtract))
                    dve.tensor_copy(lo[:], t1[:]).then_inc(s["parts_ready"], 1)
                    ch.do(dve.tensor_copy(Vaug[:, bass.ds(i, 1), :, 0:D0].rearrange("p a h d -> p (a h) d"),
                                          qkv[:, 2 * C:3 * C].rearrange("p (h d) -> p h d", h=HEADS)))
                    dve.wait_ge(s["xd_kept"], n + 1)
                    dve.wait_ge(s["k_slots"], n + 1)
                    dve.wait_ge(s["q_slots"], n + 1)
                    ch.close()
                with dve.Fori(0, NT) as i:
                    n = b * NT + i
                    ch = Chain(dve, s["b_chain"])
                    qi = Qtok[:, bass.ds(i, 1), :, :].rearrange("p a h d -> p (a h d)")
                    qf = Qs[:].rearrange("p h d -> p (h d)")
                    dve.tensor_copy(qf, qi).then_inc(s["q_copied"], 1)
                    for h in range(HEADS):
                        dve.wait_ge(s["s_ready"], n * HEADS + h + 1)
                        dve.tensor_reduce(mx[:, h:h + 1], pS[:].rearrange("p a k -> p (a k)"), AX_X, ALU.max)\
                           .then_inc(s["max_done"], 1)
                    at = lambda k: Qs[:, :, SHIFT_AT + k:SHIFT_AT + k + 1].rearrange("p h d -> p (h d)")
                    dve.wait_ge(s["max_done"], n * HEADS + HEADS)
                    dve.wait_ge(s["q_turned"], n + 1)
                    ch.do(dve.tensor_scalar(m1[:], mx[:], -1.0, None, ALU.mult))
                    ch.do(dve.tensor_copy(at(0), m1[:]))
                    ch.do(dve.tensor_tensor(m1[:], m1[:], at(0), ALU.subtract))
                    ch.do(dve.tensor_copy(at(1), m1[:]))
                    ch.do(dve.tensor_tensor(m1[:], m1[:], at(1), ALU.subtract))
                    dve.tensor_copy(at(2), m1[:]).then_inc(s["qe_copied"], 1)
                    dve.wait_ge(s["o_ready"], n * HEADS + HEADS)
                    ch.do(dve.reciprocal(rden[:], oh[:, :, D0:D0 + 1].rearrange("p h d -> p (h d)")))
                    dve.tensor_tensor(att[:].rearrange("p (h d) -> p h d", h=HEADS), oh[:, :, 0:D0],
                                      rden[:].unsqueeze(2).broadcast_to([P, HEADS, D0]), ALU.mult)\
                       .then_inc(s["att_ready"], 1)
                    dve.wait_ge(s["y_ready"], n + 1)
                    ch.do(dve.tensor_tensor(x1[:], pY, bsum[:], ALU.add))
                    ch.do(dve.tensor_tensor(x1[:], x1[:], one(X, n), ALU.add))
                    ch.do(dve.tensor_copy(one(X, n), x1[:]))
                    normalize(dve, ch, x1[:], xn2[:]).then_inc(s["xn2_ready"], 1)
                    dve.wait_ge(s["xn2_turned"], n + 1)
                    ch.close()


def l1_attn_phase(nc, io, keep):
    ident, X, XA = keep["ident"], keep["X"], keep["XA"]
    with ExitStack() as ctx:
        sem = lambda n: ctx.enter_context(nc.semaphore(n))
        sb = lambda n, s, d=F32: ctx.enter_context(nc.sbuf_tensor(n, s, d))
        ps = lambda n, s, d=F32: ctx.enter_context(nc.psum_tensor(n, s, d))

        W5 = sb("W5", [P, 5, INNER])
        wb = sb("wb", [P, HEADS])
        wo = sb("wo1", [P, NCH, C])
        brow = sb("brow1", [1, 2, INNER])
        ones = sb("ones1", [1, P])
        alog, neA = sb("alog", [P, HEADS]), sb("neA", [P, HEADS])
        alogF, neAF = sb("alogF", [P, NCH]), sb("neAF", [P, NCH])
        dist, before = sb("dist", [P, P]), sb("before", [P, P])
        trow, rev = sb("trow", [P, P]), sb("rev", [P, 1])
        nw = sb("nw", [P, D1])
        Dec = sb("Dec", [P, 2, NCH, P])
        decT = sb("decT", [P, NCH, P])
        A128 = sb("A128", [P, NCH])
        kdec = sb("kdec", [P, HEADS])
        xT = sb("xT1", [P, P])
        qs, ks, vs = sb("qs1", [P, INNER]), sb("ks1", [P, INNER]), sb("vs1", [P, INNER])
        fs, gs = sb("fs1", [P, INNER]), sb("gs1", [P, INNER])
        sqa, sqb = sb("sqa1", [P, INNER]), sb("sqb1", [P, INNER])
        bt, bv = sb("bt1", [P, HEADS]), sb("bv1", [P, HEADS])
        ss, rr, tn = sb("ss1", [P, 2 * HEADS]), sb("rr1", [P, 2 * HEADS]), sb("tn1", [P, 2 * HEADS])
        qT, kT, qdT = sb("qT1", [P, NCH, P]), sb("kT1", [P, NCH, P]), sb("qdT1", [P, NCH, P])
        vp, kp = sb("vp1", [P, INNER]), sb("kp1", [P, INNER])
        Wd = sb("Wd1", [P, 2, NCH, P])
        St, StA = sb("St", [P, NCH, D1]), sb("StA", [P, NCH, D1])
        o1, oT = sb("o1", [P, INNER]), sb("oT1", [P, NCH, P])

        PA, PB = ps("PA1", [P, 2, 512]), ps("PB1", [P, 2, 512])
        PC, PD = ps("PC1", [P, 2, 512]), ps("PD1", [P, 2, 512])
        flat = lambda t: t[:].rearrange("p a k -> p (a k)")
        tiles = lambda t: t[:].rearrange("p a (c t) -> p (a c) t", t=P)
        heads = lambda t: t.rearrange("p (h d) -> p h d", d=D1)
        wide = lambda t: t.unsqueeze(2).broadcast_to([P, HEADS, D1])
        o_feat = PA[:].rearrange("p a (c d) -> p c a d", d=D1)
        feat4 = lambda t: t.rearrange("p (c a d) -> p c a d", a=2, d=D1)

        names = ["w_in", "passed", "t_chain", "t_exp", "v_chain", "p_chain", "x_kept", "q_ready", "k_ready", "v_ready",
                 "b_ready", "f_ready", "g_ready", "q_kept", "k_kept", "v_kept", "b_kept", "f_kept", "g_kept",
                 "sqq", "sqk", "r_ready", "q_turned", "k_turned", "qT_kept", "kT_kept", "qd_ready", "vp_ready",
                 "kp_ready", "gq_ready", "gw_ready", "s_ready", "w_ready", "o_ready", "st_ready", "st_kept",
                 "o1_ready", "sqo", "o2_ready", "o_turned", "oT_kept", "y_ready", "y_kept", "tables", "st_zeroed"]
        s = {n: sem("l1_" + n) for n in names}
        W_IN = 16 * 18
        block = ctx.enter_context(nc.Block())

        @block.sync
        def _(sp):
            load = lambda dst, src: sp.dma_start(dst, src).then_inc(s["w_in"], 16)
            for k, n in enumerate(("Wq", "Wk", "Wv", "Wf", "Wg")):
                load(W5[:, k, :], io["L1_attn_" + n])
            load(wb[:], io["L1_attn_Wb"])
            load(wo[:], io["L1_attn_Wo"].rearrange("(c p) n -> p c n", p=P))
            load(brow[:, 0, :], io["L1_attn_dt_bias"].rearrange("(a n) -> a n", a=1))
            load(brow[:, 1, :], io["L1_attn_bg"].rearrange("(a n) -> a n", a=1))
            load(alog[:], io["L1_attn_A_log"].partition_broadcast(P))
            pairs = io["L1_attn_A_log"].rearrange("(c a) -> a c", a=2)
            with nc.allow_non_contiguous_dma(reason="8 values"):
                load(alogF[0:D1, :], pairs[0].partition_broadcast(D1))
                load(alogF[D1:P, :], pairs[1].partition_broadcast(D1))
            load(nw[:], io["L1_attn_norm_w"].partition_broadcast(P))
            load(dist[:], io["dist"])
            load(before[:], io["before"])
            load(trow[:], io["trow"])
            load(rev[:], io["rev"])
            load(ones[:], io["trow1"])

        @block.gpsimd
        def _(pool):
            pool.wait_ge(s["w_in"], W_IN)
            with pool.Fori(0, B * NT) as n:
                ch = Chain(pool, s["p_chain"])
                pool.wait_ge(s["k_kept"], n + 1)
                pool.sem_inc(s["passed"], 1)
                pool.tensor_tensor(heads(kp[:]), heads(ks[:]), wide(kdec[:]), ALU.mult).then_inc(s["kp_ready"], 1)
                pool.wait_ge(s["f_kept"], n + 1)
                pool.sem_inc(s["passed"], 1)
                pool.wait_ge(s["r_ready"], n + 1)
                pool.sem_inc(s["passed"], 1)
                pool.tensor_tensor(heads(fs[:]), heads(fs[:]), wide(rr[:, 0:HEADS]), ALU.mult)\
                    .then_inc(s["gq_ready"], 1)
                pool.wait_ge(s["g_kept"], n + 1)
                pool.sem_inc(s["passed"], 1)
                pool.tensor_tensor(heads(gs[:]), heads(gs[:]), nw[:].unsqueeze(1).broadcast_to([P, HEADS, D1]),
                                   ALU.mult).then_inc(s["gw_ready"], 1)

        @block.scalar
        def _(act):
            act.wait_ge(s["w_in"], W_IN)
            act.activation(neA[:], alog[:], ACT.Exp).then_inc(s["t_exp"], 1)
            act.activation(neAF[:], alogF[:], ACT.Exp).then_inc(s["t_exp"], 1)
            act.wait_ge(s["t_chain"], 2)
            for h in range(HEADS):
                act.activation(Dec[:, h % 2, h // 2, :], dist[:], ACT.Exp, scale=neA[:, h:h + 1])\
                   .then_inc(s["t_exp"], 1)
            for c in range(NCH):
                act.activation(decT[:, c, :], trow[:], ACT.Exp, scale=neAF[:, c:c + 1])
            act.activation(A128[:], neAF[:], ACT.Exp, scale=float(P))
            act.activation(kdec[:], neA[:], ACT.Exp, scale=rev[:, 0:1]).then_inc(s["tables"], 1)
            with act.Fori(0, B) as b:
                with act.Fori(0, NT) as i:
                    n = b * NT + i
                    act.activation(xT[:], XA[:, bass.ds(b, 1), bass.ds(1 + i * P, P)].rearrange("p a t -> p (a t)"),
                                   ACT.Copy).then_inc(s["x_kept"], 1)
                    for src, dst, r, k in ((PA, qs, "q_ready", "q_kept"), (PB, ks, "k_ready", "k_kept"),
                                           (PC, vs, "v_ready", "v_kept")):
                        act.wait_ge(s[r], n + 1)
                        act.activation(dst[:], flat(src), ACT.Silu).then_inc(s[k], 1)
                    act.wait_ge(s["k_kept"], n + 1)
                    act.activation(sqa[:], qs[:], ACT.Square).then_inc(s["sqq"], 1)
                    act.activation(sqb[:], ks[:], ACT.Square).then_inc(s["sqk"], 1)
                    act.wait_ge(s["b_ready"], n + 1)
                    act.activation(bt[:], PD[:, 0, 0:HEADS], ACT.Sigmoid).then_inc(s["b_kept"], 1)
                    for src, dst, r, k in ((PA, fs, "f_ready", "f_kept"), (PB, gs, "g_ready", "g_kept")):
                        act.wait_ge(s[r], n + 1)
                        act.activation(dst[:], flat(src), ACT.Sigmoid).then_inc(s[k], 1)
                    act.wait_ge(s["q_turned"], n + 1)
                    act.activation(qT[:], tiles(PC), ACT.Copy).then_inc(s["qT_kept"], 1)
                    act.wait_ge(s["k_turned"], n + 1)
                    act.activation(kT[:], tiles(PD), ACT.Copy).then_inc(s["kT_kept"], 1)
                    act.wait_ge(s["o1_ready"], n + 1)
                    act.activation(sqa[:], o1[:], ACT.Square).then_inc(s["sqo"], 1)
                    act.wait_ge(s["o_turned"], n + 1)
                    act.activation(oT[:], tiles(PC), ACT.Copy).then_inc(s["oT_kept"], 1)
                    act.wait_ge(s["y_kept"], n + 1)

        @block.tensor
        def _(pe):
            pe.wait_ge(s["w_in"], W_IN)
            pe.wait_ge(s["t_chain"], 4)
            pe.wait_ge(s["tables"], 1)
            with pe.Fori(0, B * NT) as n:
                def project(dst, k, bias, done):
                    for a in range(2):
                        r = slice(a * 512, a * 512 + 512)
                        mm = pe.matmul(dst[:, a, :], xT[:], W5[:, k, r], start=True, stop=(bias is None))
                        if bias is not None:
                            mm = pe.matmul(dst[:, a, :], ones[:], brow[:, bias, r], start=False, stop=True)
                    mm.then_inc(s[done], 1)

                def turn(dst, src, done):
                    for c in range(NCH):
                        mm = pe.transpose(tiles(dst)[:, c, :], src[:, c * P:c * P + P], ident[:])
                    mm.then_inc(s[done], 1)

                pe.wait_ge(s["x_kept"], n + 1)
                project(PA, 0, None, "q_ready")
                project(PB, 1, None, "k_ready")
                project(PC, 2, None, "v_ready")
                pe.matmul(PD[:, 0, 0:HEADS], xT[:], wb[:], start=True, stop=True).then_inc(s["b_ready"], 1)
                pe.wait_ge(s["q_kept"], n + 1)
                project(PA, 3, 0, "f_ready")
                pe.wait_ge(s["k_kept"], n + 1)
                project(PB, 4, 1, "g_ready")
                pe.wait_ge(s["v_kept"], n + 1)
                turn(PC, qs, "q_turned")
                pe.wait_ge(s["b_kept"], n + 1)
                turn(PD, ks, "k_turned")
                pe.wait_ge(s["qT_kept"], n + 1)
                pe.wait_ge(s["kT_kept"], n + 1)
                pe.wait_ge(s["qd_ready"], n + 1)
                for a, bank in ((0, PC), (1, PD)):
                    r = slice(a * D1, a * D1 + D1)
                    for j in range(2):
                        for c in range(4 * j, 4 * j + 4):
                            mm = pe.matmul(tiles(bank)[:, c, :], kT[r, c, :], qT[r, c, :], start=True, stop=True)
                        mm.then_inc(s["s_ready"], 1)
                pe.wait_ge(s["f_kept"], n + 1)
                pe.wait_ge(s["vp_ready"], n + 1)
                for a in range(2):
                    r = slice(a * D1, a * D1 + D1)
                    for j in range(2):
                        pe.wait_ge(s["w_ready"], 4 * n + 2 * a + j + 1)
                        for c in range(4 * j, 4 * j + 4):
                            h = 2 * c + a
                            pe.matmul(PA[:, a, c * D1:c * D1 + D1], Wd[:, a, c, :], vp[:, h * D1:h * D1 + D1],
                                      start=True, stop=False)
                            mm = pe.matmul(PA[:, a, c * D1:c * D1 + D1], qdT[r, c, :], St[r, c, :],
                                           start=False, stop=True)
                mm.then_inc(s["o_ready"], 1)
                pe.wait_ge(s["g_kept"], n + 1)
                pe.wait_ge(s["kp_ready"], n + 1)
                for c in range(NCH):
                    r = slice(c * P, c * P + P)
                    mm = pe.matmul(tiles(PB)[:, c, :], kp[:, r], vp[:, r], start=True, stop=True)
                mm.then_inc(s["st_ready"], 1)
                pe.wait_ge(s["o2_ready"], n + 1)
                turn(PC, o1, "o_turned")
                pe.wait_ge(s["oT_kept"], n + 1)
                for c in range(NCH):
                    mm = pe.matmul(PD[:, 0, 0:C], oT[:, c, :], wo[:, c, :], start=(c == 0), stop=(c == NCH - 1))
                mm.then_inc(s["y_ready"], 1)
                pe.wait_ge(s["st_kept"], n + 1)

        @block.vector
        def _(dve):
            dve.wait_ge(s["w_in"], W_IN)
            dve.wait_ge(s["t_exp"], 2)
            dve.tensor_scalar(neA[:], neA[:], 1e30, -1.0, ALU.min, ALU.mult).then_inc(s["t_chain"], 1)
            dve.tensor_scalar(neAF[:], neAF[:], 1e30, -1.0, ALU.min, ALU.mult).then_inc(s["t_chain"], 1)
            dve.tensor_scalar(brow[:, 0, :], brow[:, 0, :], -1.0, None, ALU.mult).then_inc(s["t_chain"], 1)
            dve.wait_ge(s["t_exp"], 2 + HEADS)
            dec = Dec[:].rearrange("p a c t -> p (a c) t")
            dve.tensor_tensor(dec, dec, before[:].unsqueeze(1).broadcast_to([P, HEADS, P]), ALU.mult)\
               .then_inc(s["t_chain"], 1)
            dve.wait_ge(s["t_chain"], 4)
            dve.wait_ge(s["tables"], 1)
            with dve.Fori(0, B) as b:
                dve.memset(St[:], 0.0).then_inc(s["st_zeroed"], 1)
                dve.wait_ge(s["st_zeroed"], b + 1)
                dve.sem_inc(s["passed"], 1)
                with dve.Fori(0, NT) as i:
                    n = b * NT + i
                    ch = Chain(dve, s["v_chain"])
                    dve.wait_ge(s["sqq"], n + 1)
                    ch.mark(dve.tensor_reduce(ss[:, 0:HEADS], heads(sqa[:]), AX_X, ALU.add))
                    dve.wait_ge(s["sqk"], n + 1)
                    ch.do(dve.tensor_reduce(ss[:, HEADS:2 * HEADS], heads(sqb[:]), AX_X, ALU.add))
                    ch.do(dve.tensor_scalar(ss[:], ss[:], L2_TINY, None, ALU.max))
                    rsqrt(dve, ch, rr[:], ss[:], tn[:])
                    dve.wait_ge(s["b_kept"], n + 1)
                    dve.tensor_tensor(bv[:], bt[:], rr[:, HEADS:2 * HEADS], ALU.mult).then_inc(s["r_ready"], 1)
                    dve.wait_ge(s["r_ready"], n + 1)
                    dve.wait_ge(s["v_kept"], n + 1)
                    dve.tensor_tensor(heads(vp[:]), heads(vs[:]), wide(bv[:]), ALU.mult).then_inc(s["vp_ready"], 1)
                    dve.wait_ge(s["q_turned"], n + 1)
                    dve.wait_ge(s["qT_kept"], n + 1)
                    dve.tensor_tensor(qdT[:], tiles(PC), decT[:], ALU.mult).then_inc(s["qd_ready"], 1)
                    for q in range(4):
                        a, j = q // 2, q % 2
                        dve.wait_ge(s["s_ready"], 4 * n + q + 1)
                        dve.tensor_tensor(Wd[:, a, 4 * j:4 * j + 4, :], tiles((PC, PD)[a])[:, 4 * j:4 * j + 4, :],
                                          Dec[:, a, 4 * j:4 * j + 4, :], ALU.mult).then_inc(s["w_ready"], 1)
                    dve.wait_ge(s["o_ready"], n + 1)
                    dve.wait_ge(s["gq_ready"], n + 1)
                    dve.tensor_tensor(feat4(o1[:]), o_feat, feat4(fs[:]), ALU.mult).then_inc(s["o1_ready"], 1)
                    ch.do(dve.tensor_tensor(StA[:], St[:], A128[:].unsqueeze(2).broadcast_to([P, NCH, D1]), ALU.mult))
                    dve.wait_ge(s["st_ready"], n + 1)
                    ch.mark(dve.tensor_tensor(St[0:D1], StA[0:D1], tiles(PB)[0:D1, :, 0:D1], ALU.add))
                    dve.tensor_tensor(St[D1:P], StA[D1:P], tiles(PB)[D1:P, :, D1:P], ALU.add).then_inc(s["st_kept"], 1)
                    dve.wait_ge(s["sqo"], n + 1)
                    ch.do(dve.tensor_reduce(ss[:, 0:HEADS], heads(sqa[:]), AX_X, ALU.add))
                    ch.do(dve.tensor_scalar(ss[:, 0:HEADS], ss[:, 0:HEADS], 1.0 / D1, RMS_EPS, ALU.mult, ALU.add))
                    rsqrt(dve, ch, bv[:], ss[:, 0:HEADS], tn[:, 0:HEADS])
                    ch.do(dve.tensor_tensor(heads(o1[:]), heads(o1[:]), wide(bv[:]), ALU.mult))
                    dve.wait_ge(s["gw_ready"], n + 1)
                    dve.tensor_tensor(o1[:], o1[:], gs[:], ALU.mult).then_inc(s["o2_ready"], 1)
                    dve.wait_ge(s["y_ready"], n + 1)
                    dve.tensor_tensor(one(X, n), PD[:, 0, 0:C], one(X, n), ALU.add).then_inc(s["y_kept"], 1)
                    dve.wait_ge(s["st_kept"], n + 1)
                    ch.close()


def l1_ffn_phase(nc, io, keep):
    ident, identb, XA, XB = keep["ident"], keep["identb"], keep["XA"], keep["XB"]
    with ExitStack() as ctx:
        sem = lambda n: ctx.enter_context(nc.semaphore(n))
        sb = lambda n, s, d=F32: ctx.enter_context(nc.sbuf_tensor(n, s, d))
        ps = lambda n, s, d=F32: ctx.enter_context(nc.psum_tensor(n, s, d))

        Wqkv = sb("Wqkv", [P, 3 * INNER])
        Wo = sb("Wo", [P, NCH, C])
        qsc, ksc = sb("qsc", [P, D1]), sb("ksc", [P, D1])
        rot = {k: sb(k, [P, NT, D1]) for k in ("cos_q", "sin_q", "cos_k", "sin_k")}
        tab = {k: sb("t_" + k, [P, NT, D1]) for k in rot}
        mask = sb("mask", [P, NT, 2 * KEYS], BF16)
        stays = sb("stays", [P, NT])
        W1 = sb("W1", [P, 2 * FFN])
        W2 = sb("W2", [P, 3, C])
        lng, lnb, b2 = sb("lng", [P, 1]), sb("lnb", [P, 1]), sb("b2", [P, 1])
        b1 = sb("b1", [P, 6])
        xs = sb("xs", [P, P])
        t1q, t2q, t1k, t2k = (sb(n, [P, INNER]) for n in ("t1q", "t2q", "t1k", "t2k"))
        sqa, sqb = sb("sqa", [P, INNER]), sb("sqb", [P, INNER])
        qr, kr = sb("qr", [P, INNER]), sb("kr", [P, INNER])
        ss, rr, tn = sb("ss", [P, 2 * HEADS]), sb("rr", [P, 2 * HEADS]), sb("tn", [P, 2 * HEADS])
        rq8 = sb("rq8", [P, HEADS])
        qT = sb("qT", [P, NCH, P])
        kT = sb("kT", [P, NCH, KEYS])
        V, VL = sb("V", [P, INNER]), sb("VL", [WINDOW, INNER])
        mx, nb, den, rden = (sb(n, [P, HEADS]) for n in ("mx", "nb", "den", "rden"))
        Pr = sb("Pr", [P, 2, 4, KEYS])
        PT, PL = sb("PTs", [P, 2, 4, P]), sb("PLs", [WINDOW, 2, 4, WINDOW])
        on, oT = sb("on", [P, INNER]), sb("oT", [P, NCH, P])
        xf = sb("xf", [P, FTOK])
        st, mv = sb("st", [P, 4, 6]), sb("mv", [P, 4, 2])
        ve, rs, tv = sb("ve", [P, 4]), sb("rs", [P, 4]), sb("tv", [P, 4])
        xn, xnT = sb("xn", [P, 4, P]), sb("xnT", [P, FTOK])
        G, H = sb("G", [P, 3, FTOK]), sb("H", [P, 3, FTOK])

        PA, PB = ps("PA", [P, 2, 512]), ps("PB", [P, 2, 512])
        PC, PD = ps("PC", [P, 2, 512]), ps("PD", [P, 2, 512])
        flat = lambda t: t[:].rearrange("p a k -> p (a k)")
        tiles = lambda t: t[:].rearrange("p a (c t) -> p (a c) t", t=P)
        heads = lambda t: t.rearrange("p (h d) -> p h d", d=D1)
        halves = lambda t: t.rearrange("p (h a j) -> p h a j", a=2, j=D1 // 2)
        wide = lambda t: t.unsqueeze(2).broadcast_to([P, HEADS, D1])
        yA = PD[:, 0, 0:P]
        turned_p = PB[:, 0, :].rearrange("p (h t) -> p h t", t=P)
        turned_l = PB[0:WINDOW, 1, 0:4 * WINDOW].rearrange("p (h t) -> p h t", t=WINDOW)
        fbank = [PB[:, 0, :], PB[:, 1, :], PC[:, 0, :], PC[:, 1, :], PD[:, 0, :], PD[:, 1, :]]

        names = ["consts", "passed", "aw_in", "fw_in", "first", "v_chain", "f_chain", "xs_ready", "q_ready", "k_ready",
                 "v_ready", "sqq", "sqk", "tq_ready", "tk_ready", "qr_ready", "ks_ready", "kr_ready", "v_kept",
                 "q_turned", "k_turned", "qT_kept", "kT_kept", "s_ready", "nb_ready", "exp_done", "p_turned", "p_kept",
                 "o_ready", "on_ready", "o_turned", "oT_kept", "y_ready", "xb_kept", "xf_ready", "xf_turned",
                 "xn_ready", "xn_turned", "xnT_kept", "hg_ready", "g_ready", "h_ready", "yf_ready", "xa_kept"]
        s = {n: sem("f_" + n) for n in names}
        AW, FW = 16 * 4, 16 * 13
        TILES, BLOCKS = B * NT, B * T // FTOK
        block = ctx.enter_context(nc.Block())

        @block.sync
        def _(sp):
            for k in rot:
                sp.dma_start(rot[k][:], io[k]).then_inc(s["consts"], 16)
            sp.dma_start(mask[:], io["mask"]).then_inc(s["consts"], 16)
            sp.dma_start(stays[:], io["stays"]).then_inc(s["consts"], 16)

            def at(name, l):
                a = io["L1_ffn_" + name]
                a = a[bass.ds(l, 1)]
                return a.rearrange("a m n -> (a m) n") if len(a.shape) == 3 else a

            def attn_weights(l):
                load = lambda dst, src: sp.dma_start(dst, src).then_inc(s["aw_in"], 16)
                load(Wqkv[:], at("Wqkv", l))
                load(Wo[:], at("Wo", l).rearrange("(c p) n -> p c n", p=P))
                load(qsc[:], at("q_scale", l).broadcast_to([P, D1]))
                load(ksc[:], at("k_scale", l).broadcast_to([P, D1]))

            def ffn_weights(l):
                load = lambda dst, src: sp.dma_start(dst, src).then_inc(s["fw_in"], 16)
                load(W1[:], at("W1", l))
                for k, (f, m) in enumerate(FCH):
                    load(W2[0:m, k, :], at("W2", l)[f:f + m, :])
                with nc.allow_non_contiguous_dma(reason="a column of channels"):
                    col = lambda name, f, m: at(name, l)[:, f:f + m].rearrange("a m -> m a")
                    load(lng[:], col("ln_g", 0, C))
                    load(lnb[:], col("ln_b", 0, C))
                    load(b2[:], col("b2", 0, C))
                    for k, (f, m) in enumerate(FCH):
                        load(b1[0:m, k:k + 1], col("b1", f, m))
                        load(b1[0:m, 3 + k:4 + k], col("b1", FFN + f, m))

            attn_weights(0)
            ffn_weights(0)
            with sp.Fori(0, DEPTH - 1) as l:
                sp.wait_ge(s["xb_kept"], (l + 1) * TILES)
                attn_weights(l + 1)
                sp.wait_ge(s["xa_kept"], (l + 1) * BLOCKS + 1)
                ffn_weights(l + 1)

        @block.gpsimd
        def _(pool):
            pool.memset(kT[:], 0.0).then_inc(s["first"], 1)
            pool.memset(VL[:], 0.0).then_inc(s["first"], 1)
            pool.wait_ge(s["first"], 2)

            def shifted(dst, src, b, i, m, done, n):
                h = C // 2
                for k, (r, first) in enumerate(((slice(0, h), 1), (slice(h, C), 0))):
                    pool.tensor_copy(dst[r, :], src[r, bass.ds(b, 1), bass.ds(first + i * m, m)]
                                     .rearrange("p a t -> p (a t)")).then_inc(s[done], 1)
                    pool.wait_ge(s[done], 2 * n + k + 1)
                    pool.sem_inc(s["passed"], 1)

            with pool.Fori(0, DEPTH) as l:
                pool.wait_ge(s["xa_kept"], l * BLOCKS + 1)
                pool.sem_inc(s["passed"], 1)
                with pool.Fori(0, B) as b:
                    with pool.Fori(0, NT) as i:
                        n = l * TILES + b * NT + i
                        shifted(xs, XA, b, i, P, "xs_ready", n)
                        pool.wait_ge(s["tq_ready"], n + 1)
                        pool.sem_inc(s["passed"], 1)
                        pool.tensor_tensor(qr[:], t1q[:], t2q[:], ALU.add).then_inc(s["qr_ready"], 1)
                        pool.wait_ge(s["tk_ready"], n + 1)
                        pool.sem_inc(s["passed"], 1)
                        pool.tensor_tensor(kr[:], t1k[:], t2k[:], ALU.add).then_inc(s["ks_ready"], 1)
                        pool.wait_ge(s["v_ready"], n + 1)
                        pool.sem_inc(s["passed"], 1)
                        pool.wait_ge(s["ks_ready"], n + 1)
                        pool.sem_inc(s["passed"], 1)
                pool.wait_ge(s["xb_kept"], (l + 1) * TILES)
                pool.sem_inc(s["passed"], 1)
                with pool.Fori(0, B) as b:
                    with pool.Fori(0, T // FTOK) as i:
                        m = l * BLOCKS + b * (T // FTOK) + i
                        shifted(xf, XB, b, i, FTOK, "xf_ready", m)
                        pool.wait_ge(s["xf_turned"], m + 1)
                        pool.sem_inc(s["passed"], 1)

        @block.scalar
        def _(act):
            act.wait_ge(s["first"], 2)
            act.wait_ge(s["consts"], 16 * 6)
            with act.Fori(0, DEPTH) as l:
                with act.Fori(0, B) as b:
                    with act.Fori(0, NT) as i:
                        n = l * TILES + b * NT + i
                        act.wait_ge(s["q_ready"], n + 1)
                        act.activation(sqa[:], flat(PA), ACT.Square).then_inc(s["sqq"], 1)
                        act.wait_ge(s["k_ready"], n + 1)
                        act.activation(sqb[:], flat(PB), ACT.Square).then_inc(s["sqk"], 1)
                        act.wait_ge(s["v_ready"], n + 1)
                        act.activation(V[:], flat(PC), ACT.Copy).then_inc(s["v_kept"], 1)
                        act.wait_ge(s["q_turned"], n + 1)
                        act.activation(qT[:], tiles(PD), ACT.Copy).then_inc(s["qT_kept"], 1)
                        act.wait_ge(s["k_turned"], n + 1)
                        act.activation(kT[:, :, WINDOW:KEYS], tiles(PC), ACT.Copy).then_inc(s["kT_kept"], 1)
                        for g in range(4):
                            act.wait_ge(s["nb_ready"], 4 * n + g + 1)
                            if g >= 2:
                                act.wait_ge(s["p_turned"], 4 * n + g - 1)
                            for j in range(4):
                                h = 4 * g + j
                                ins = act.activation(Pr[:, g % 2, j, :], PD[:, j % 2, (j // 2) * KEYS:(j // 2 + 1) * KEYS],
                                                     ACT.Exp, bias=nb[:, h:h + 1], scale=rq8[:, h:h + 1],
                                                     accum_out=den[:, h:h + 1])
                            ins.then_inc(s["exp_done"], 1)
                        act.wait_ge(s["o_ready"], n + 1)
                        act.activation(kT[:, :, 0:WINDOW], kT[:, :, P:KEYS], ACT.Copy,
                                       scale=stays[:, bass.ds(i, 1)])
                        act.activation(VL[:], V[P - WINDOW:P, :], ACT.Copy)
                        act.wait_ge(s["o_turned"], n + 1)
                        act.activation(oT[:], tiles(PC), ACT.Copy).then_inc(s["oT_kept"], 1)
                with act.Fori(0, BLOCKS) as t:
                    m = l * BLOCKS + t
                    act.wait_ge(s["fw_in"], (l + 1) * FW)
                    act.wait_ge(s["xn_turned"], m + 1)
                    act.activation(xnT[:], PA[:, 1, :], ACT.Identity, bias=lnb[:, 0:1], scale=lng[:, 0:1])\
                       .then_inc(s["xnT_kept"], 1)
                    for k, (f, w) in enumerate(FCH):
                        act.wait_ge(s["hg_ready"], 6 * m + k + 1)
                        act.activation(G[0:w, k, :], fbank[k][0:w, :], ACT.Gelu, bias=b1[0:w, 3 + k:4 + k])\
                           .then_inc(s["g_ready"], 1)
                    act.wait_ge(s["h_ready"], 3 * m + 3)

        @block.tensor
        def _(pe):
            pe.wait_ge(s["consts"], 16 * 6)
            pe.wait_ge(s["first"], 2)

            def turn(dst, src, done):
                for c in range(NCH):
                    mm = pe.transpose(tiles(dst)[:, c, :], src[:, c * P:c * P + P], ident[:])
                mm.then_inc(s[done], 1)

            with pe.Fori(0, DEPTH) as l:
                pe.wait_ge(s["aw_in"], (l + 1) * AW)
                pe.sem_inc(s["passed"], 1)
                with pe.Fori(0, B) as b:
                    with pe.Fori(0, NT) as i:
                        n = l * TILES + b * NT + i

                        def project(dst, k, done):
                            for a in range(2):
                                f = k * INNER + a * 512
                                mm = pe.matmul(dst[:, a, :], xs[:], Wqkv[:, f:f + 512], start=True, stop=True)
                            mm.then_inc(s[done], 1)

                        def scores(g):
                            for a in range(2):
                                r = slice(a * D1, a * D1 + D1)
                                pe.matmul(PD[:, a, 0:2 * KEYS], identb[:],
                                          mask[:, bass.ds(i, 1), :].rearrange("p a k -> p (a k)"),
                                          start=True, stop=False)
                                for k in range(2):
                                    c = 2 * g + k
                                    mm = pe.matmul(PD[:, a, k * KEYS:k * KEYS + KEYS], qT[r, c, :], kT[r, c, :],
                                                   start=False, stop=(k == 1))
                            mm.then_inc(s["s_ready"], 1)

                        def turn_p(g):
                            if g:
                                pe.wait_ge(s["p_kept"], 4 * n + g)
                            for j in range(4):
                                pe.transpose(turned_p[:, j, :], Pr[:, g % 2, j, WINDOW:KEYS], ident[:])
                            for j in range(4):
                                mm = pe.transpose(turned_l[:, j, :], Pr[0:WINDOW, g % 2, j, 0:WINDOW],
                                                  ident[0:WINDOW, 0:WINDOW])
                            mm.then_inc(s["p_turned"], 1)

                        def values(g):
                            pe.wait_ge(s["p_kept"], 4 * n + g + 1)
                            for j in range(4):
                                h = 4 * g + j
                                f = slice(h * D1, h * D1 + D1)
                                o = flat(PA)[:, f]
                                pe.matmul(o, PT[:, g % 2, j, :], V[:, f], start=True, stop=True)
                                mm = pe.matmul(flat(PA)[0:WINDOW, f], PL[:, g % 2, j, :], VL[:, f],
                                               start=False, stop=True, skip_group_check=True)
                            if g == 3:
                                mm.then_inc(s["o_ready"], 1)

                        pe.wait_ge(s["xs_ready"], 2 * n + 2)
                        project(PA, 0, "q_ready")
                        project(PB, 1, "k_ready")
                        project(PC, 2, "v_ready")
                        pe.wait_ge(s["qr_ready"], n + 1)
                        turn(PD, qr, "q_turned")
                        pe.wait_ge(s["v_kept"], n + 1)
                        pe.wait_ge(s["kr_ready"], n + 1)
                        turn(PC, kr, "k_turned")
                        pe.wait_ge(s["qT_kept"], n + 1)
                        pe.wait_ge(s["kT_kept"], n + 1)
                        scores(0)
                        for g in range(4):
                            pe.wait_ge(s["exp_done"], 4 * n + g + 1)
                            if g < 3:
                                scores(g + 1)
                            turn_p(g)
                            values(g)
                        pe.wait_ge(s["on_ready"], n + 1)
                        turn(PC, on, "o_turned")
                        pe.wait_ge(s["oT_kept"], n + 1)
                        for c in range(NCH):
                            mm = pe.matmul(yA, Wo[:, c, :], oT[:, c, :], start=(c == 0), stop=(c == NCH - 1))
                        mm.then_inc(s["y_ready"], 1)
                pe.wait_ge(s["fw_in"], (l + 1) * FW)
                pe.sem_inc(s["passed"], 1)
                pe.wait_ge(s["xb_kept"], (l + 1) * TILES)
                pe.sem_inc(s["passed"], 1)
                with pe.Fori(0, BLOCKS) as t:
                    m = l * BLOCKS + t
                    pe.wait_ge(s["xf_ready"], 2 * m + 2)
                    for c in range(4):
                        mm = pe.transpose(PA[:, 0, c * P:c * P + P], xf[:, c * P:c * P + P], ident[:])
                    mm.then_inc(s["xf_turned"], 1)
                    pe.wait_ge(s["xn_ready"], m + 1)
                    for c in range(4):
                        mm = pe.transpose(PA[:, 1, c * P:c * P + P], xn[:, c, :], ident[:])
                    mm.then_inc(s["xn_turned"], 1)
                    pe.wait_ge(s["xnT_kept"], m + 1)
                    for k in range(6):
                        f, w = FCH[k % 3]
                        f += FFN if k < 3 else 0
                        pe.matmul(fbank[k][0:w, :], W1[:, f:f + w], xnT[:], start=True, stop=True)\
                          .then_inc(s["hg_ready"], 1)
                    pe.wait_ge(s["h_ready"], 3 * m + 3)
                    for k, (f, w) in enumerate(FCH):
                        mm = pe.matmul(PA[:, 0, :], W2[0:w, k, :], H[0:w, k, :], start=(k == 0), stop=(k == 2))
                    mm.then_inc(s["yf_ready"], 1)
                    pe.wait_ge(s["xa_kept"], m + 2)

        @block.vector
        def _(dve):
            dve.wait_ge(s["consts"], 16 * 6)
            dve.sem_inc(s["xa_kept"], 1)
            with dve.Fori(0, DEPTH) as l:
                dve.wait_ge(s["aw_in"], (l + 1) * AW)
                dve.sem_inc(s["passed"], 1)
                ch = Chain(dve, s["v_chain"])
                hh = D1 // 2
                for k, sc in (("q", qsc), ("k", ksc)):
                    ch.mark(dve.tensor_tensor(tab["cos_" + k][:], rot["cos_" + k][:],
                                              sc[:].unsqueeze(1).broadcast_to([P, NT, D1]), ALU.mult))
                    for a in range(2):
                        r, o = slice(a * hh, a * hh + hh), slice((1 - a) * hh, (1 - a) * hh + hh)
                        ch.mark(dve.tensor_tensor(tab["sin_" + k][:, :, r], rot["sin_" + k][:, :, r],
                                                  sc[:, o].unsqueeze(1).broadcast_to([P, NT, hh]), ALU.mult))
                ch.close()
                with dve.Fori(0, B) as b:
                    with dve.Fori(0, NT) as i:
                        n = l * TILES + b * NT + i
                        ch = Chain(dve, s["v_chain"])

                        def rotate(src, k, ta, tb, done):
                            cs = tab["cos_" + k][:, bass.ds(i, 1), :].broadcast_to([P, HEADS, D1])
                            ch.mark(dve.tensor_tensor(heads(ta[:]), heads(flat(src)), cs, ALU.mult))
                            for a in range(2):
                                sn = tab["sin_" + k][:, bass.ds(i, 1), a * hh:a * hh + hh]\
                                    .broadcast_to([P, HEADS, hh])
                                ins = dve.tensor_tensor(halves(tb[:])[:, :, a, :], halves(flat(src))[:, :, 1 - a, :],
                                                        sn, ALU.mult)
                                if a == 0:
                                    ch.mark(ins)
                            ins.then_inc(s[done], 1)

                        dve.wait_ge(s["q_ready"], n + 1)
                        dve.wait_ge(s["sqq"], n + 1)
                        rotate(PA, "q", t1q, t2q, "tq_ready")
                        dve.wait_ge(s["sqk"], n + 1)
                        rotate(PB, "k", t1k, t2k, "tk_ready")
                        ch.mark(dve.tensor_reduce(ss[:, 0:HEADS], heads(sqa[:]), AX_X, ALU.add))
                        ch.do(dve.tensor_reduce(ss[:, HEADS:2 * HEADS], heads(sqb[:]), AX_X, ALU.add))
                        ch.do(dve.tensor_scalar(ss[:], ss[:], L2_TINY, None, ALU.max))
                        rsqrt(dve, ch, rr[:], ss[:], tn[:])
                        ch.mark(dve.tensor_scalar(rq8[:], rr[:, 0:HEADS], QK_SCALE, None, ALU.mult))
                        dve.wait_ge(s["ks_ready"], n + 1)
                        dve.tensor_tensor(heads(kr[:]), heads(kr[:]), wide(rr[:, HEADS:2 * HEADS]), ALU.mult)\
                           .then_inc(s["kr_ready"], 1)

                        def maxima(g):
                            dve.wait_ge(s["s_ready"], 4 * n + g + 1)
                            q = slice(4 * g, 4 * g + 4)
                            ch.do(dve.tensor_reduce(mx[:, q].rearrange("p (c a) -> p a c", a=2),
                                                    PD[:, :, 0:2 * KEYS].rearrange("p a (c j) -> p a c j", j=KEYS),
                                                    AX_X, ALU.max))
                            dve.scalar_tensor_tensor(out=nb[:, q], in0=mx[:, q], scalar=-1.0, in1=rq8[:, q],
                                                     op0=ALU.mult, op1=ALU.mult).then_inc(s["nb_ready"], 1)

                        def keep_p(g):
                            dve.wait_ge(s["p_turned"], 4 * n + g + 1)
                            ch.mark(dve.tensor_copy(PL[:, g % 2], turned_l))
                            dve.tensor_copy(PT[:, g % 2], turned_p).then_inc(s["p_kept"], 1)
                            ch.after()

                        for g in range(4):
                            maxima(g)
                            if g:
                                keep_p(g - 1)
                        keep_p(3)
                        ch.do(dve.reciprocal(rden[:], den[:]))
                        dve.wait_ge(s["o_ready"], n + 1)
                        dve.tensor_tensor(heads(on[:]), heads(flat(PA)), wide(rden[:]), ALU.mult)\
                           .then_inc(s["on_ready"], 1)
                        dve.wait_ge(s["y_ready"], n + 1)
                        here = lambda t: t[:, bass.ds(b, 1), bass.ds(1 + i * P, P)].rearrange("p a t -> p (a t)")
                        dve.tensor_tensor(here(XB), yA, here(XA), ALU.add).then_inc(s["xb_kept"], 1)
                dve.wait_ge(s["fw_in"], (l + 1) * FW)
                dve.sem_inc(s["passed"], 1)
                with dve.Fori(0, B) as b:
                    with dve.Fori(0, T // FTOK) as i:
                        m = l * BLOCKS + b * (T // FTOK) + i
                        ch = Chain(dve, s["f_chain"])
                        dve.wait_ge(s["xf_turned"], m + 1)
                        for c in range(4):
                            ch.mark(dve.bn_stats(st[:, c, :], PA[:, 0, c * P:c * P + P]))
                        ch.after()
                        for c in range(4):
                            ch.mark(dve.bn_aggr(mv[:, c, :], st[:, c, :]))
                        ch.after()
                        ch.do(dve.tensor_scalar(ve[:].unsqueeze(2), mv[:, :, 1:2], LN_EPS, None, ALU.add))
                        rsqrt(dve, ch, rs[:], ve[:], tv[:])
                        for c in range(4):
                            ins = dve.tensor_scalar(xn[:, c, :], PA[:, 0, c * P:c * P + P], mv[:, c, 0:1],
                                                    rs[:, c:c + 1], ALU.subtract, ALU.mult)
                        ins.then_inc(s["xn_ready"], 1)
                        for k, (f, w) in enumerate(FCH):
                            dve.wait_ge(s["hg_ready"], 6 * m + k + 4)
                            dve.wait_ge(s["g_ready"], 3 * m + k + 1)
                            dve.scalar_tensor_tensor(out=H[0:w, k, :], in0=fbank[3 + k][0:w, :], scalar=b1[0:w, k:k + 1],
                                                     in1=G[0:w, k, :], op0=ALU.add, op1=ALU.mult)\
                               .then_inc(s["h_ready"], 1)
                        dve.wait_ge(s["yf_ready"], m + 1)
                        here = lambda t: t[:, bass.ds(b, 1), bass.ds(1 + i * FTOK, FTOK)].rearrange("p a t -> p (a t)")
                        dve.scalar_tensor_tensor(out=here(XA), in0=PA[:, 0, :], scalar=b2[:, 0:1], in1=here(XB),
                                                 op0=ALU.add, op1=ALU.add).then_inc(s["xa_kept"], 1)


def store_phase(nc, io, keep):
    ident, X, XA = keep["ident"], keep["X"], keep["XA"]
    with ExitStack() as ctx:
        sem = lambda n: ctx.enter_context(nc.semaphore(n))
        tile = ctx.enter_context(nc.sbuf_tensor("tile", [P, 2, 4, P], F32))
        turned = ctx.enter_context(nc.psum_tensor("turned", [P, 2, 512], F32))
        copied, ready, added, stored = (sem(n) for n in ("z_copied", "z_ready", "z_added", "z_stored"))
        block = ctx.enter_context(nc.Block())
        QUADS = B * NT // 4

        @block.scalar
        def _(act):
            for q in range(QUADS):
                if q >= 2:
                    act.wait_ge(ready, q - 1)
                b, t = q // 2, 1 + (q % 2) * 4 * P
                act.activation(tile[:, q % 2].rearrange("p c t -> p (c t)"), XA[:, b, t:t + 4 * P], ACT.Copy)\
                   .then_inc(copied, 1)

        @block.tensor
        def _(pe):
            for q in range(QUADS):
                pe.wait_ge(copied, q + 1)
                if q >= 2:
                    pe.wait_ge(added, q - 1)
                for c in range(4):
                    mm = pe.transpose(turned[:, q % 2, c * P:c * P + P], tile[:, q % 2, c, :], ident[:])
                mm.then_inc(ready, 1)

        @block.vector
        def _(dve):
            for q in range(QUADS):
                dve.wait_ge(ready, q + 1)
                here = X[:, 4 * q:4 * q + 4, :].rearrange("p n c -> p (n c)")
                dve.tensor_tensor(here, turned[:, q % 2, :], here, ALU.add).then_inc(added, 1)

        @block.sync
        def _(sp):
            for q in range(QUADS):
                sp.wait_ge(added, q + 1)
                t = (q % 2) * 4 * P
                sp.dma_start(io["out"][q // 2, t:t + 4 * P].rearrange("(n p) c -> p n c", p=P),
                             X[:, 4 * q:4 * q + 4, :]).then_inc(stored, 16)
            sp.wait_ge(stored, 16 * QUADS)


PHASES = [load_phase, l0_phase, l1_attn_phase, l1_ffn_phase, store_phase]


def build(nc, io):
    with ExitStack() as ctx:
        keep = {
            "ident": ctx.enter_context(nc.sbuf_tensor("ident", [P, P], F32)),
            "identb": ctx.enter_context(nc.sbuf_tensor("identb", [P, P], BF16)),
            "X": ctx.enter_context(nc.sbuf_tensor("X", [P, B * NT, C], F32)),
            "XA": ctx.enter_context(nc.sbuf_tensor("XA", [P, B, 1 + T], F32)),
            "XB": ctx.enter_context(nc.sbuf_tensor("XB", [P, B, 1 + T], F32)),
        }
        for phase in PHASES:
            phase(nc, io, keep)


def constants():
    import numpy as np

    f = np.float32
    half = D0 // 2
    theta = f(10000.0) ** (-np.arange(half, dtype=f) / f(half))
    freqs = np.arange(T, dtype=f)[:, None] * theta[None, :]
    tile = lambda a: np.ascontiguousarray(a.reshape(NT, P, -1).transpose(1, 0, 2))
    out = {"cos0": tile(np.cos(freqs).astype(f)), "sin0": tile(np.sin(freqs).astype(f))}
    hf = np.arange(0, D1, 2, dtype=f)
    inv = (f(1.0) / f(10000.0) ** (hf / f(D1))).astype(f)
    fr = np.arange(T, dtype=f)[:, None] * inv[None, :]
    fr = np.concatenate([fr, fr], -1)
    base = ((hf + f(0.4 * D1)) / f(1.4 * D1)).astype(f)
    power = (np.arange(T, dtype=f) - f(T // 2)) / f(WINDOW // 2)
    sc = (base[None, :] ** power[:, None]).astype(f)
    sc = np.concatenate([sc, sc], -1)
    sign = np.where(np.arange(D1) < D1 // 2, f(-1), f(1))[None, :]
    cos, sin = np.cos(fr).astype(f), np.sin(fr).astype(f) * sign
    for name, s in (("q", sc), ("k", (f(1.0) / sc).astype(f))):
        out["cos_" + name] = tile((cos * s).astype(f))
        out["sin_" + name] = tile((sin * s).astype(f))
    t = np.arange(P, dtype=f)
    out["dist"] = np.maximum(t[None, :] - 1 - t[:, None], 0)
    out["before"] = (t[:, None] < t[None, :]).astype(f)
    out["trow"] = np.tile(t[None, :], (P, 1))
    out["trow1"] = np.ones((1, P), f)
    j, i = np.arange(KEYS)[None, :], np.arange(P)[:, None]
    seen = (j >= i) & (j <= i + WINDOW)
    first = seen & (j >= WINDOW)
    m = np.stack([first] + [seen] * (NT - 1), 1)
    m = np.where(m, f(0), f(MASKED))
    out["mask"] = np.concatenate([m, m], 2).astype(mybir.dt.np(BF16))
    out["stays"] = np.tile((np.arange(NT) < NT - 1).astype(f), (P, 1))
    out["rev"] = (P - 1 - t)[:, None]
    return out


def kernel(**inputs):
    import numpy as _np
    import concourse.bacc as _bacc
    from concourse import mybir as _mybir
    from concourse.bass_utils import run_bass_kernel_spmd as _run

    nc = _bacc.Bacc("TRN2", target_bir_lowering=False, num_devices=1)
    g = {k: _np.asarray(v) for k, v in inputs.items()}
    laid = {
        "x": g["L0_attn_x"],
        "wqkv0": _np.concatenate([g["L0_attn_Wq"].T, g["L0_attn_Wk"].T, g["L0_attn_Wv"].T], 1),
        "woT0": g["L0_attn_Wo"].T,
        "w_ffn0": g["L0_ffn_weight"],
    }
    for k, v in g.items():
        if k.startswith(("L0_attn_b", "L0_ffn_bias", "L1_")):
            laid[k] = v
    laid.update(constants())
    arrays, io = {}, {}
    for name, a in laid.items():
        if False:
            continue
        a = _np.ascontiguousarray(a)
        arrays[f"in_{name}_dram"] = a
        io[name] = nc.dram_tensor(f"in_{name}_dram", a.shape, _mybir.dt.from_np(a.dtype), kind="ExternalInput").ap()
    io["out"] = nc.dram_tensor("out_dram", (B, T, C), F32, kind="ExternalOutput").ap()
    build(nc, io)
    r = _run(nc, [arrays], core_ids=[0])
    return r.results[0]["out_dram"]
```

```python
from contextlib import ExitStack

import concourse.bass as bass
from concourse import mybir

F32 = mybir.dt.float32
BF16 = mybir.dt.bfloat16
I32 = mybir.dt.int32
ALU = mybir.AluOpType
ACT = mybir.ActivationFunctionType
AX_X = mybir.AxisListType.X

P = 128
B, T, C = 4, 1024, 128
NT = T // P
HEADS = 16
LN_EPS = 1e-5

D0 = C // HEADS
SLOT = 64
NPART = 6
SHIFT_AT = NPART * D0
SCALE0 = float(D0) ** -0.5
FP6_MAX, FP6_TINY = 7.5, 1e-30
ROUND = 1.5 * 2.0 ** 23

D1 = 64
INNER = HEADS * D1
NCH = INNER // P
RMS_EPS = 1e-5
L2_TINY = 1e-24

DEPTH = 6
WINDOW = 32
KEYS = WINDOW + P
QK_SCALE = 8.0
FFN = int(C * 4 * 2 / 3)
FCH = [(0, 128), (128, 128), (256, FFN - 256)]
FTOK = 512
MASKED = -1e30




class Chain:

    def __init__(self, eng, sem):
        self.eng, self.sem, self.n = eng, sem, 0
        eng.sem_clear(sem)

    def mark(self, ins):
        self.n += 1
        ins.then_inc(self.sem, 1)
        return self.n

    def after(self, n=None):
        self.eng.wait_ge(self.sem, self.n if n is None else n)

    def do(self, ins):
        self.mark(ins)
        self.after()

    def close(self):
        self.after()


def rsqrt_start(dve, ch, y, x):
    ch.do(dve.tensor_scalar(y.bitcast(I32), x.bitcast(I32), 1, None, ALU.logical_shift_right))
    ch.do(dve.tensor_scalar(y.bitcast(I32), y.bitcast(I32), -1.0, 1597463007.0, ALU.mult, ALU.add))


def newton(dve, ch, y, x, tmp, steps):
    for _ in range(steps):
        ch.do(dve.tensor_tensor(tmp, y, y, ALU.mult))
        ch.do(dve.scalar_tensor_tensor(out=tmp, in0=tmp, scalar=-0.5, in1=x, op0=ALU.mult, op1=ALU.mult))
        ch.do(dve.scalar_tensor_tensor(out=y, in0=tmp, scalar=1.5, in1=y, op0=ALU.add, op1=ALU.mult))


def rsqrt(dve, ch, y, x, tmp):
    rsqrt_start(dve, ch, y, x)
    newton(dve, ch, y, x, tmp, 3)


def one(t, n):
    return t[:, bass.ds(n, 1), :].rearrange("p a m -> p (a m)")


def load_phase(nc, io, keep):
    with ExitStack() as ctx:
        sem = lambda n: ctx.enter_context(nc.semaphore(n))
        loaded, ident_zero, ident_set, zeroed = sem("ld_x"), sem("ld_id0"), sem("ld_id"), sem("ld_zero")
        block = ctx.enter_context(nc.Block())
        ident, identb, X, XA, XB = keep["ident"], keep["identb"], keep["X"], keep["XA"], keep["XB"]

        @block.sync
        def _(sp):
            for b in range(B):
                sp.dma_start(X[:, NT * b:NT * b + NT, :],
                             io["x"][b].rearrange("(n p) c -> p n c", p=P)).then_inc(loaded, 16)
            sp.wait_ge(loaded, 16 * B)

        @block.gpsimd
        def _(pool):
            pool.memset(ident[:], 0.0).then_inc(ident_zero, 1)
            pool.memset(identb[:], 0.0).then_inc(ident_zero, 1)
            pool.wait_ge(ident_zero, 2)
            for m in (ident, identb):
                pool.affine_select(out=m[:], in_=m[:], compare_op=ALU.not_equal, fill=1.0, base=0,
                                   pattern=[[-1, P]], channel_multiplier=1).then_inc(ident_set, 1)
            pool.wait_ge(ident_set, 2)

        @block.vector
        def _(dve):
            dve.memset(XA[:, :, 0:1], 0.0).then_inc(zeroed, 1)
            dve.memset(XB[:, :, 0:1], 0.0).then_inc(zeroed, 1)
            dve.wait_ge(zeroed, 2)


def quantize(pool, ch, u, scale, out, a, g):
    ch.do(pool.tensor_tensor(a, u, u, ALU.mult))
    ch.do(pool.tensor_scalar(g, a, 4.0, -4.0, ALU.is_ge, ALU.mult))
    ch.do(pool.tensor_scalar(a, a, 16.0, -2.0, ALU.is_ge, ALU.mult))
    ch.do(pool.tensor_tensor(g, g, a, ALU.add))
    ch.do(pool.tensor_scalar(g, g, 8.0, None, ALU.add))
    ch.do(pool.tensor_tensor(u, u, g, ALU.mult))
    ch.do(pool.tensor_scalar(a, u, ROUND, -ROUND, ALU.add, ALU.add))
    ch.do(pool.tensor_tensor(u, a, u, ALU.subtract))
    ch.do(pool.tensor_scalar(u, u, 0.5, None, ALU.is_ge))
    ch.do(pool.tensor_tensor(a, a, u, ALU.subtract))
    ch.do(pool.tensor_scalar(u, g, -14.0, None, ALU.add))
    ch.do(pool.tensor_tensor(u, u, g, ALU.mult))
    ch.do(pool.tensor_scalar(u, u, 56.0, 1.0 / 64.0, ALU.add, ALU.mult))
    ch.do(pool.tensor_tensor(a, a, u, ALU.mult))
    return pool.tensor_tensor(out, a, scale, ALU.mult)



def block_scales(dve, ch, x, mx, inv, u):
    ch.do(dve.tensor_reduce(mx, x.rearrange("p (k j) -> p k j", j=32), AX_X, ALU.max,
                            apply_absolute_value=True))
    ch.do(dve.tensor_scalar(mx, mx, 1.0 / FP6_MAX, FP6_TINY, ALU.mult, ALU.max))
    ch.do(dve.reciprocal(inv, mx))
    return dve.tensor_tensor(u.rearrange("p (k j) -> p k j", j=32), x.rearrange("p (k j) -> p k j", j=32),
                             wide(inv), ALU.mult)


def blocks(t):
    return t.rearrange("p (k j) -> p k j", j=32)


def wide(mx):
    return mx.unsqueeze(2).broadcast_to([P, C // 32, 32])


def l0_phase(nc, io, keep):
    ident, identb, X, XA = keep["ident"], keep["identb"], keep["X"], keep["XA"]
    with ExitStack() as ctx:
        sem = lambda n: ctx.enter_context(nc.semaphore(n))
        sb = lambda n, s, d=F32: ctx.enter_context(nc.sbuf_tensor(n, s, d))
        ps = lambda n, s, d=F32: ctx.enter_context(nc.psum_tensor(n, s, d))

        wqkv = sb("wqkv0", [P, 3 * C])
        bqkv = sb("bqkv0", [P, 3 * C])
        wo = sb("wo0", [P, C])
        bsum = sb("bsum", [P, C])
        fbias = sb("fbias", [P, C])
        wraw = sb("wraw", [P, C])
        wdq = sb("wdq", [P, C])
        wdT = sb("wdT", [P, C])
        cos = sb("cos0", [P, NT, 4])
        sin = sb("sin0", [P, NT, 4])
        nsin = sb("nsin0", [P, NT, 4])
        st = sb("st0", [P, 6])
        mv = sb("mv0", [P, 2])
        ve, rs, nt_ = sb("ve0", [P, 1]), sb("rs0", [P, 1]), sb("nt0", [P, 1])
        xn = sb("xn0", [P, C])
        u, ua, ug = sb("u0", [P, C]), sb("ua0", [P, C]), sb("ug0", [P, C])
        mx6, inv6 = sb("mx6", [P, C // 32]), sb("inv6", [P, C // 32])
        xnT = sb("xnT0", [P, C])
        qkv = sb("qkv0", [P, 3 * C])
        t1, t2 = sb("ropea", [P, 2 * C]), sb("ropeb", [P, 2 * C])
        hi, mid, lo = sb("hi", [P, 2 * C], BF16), sb("mid", [P, 2 * C], BF16), sb("lo", [P, 2 * C], BF16)
        Ktok = sb("Ktok", [P, HEADS, SLOT], BF16)
        Qtok = sb("Qtok", [P, NT, HEADS, SLOT], BF16)
        Qs = sb("Qs", [P, HEADS, SLOT], BF16)
        kT = sb("kT0", [P, NCH, T], BF16)
        qTm = sb("qTm", [P, NCH, P], BF16)
        qTe = sb("qTe", [P, NCH, P], BF16)
        Vaug = sb("Vaug", [P, NT, HEADS, D0 + 1])
        XD = sb("XD", [P, NT, C])
        mx = sb("mx0", [P, HEADS])
        m1 = sb("m1", [P, HEADS])
        PT = sb("PT0", [P, 4, NT, P])
        oS = sb("oS", [P, 4, P])
        rden = sb("rden0", [P, HEADS])
        att = sb("att0", [P, C])
        attT = sb("attT0", [P, C])
        xds = sb("xds", [P, C])
        xdT = sb("xdT", [P, C])
        x1 = sb("x1", [P, C])
        xn2 = sb("xn2", [P, C])

        pS = ps("pS", [P, 2, 512])
        pE = ps("pE", [P, 2, NT, P])
        pE2 = pE[:, 0].rearrange("p (a c) t -> p a (c t)", a=2)
        pM = ps("pM", [P, 512])
        pTb = pM[:].bitcast(BF16).rearrange("p (c t) -> p c t", t=P)
        pO = ps("pO", [P, 4, P])
        oh = pM[:].rearrange("p (h d) -> p h d", d=32)
        pP = pS[:, 0, 0:3 * C]
        pX = pS[:, 1, 0:P]
        pA, pX2, pY, pN = (pM[:, k * P:k * P + P] for k in range(4))

        names = ["w_in", "passed", "w_over", "w_quant", "w_turned", "w_kept", "p_chain", "v_chain", "xn_ready", "u_ready",
                 "xd_kept", "xn_turned", "xn_kept", "qkv_ready", "parts_ready", "k_slots", "q_slots", "k_turned", "k_kept",
                 "preset", "b_chain", "q_copied", "q_turned", "q_kept", "s_ready", "max_done", "qe_copied",
                 "qe_turned", "qe_kept", "e_ready", "exp_done", "o_cleared", "o_ready", "o_kept", "o_back", "att_ready", "xd_copied", "out_turned",
                 "out_kept", "y_ready", "xn2_ready", "xn2_turned", "xn2_kept"]
        s = {n: sem("l0_" + n) for n in names}
        block = ctx.enter_context(nc.Block())

        def rounds(eng):
            return eng.Fori(0, B)

        PAIRS = HEADS // 2
        SCORED = (0, 1, 4, 7, 10, 12, 14, 16, 16)

        @block.sync
        def _(sp):
            for dst, src in ((wqkv, "wqkv0"), (wo, "woT0"), (wraw, "w_ffn0"), (cos, "cos0"), (sin, "sin0")):
                sp.dma_start(dst[:], io[src]).then_inc(s["w_in"], 16)
            for k, n in enumerate(("L0_attn_bq", "L0_attn_bk", "L0_attn_bv")):
                sp.dma_start(bqkv[:, k * C:k * C + C], io[n].partition_broadcast(P)).then_inc(s["w_in"], 16)
            sp.dma_start(bsum[:], io["L0_attn_bo"].partition_broadcast(P)).then_inc(s["w_in"], 16)
            sp.dma_start(fbias[:], io["L0_ffn_bias"].partition_broadcast(P)).then_inc(s["w_in"], 16)

        W_IN = 16 * 10

        @block.gpsimd
        def _(pool):
            pool.memset(Ktok[:], 0.0).then_inc(s["preset"], 1)
            pool.memset(Qtok[:], 0.0).then_inc(s["preset"], 1)
            pool.memset(Vaug[:], 1.0).then_inc(s["preset"], 1)
            pool.wait_ge(s["preset"], 3)
            pool.memset(Ktok[:, :, SHIFT_AT:SHIFT_AT + 3], 1.0).then_inc(s["preset"], 1)
            pool.wait_ge(s["preset"], 4)
            pool.wait_ge(s["w_over"], 1)
            ch = Chain(pool, s["p_chain"])
            quantize(pool, ch, blocks(u[:]), wide(mx6[:]), blocks(wdq[:]), blocks(ua[:]), blocks(ug[:])).then_inc(s["w_quant"], 1)
            with rounds(pool) as b:
                with pool.Fori(0, NT) as i:
                    n = b * NT + i
                    ch = Chain(pool, s["p_chain"])
                    pool.wait_ge(s["u_ready"], n + 1)
                    pool.sem_inc(s["passed"], 1)
                    quantize(pool, ch, blocks(u[:]), wide(mx6[:]),
                             XD[:, bass.ds(i, 1), :].rearrange("p a (k j) -> p (a k) j", j=32),
                             blocks(ua[:]), blocks(ug[:])).then_inc(s["xd_kept"], 1)
                    ch.close()
                pool.wait_ge(s["xd_kept"], (b + 1) * NT)
                pool.sem_inc(s["passed"], 1)
                with pool.Fori(0, NT) as i:
                    n = b * NT + i
                    pool.tensor_copy(xds[:], one(XD, i)).then_inc(s["xd_copied"], 1)
                    pool.wait_ge(s["out_turned"], n + 1)
                    pool.sem_inc(s["passed"], 1)

        @block.scalar
        def _(act):
            act.wait_ge(s["w_turned"], 1)
            act.activation(wdT[:], pX, ACT.Copy).then_inc(s["w_kept"], 1)
            with rounds(act) as b:
                def keep_xn(n):
                    act.wait_ge(s["xn_turned"], n + 1)
                    act.activation(xnT[:], pX, ACT.Copy).then_inc(s["xn_kept"], 1)

                def slots(n, i):
                    act.wait_ge(s["parts_ready"], n + 1)
                    hh = lambda t, a: t[:, a * C:a * C + C].rearrange("p (h d) -> p h d", h=HEADS)
                    qd = Qtok[:, bass.ds(i, 1), :, :].rearrange("p a h d -> p (a h) d")

                    def put(t, k, src, a, m):
                        dst = t[:, :, a * D0:(a + m) * D0]
                        sr = hh(src, k)
                        if m > 1:
                            dst = dst.rearrange("p h (m d) -> p h m d", m=m)
                            sr = sr.unsqueeze(2).broadcast_to([P, HEADS, m, D0])
                        return act.activation(dst, sr, ACT.Copy)
                    put(Ktok, 1, hi, 0, 1)
                    put(Ktok, 1, hi, 3, 2)
                    put(Ktok, 1, mid, 1, 1)
                    put(Ktok, 1, mid, 5, 1)
                    put(Ktok, 1, lo, 2, 1).then_inc(s["k_slots"], 1)
                    put(qd, 0, hi, 0, 3)
                    put(qd, 0, mid, 3, 1)
                    put(qd, 0, mid, 5, 1)
                    put(qd, 0, lo, 4, 1).then_inc(s["q_slots"], 1)

                def keep_k(n, i):
                    act.wait_ge(s["k_turned"], n + 1)
                    act.activation(kT[:, :, bass.ds(i * P, P)], pTb, ACT.Copy).then_inc(s["k_kept"], 1)

                keep_xn(b * NT)
                with act.Fori(0, NT - 1) as i:
                    n = b * NT + i
                    slots(n, i)
                    keep_xn(n + 1)
                    keep_k(n, i)
                slots(b * NT + NT - 1, NT - 1)
                keep_k(b * NT + NT - 1, NT - 1)

                def keep_q(n):
                    act.wait_ge(s["q_turned"], n + 1)
                    act.activation(qTm[:], pTb, ACT.Copy).then_inc(s["q_kept"], 1)

                def keep_qe(n):
                    act.wait_ge(s["qe_turned"], n + 1)
                    act.activation(qTe[:], pTb, ACT.Copy).then_inc(s["qe_kept"], 1)

                def keep_o(n):
                    act.wait_ge(s["o_ready"], (n + 1) * PAIRS)
                    act.activation(oS[:].rearrange("p g t -> p (g t)"), pO[:].rearrange("p g t -> p (g t)"),
                                   ACT.Copy).then_inc(s["o_kept"], 1)

                def keep_out(n):
                    act.wait_ge(s["out_turned"], n + 1)
                    act.activation(attT[:], pA, ACT.Copy).then_inc(s["out_kept"], 1)
                    act.activation(xdT[:], pX2, ACT.Copy).then_inc(s["out_kept"], 1)

                def keep_xn2(n, i):
                    act.wait_ge(s["xn2_turned"], n + 1)
                    act.activation(XA[:, bass.ds(b, 1), bass.ds(1 + i * P, P)].rearrange("p a t -> p (a t)"),
                                   pN, ACT.Copy).then_inc(s["xn2_kept"], 1)

                def tile(n, i, ahead, behind):
                    if behind:
                        keep_o(n - 1)
                    for h in range(HEADS):
                        act.wait_ge(s["e_ready"], n * HEADS + h + 1)
                        if h >= 4:
                            act.wait_ge(s["o_ready"], n * PAIRS + h // 2 - 1)
                        act.activation(PT[:, h % 4], pE[:, h % 2], ACT.Exp, scale=SCALE0)\
                           .then_inc(s["exp_done"], 1)
                        if ahead and h == 0:
                            keep_q(n + 1)
                        if behind and h == 6:
                            keep_out(n - 1)
                        if behind and h == 14:
                            keep_xn2(n - 1, i - 1)
                    if ahead:
                        keep_qe(n + 1)

                first, last = b * NT, b * NT + NT - 1
                keep_q(first)
                keep_qe(first)
                tile(first, 0, True, False)
                with act.Fori(1, NT - 1) as i:
                    tile(b * NT + i, i, True, True)
                tile(last, NT - 1, False, True)
                keep_o(last)
                keep_out(last)
                keep_xn2(last, NT - 1)

        @block.tensor
        def _(pe):
            pe.wait_ge(s["w_quant"], 1)
            pe.transpose(pX, wdq[:], ident[:]).then_inc(s["w_turned"], 1)
            pe.wait_ge(s["w_in"], W_IN)
            pe.wait_ge(s["w_kept"], 1)
            pe.wait_ge(s["o_cleared"], 1)
            with rounds(pe) as b:
                def project_qkv(n):
                    pe.wait_ge(s["xn_ready"], n + 1)
                    pe.transpose(pX, xn[:], ident[:]).then_inc(s["xn_turned"], 1)
                    pe.wait_ge(s["xn_kept"], n + 1)
                    pe.matmul(pP, xnT[:], wqkv[:], start=True, stop=True).then_inc(s["qkv_ready"], 1)

                def turn_k(n):
                    pe.wait_ge(s["k_slots"], n + 1)
                    for c in range(NCH):
                        mm = pe.transpose(pTb[:, c, :], Ktok[:, 2 * c:2 * c + 2, :].rearrange("p h d -> p (h d)"),
                                          identb[:])
                    mm.then_inc(s["k_turned"], 1)

                project_qkv(b * NT)
                with pe.Fori(0, NT - 1) as i:
                    turn_k(b * NT + i)
                    pe.wait_ge(s["parts_ready"], b * NT + i + 1)
                    project_qkv(b * NT + i + 1)
                    pe.wait_ge(s["k_kept"], b * NT + i + 1)
                turn_k(b * NT + NT - 1)
                pe.wait_ge(s["k_kept"], (b + 1) * NT)

                def turn_q(n, done, turned):
                    pe.wait_ge(s[done], n + 1)
                    for c in range(NCH):
                        mm = pe.transpose(pTb[:, c, :], Qs[:, 2 * c:2 * c + 2, :].rearrange("p h d -> p (h d)"),
                                          identb[:])
                    mm.then_inc(s[turned], 1)

                def head_rows(h):
                    return slice(SLOT * (h % 2), SLOT * (h % 2) + SLOT)

                def scores(n, h, bank=pS[:], banks=1):
                    r = head_rows(h)
                    if h == 0:
                        pe.wait_ge(s["q_kept"], n + 1)
                    if h >= banks:
                        pe.wait_ge(s["max_done"], n * HEADS + h - banks + 1)
                    for a in range(2):
                        mm = pe.matmul(bank[:, a, :], qTm[r, h // 2, :], kT[r, h // 2, a * 512:a * 512 + 512],
                                       start=True, stop=True)
                    mm.then_inc(s["s_ready"], 1)

                def exponents(n, h):
                    r = head_rows(h)
                    if h == 0:
                        pe.wait_ge(s["qe_kept"], n + 1)
                    if h >= 2:
                        pe.wait_ge(s["exp_done"], n * HEADS + h - 1)
                    for j in range(NT):
                        mm = pe.matmul(pE[:, h % 2, j, :], kT[r, h // 2, j * P:j * P + P], qTe[r, h // 2, :],
                                       start=True, stop=True)
                    mm.then_inc(s["e_ready"], 1)

                def values(n, p, js):
                    if js[0] == 0:
                        pe.wait_ge(s["exp_done"], n * HEADS + 2 * p + 2)
                    for j in js:
                        for h in (2 * p, 2 * p + 1):
                            r = 32 * (h % 4)
                            mm = pe.matmul(pO[r:r + D0 + 1, h // 4, :], Vaug[:, j, h, :], PT[:, h % 4, j, :],
                                           start=(j == 0), stop=(j == NT - 1), skip_group_check=True)
                    if js[-1] == NT - 1:
                        mm.then_inc(s["o_ready"], 1)

                def turn_o(n):
                    pe.wait_ge(s["o_kept"], n + 1)
                    for g in range(4):
                        mm = pe.transpose(pM[:, g * P:g * P + P], oS[:, g, :], ident[:])
                    mm.then_inc(s["o_back"], 1)

                def turn_out(n):
                    pe.wait_ge(s["att_ready"], n + 1)
                    pe.transpose(pA, att[:], ident[:])
                    pe.wait_ge(s["xd_copied"], n + 1)
                    pe.transpose(pX2, xds[:], ident[:]).then_inc(s["out_turned"], 1)

                def project(n):
                    pe.wait_ge(s["out_kept"], 2 * n + 2)
                    pe.matmul(pY, attT[:], wo[:], start=True, stop=False)
                    pe.matmul(pY, xdT[:], wdT[:], start=False, stop=True).then_inc(s["y_ready"], 1)

                def turn_xn2(n):
                    pe.wait_ge(s["xn2_ready"], n + 1)
                    pe.transpose(pN, xn2[:], ident[:]).then_inc(s["xn2_turned"], 1)

                def tile(n, ahead, behind):
                    exponents(n, 0)
                    if ahead:
                        turn_q(n + 1, "q_copied", "q_turned")
                    exponents(n, 1)
                    if behind:
                        pe.wait_ge(s["o_kept"], n)
                    for p in range(PAIRS):
                        for h in (2 * p + 2, 2 * p + 3):
                            if h < HEADS:
                                exponents(n, h)
                        if behind and p == 1:
                            if ahead:
                                pe.wait_ge(s["q_kept"], n + 2)
                            turn_o(n - 1)
                        if behind and p == 2:
                            turn_out(n - 1)
                        if behind and p == 3:
                            project(n - 1)
                        if behind and p == 6:
                            turn_xn2(n - 1)
                        if ahead and p == 7:
                            if behind:
                                pe.wait_ge(s["xn2_kept"], n)
                            turn_q(n + 1, "qe_copied", "qe_turned")
                        g = SCORED[p]
                        for k, js in enumerate(((0, 1, 2), (3, 4, 5), (6, 7))):
                            if ahead and g + k < SCORED[p + 1]:
                                scores(n + 1, g + k)
                            values(n, p, js)

                first, last = b * NT, b * NT + NT - 1
                turn_q(first, "q_copied", "q_turned")
                for h in range(HEADS):
                    scores(first, h, (pS[:], pE2)[h % 2], 2)
                turn_q(first, "qe_copied", "qe_turned")
                tile(first, True, False)
                with pe.Fori(1, NT - 1) as i:
                    tile(b * NT + i, True, True)
                tile(last, False, True)
                turn_o(last)
                turn_out(last)
                project(last)
                turn_xn2(last)
                pe.wait_ge(s["xn2_kept"], (b + 1) * NT)
                pe.sem_inc(s["passed"], 1)

        def statistics(dve, ch, x):
            ch.do(dve.bn_stats(st[:], x))
            ch.do(dve.bn_aggr(mv[:], st[:]))
            ch.do(dve.tensor_scalar(ve[:], mv[:, 1:2], LN_EPS, None, ALU.add))
            rsqrt_start(dve, ch, rs[:], ve[:])

        def normalized(dve, x, out):
            return dve.tensor_scalar(out, x, mv[:, 0:1], rs[:, 0:1], ALU.subtract, ALU.mult)

        @block.vector
        def _(dve):
            dve.wait_ge(s["w_in"], W_IN)
            ch = Chain(dve, s["v_chain"])
            ch.mark(dve.tensor_tensor(bsum[:], bsum[:], fbias[:], ALU.add))
            block_scales(dve, ch, wraw[:], mx6[:], inv6[:], u[:]).then_inc(s["w_over"], 1)
            ch.do(dve.tensor_scalar(nsin[:], sin[:], -1.0, None, ALU.mult))
            ch.close()
            dve.wait_ge(s["w_quant"], 1)
            dve.memset(pO[:].rearrange("p g t -> p (g t)"), 0.0).then_inc(s["o_cleared"], 1)
            dve.wait_ge(s["o_cleared"], 1)
            with rounds(dve) as b:
                def norm(n, ch, others):
                    statistics(dve, ch, one(X, n))
                    newton(dve, ch, rs[:], ve[:], nt_[:], 3)
                    normalized(dve, one(X, n), xn[:]).then_inc(s["xn_ready"], 1)
                    dve.wait_ge(s["xn_ready"], n + 1)
                    if others:
                        dve.wait_ge(s["xd_kept"], n)
                    block_scales(dve, ch, xn[:], mx6[:], inv6[:], u[:]).then_inc(s["u_ready"], 1)

                def parts(n, i, ch, others):
                    dve.wait_ge(s["qkv_ready"], n + 1)
                    ch.do(dve.tensor_tensor(qkv[:], pP, bqkv[:], ALU.add))
                    v4 = lambda t: t[:, 0:2 * C].rearrange("p (h a j) -> p h a j", a=2, j=D0 // 2)
                    cb = cos[:, bass.ds(i, 1), :].unsqueeze(2).broadcast_to([P, 2 * HEADS, 2, D0 // 2])
                    sn = nsin[:, bass.ds(i, 1), :].broadcast_to([P, 2 * HEADS, D0 // 2])
                    sp_ = sin[:, bass.ds(i, 1), :].broadcast_to([P, 2 * HEADS, D0 // 2])
                    ch.mark(dve.tensor_tensor(v4(t1), v4(qkv), cb, ALU.mult))
                    ch.mark(dve.tensor_tensor(v4(t2)[:, :, 0, :], v4(qkv)[:, :, 1, :], sn, ALU.mult))
                    ch.do(dve.tensor_tensor(v4(t2)[:, :, 1, :], v4(qkv)[:, :, 0, :], sp_, ALU.mult))
                    ch.do(dve.tensor_tensor(t1[:], t1[:], t2[:], ALU.add))
                    if others:
                        dve.wait_ge(s["q_slots"], n)
                    ch.do(dve.tensor_copy(hi[:], t1[:]))
                    ch.do(dve.tensor_tensor(t1[:], t1[:], hi[:], ALU.subtract))
                    ch.do(dve.tensor_copy(mid[:], t1[:]))
                    ch.do(dve.tensor_tensor(t1[:], t1[:], mid[:], ALU.subtract))
                    dve.tensor_copy(lo[:], t1[:]).then_inc(s["parts_ready"], 1)
                    ch.mark(dve.tensor_copy(Vaug[:, bass.ds(i, 1), :, 0:D0].rearrange("p a h d -> p (a h) d"),
                                            qkv[:, 2 * C:3 * C].rearrange("p (h d) -> p h d", h=HEADS)))

                ch = Chain(dve, s["v_chain"])
                norm(b * NT, ch, False)
                parts(b * NT, 0, ch, False)
                norm(b * NT + 1, ch, True)
                ch.close()
                with dve.Fori(1, NT - 1) as i:
                    ch = Chain(dve, s["v_chain"])
                    parts(b * NT + i, i, ch, True)
                    norm(b * NT + i + 1, ch, True)
                    dve.wait_ge(s["parts_ready"], b * NT + i + 1)
                    dve.wait_ge(s["u_ready"], b * NT + i + 2)
                    dve.sem_inc(s["passed"], 1)
                    ch.close()
                ch = Chain(dve, s["v_chain"])
                parts(b * NT + NT - 1, NT - 1, ch, True)
                dve.wait_ge(s["xd_kept"], (b + 1) * NT)
                dve.wait_ge(s["q_slots"], (b + 1) * NT)
                dve.sem_inc(s["passed"], 1)
                ch.close()

                def copy_q(n, i):
                    qi = Qtok[:, bass.ds(i, 1), :, :].rearrange("p a h d -> p (a h d)")
                    dve.tensor_copy(Qs[:].rearrange("p h d -> p (h d)"), qi).then_inc(s["q_copied"], 1)

                def maximum(n, h, bank):
                    dve.wait_ge(s["s_ready"], n * HEADS + h + 1)
                    dve.tensor_reduce(mx[:, h:h + 1], bank.rearrange("p a k -> p (a k)"), AX_X, ALU.max)\
                       .then_inc(s["max_done"], 1)

                def add_maxima(n, ch):
                    at = lambda k: Qs[:, :, SHIFT_AT + k:SHIFT_AT + k + 1].rearrange("p h d -> p (h d)")
                    dve.wait_ge(s["max_done"], (n + 1) * HEADS)
                    dve.wait_ge(s["q_turned"], n + 1)
                    ch.do(dve.tensor_scalar(m1[:], mx[:], -1.0, None, ALU.mult))
                    ch.do(dve.tensor_copy(at(0), m1[:]))
                    ch.do(dve.tensor_tensor(m1[:], m1[:], at(0), ALU.subtract))
                    ch.do(dve.tensor_copy(at(1), m1[:]))
                    ch.do(dve.tensor_tensor(m1[:], m1[:], at(1), ALU.subtract))
                    dve.tensor_copy(at(2), m1[:]).then_inc(s["qe_copied"], 1)

                def divide(n, ch):
                    dve.wait_ge(s["o_back"], n + 1)
                    ch.do(dve.reciprocal(rden[:], oh[:, :, D0:D0 + 1].rearrange("p h d -> p (h d)")))
                    dve.tensor_tensor(att[:].rearrange("p (h d) -> p h d", h=HEADS), oh[:, :, 0:D0],
                                      rden[:].unsqueeze(2).broadcast_to([P, HEADS, D0]), ALU.mult)\
                       .then_inc(s["att_ready"], 1)

                def residual(n, ch):
                    dve.wait_ge(s["y_ready"], n + 1)
                    ch.do(dve.tensor_tensor(x1[:], pY, bsum[:], ALU.add))
                    ch.do(dve.tensor_tensor(x1[:], x1[:], one(X, n), ALU.add))
                    ch.do(dve.tensor_copy(one(X, n), x1[:]))

                def tile(n, i, ahead, behind):
                    ch = Chain(dve, s["b_chain"])
                    if ahead:
                        dve.wait_ge(s["qe_turned"], n + 1)
                        copy_q(n + 1, i + 1)
                    for h in range(HEADS):
                        if ahead:
                            maximum(n + 1, h, pS[:])
                        if behind and h == 1:
                            divide(n - 1, ch)
                        if behind and h == 7:
                            residual(n - 1, ch)
                        if behind and h == 8:
                            statistics(dve, ch, x1[:])
                        if behind and h == 9:
                            newton(dve, ch, rs[:], ve[:], nt_[:], 2)
                        if behind and h == 10:
                            newton(dve, ch, rs[:], ve[:], nt_[:], 1)
                            normalized(dve, x1[:], xn2[:]).then_inc(s["xn2_ready"], 1)
                    if ahead:
                        add_maxima(n + 1, ch)
                    if behind:
                        dve.wait_ge(s["xn2_turned"], n)
                        dve.sem_inc(s["passed"], 1)
                        ch.close()

                first, last = b * NT, b * NT + NT - 1
                ch = Chain(dve, s["b_chain"])
                copy_q(first, 0)
                for h in range(HEADS):
                    maximum(first, h, (pS[:], pE2)[h % 2])
                add_maxima(first, ch)
                ch.close()
                tile(first, 0, True, False)
                with dve.Fori(1, NT - 1) as i:
                    tile(b * NT + i, i, True, True)
                tile(last, NT - 1, False, True)
                ch = Chain(dve, s["b_chain"])
                divide(last, ch)
                residual(last, ch)
                statistics(dve, ch, x1[:])
                newton(dve, ch, rs[:], ve[:], nt_[:], 3)
                normalized(dve, x1[:], xn2[:]).then_inc(s["xn2_ready"], 1)
                ch.close()
                dve.wait_ge(s["xn2_turned"], (b + 1) * NT)
                dve.sem_inc(s["passed"], 1)


def l1_attn_phase(nc, io, keep):
    ident, X, XA = keep["ident"], keep["X"], keep["XA"]
    with ExitStack() as ctx:
        sem = lambda n: ctx.enter_context(nc.semaphore(n))
        sb = lambda n, s, d=F32: ctx.enter_context(nc.sbuf_tensor(n, s, d))
        ps = lambda n, s, d=F32: ctx.enter_context(nc.psum_tensor(n, s, d))

        W5 = sb("W5", [P, 5, INNER])
        wb = sb("wb", [P, HEADS])
        wo = sb("wo1", [P, NCH, C])
        brow = sb("brow1", [1, 2, INNER])
        ones = sb("ones1", [1, P])
        alog, neA = sb("alog", [P, HEADS]), sb("neA", [P, HEADS])
        alogF, neAF = sb("alogF", [P, NCH]), sb("neAF", [P, NCH])
        dist, before = sb("dist", [P, P]), sb("before", [P, P])
        trow, rev = sb("trow", [P, P]), sb("rev", [P, 1])
        nw = sb("nw", [P, D1])
        Dec = sb("Dec", [P, 2, NCH, P])
        decT = sb("decT", [P, NCH, P])
        A128 = sb("A128", [P, NCH])
        kdec = sb("kdec", [P, HEADS])
        xT = sb("xT1", [P, P])
        qs, ks, vs = sb("qs1", [P, INNER]), sb("ks1", [P, INNER]), sb("vs1", [P, INNER])
        fs, gs = sb("fs1", [P, INNER]), sb("gs1", [P, INNER])
        sqa, sqb = sb("sqa1", [P, INNER]), sb("sqb1", [P, INNER])
        bt, bv = sb("bt1", [P, HEADS]), sb("bv1", [P, HEADS])
        ss, rr, tn = sb("ss1", [P, 2 * HEADS]), sb("rr1", [P, 2 * HEADS]), sb("tn1", [P, 2 * HEADS])
        qT, kT, qdT = sb("qT1", [P, NCH, P]), sb("kT1", [P, NCH, P]), sb("qdT1", [P, NCH, P])
        vp, kp = sb("vp1", [P, INNER]), sb("kp1", [P, INNER])
        Wd = sb("Wd1", [P, 2, NCH, P])
        St, StA = sb("St", [P, NCH, D1]), sb("StA", [P, NCH, D1])
        o1, oT = sb("o1", [P, INNER]), sb("oT1", [P, NCH, P])

        PA, PB = ps("PA1", [P, 2, 512]), ps("PB1", [P, 2, 512])
        PC, PD = ps("PC1", [P, 2, 512]), ps("PD1", [P, 2, 512])
        flat = lambda t: t[:].rearrange("p a k -> p (a k)")
        tiles = lambda t: t[:].rearrange("p a (c t) -> p (a c) t", t=P)
        heads = lambda t: t.rearrange("p (h d) -> p h d", d=D1)
        wide = lambda t: t.unsqueeze(2).broadcast_to([P, HEADS, D1])
        o_feat = PA[:].rearrange("p a (c d) -> p c a d", d=D1)
        feat4 = lambda t: t.rearrange("p (c a d) -> p c a d", a=2, d=D1)

        names = ["w_in", "passed", "t_chain", "t_exp", "v_chain", "p_chain", "x_kept", "q_ready", "k_ready", "v_ready",
                 "b_ready", "f_ready", "g_ready", "q_kept", "k_kept", "v_kept", "b_kept", "f_kept", "g_kept",
                 "sqq", "sqk", "r_ready", "q_turned", "k_turned", "qT_kept", "kT_kept", "qd_ready", "vp_ready",
                 "kp_ready", "gq_ready", "gw_ready", "s_ready", "w_ready", "o_ready", "st_ready", "st_kept",
                 "o1_ready", "sqo", "o2_ready", "o_turned", "oT_kept", "y_ready", "y_kept", "tables", "st_zeroed"]
        s = {n: sem("l1_" + n) for n in names}
        W_IN = 16 * 18
        block = ctx.enter_context(nc.Block())

        @block.sync
        def _(sp):
            load = lambda dst, src: sp.dma_start(dst, src).then_inc(s["w_in"], 16)
            for k, n in enumerate(("Wq", "Wk", "Wv", "Wf", "Wg")):
                load(W5[:, k, :], io["L1_attn_" + n])
            load(wb[:], io["L1_attn_Wb"])
            load(wo[:], io["L1_attn_Wo"].rearrange("(c p) n -> p c n", p=P))
            load(brow[:, 0, :], io["L1_attn_dt_bias"].rearrange("(a n) -> a n", a=1))
            load(brow[:, 1, :], io["L1_attn_bg"].rearrange("(a n) -> a n", a=1))
            load(alog[:], io["L1_attn_A_log"].partition_broadcast(P))
            pairs = io["L1_attn_A_log"].rearrange("(c a) -> a c", a=2)
            with nc.allow_non_contiguous_dma(reason="8 values"):
                load(alogF[0:D1, :], pairs[0].partition_broadcast(D1))
                load(alogF[D1:P, :], pairs[1].partition_broadcast(D1))
            load(nw[:], io["L1_attn_norm_w"].partition_broadcast(P))
            load(dist[:], io["dist"])
            load(before[:], io["before"])
            load(trow[:], io["trow"])
            load(rev[:], io["rev"])
            load(ones[:], io["trow1"])

        @block.gpsimd
        def _(pool):
            pool.wait_ge(s["w_in"], W_IN)
            with pool.Fori(0, B * NT) as n:
                ch = Chain(pool, s["p_chain"])
                pool.wait_ge(s["k_kept"], n + 1)
                pool.sem_inc(s["passed"], 1)
                pool.tensor_tensor(heads(kp[:]), heads(ks[:]), wide(kdec[:]), ALU.mult).then_inc(s["kp_ready"], 1)
                pool.wait_ge(s["f_kept"], n + 1)
                pool.sem_inc(s["passed"], 1)
                pool.wait_ge(s["r_ready"], n + 1)
                pool.sem_inc(s["passed"], 1)
                pool.tensor_tensor(heads(fs[:]), heads(fs[:]), wide(rr[:, 0:HEADS]), ALU.mult)\
                    .then_inc(s["gq_ready"], 1)
                pool.wait_ge(s["g_kept"], n + 1)
                pool.sem_inc(s["passed"], 1)
                pool.tensor_tensor(heads(gs[:]), heads(gs[:]), nw[:].unsqueeze(1).broadcast_to([P, HEADS, D1]),
                                   ALU.mult).then_inc(s["gw_ready"], 1)

        @block.scalar
        def _(act):
            act.wait_ge(s["w_in"], W_IN)
            act.activation(neA[:], alog[:], ACT.Exp).then_inc(s["t_exp"], 1)
            act.activation(neAF[:], alogF[:], ACT.Exp).then_inc(s["t_exp"], 1)
            act.wait_ge(s["t_chain"], 2)
            for h in range(HEADS):
                act.activation(Dec[:, h % 2, h // 2, :], dist[:], ACT.Exp, scale=neA[:, h:h + 1])\
                   .then_inc(s["t_exp"], 1)
            for c in range(NCH):
                act.activation(decT[:, c, :], trow[:], ACT.Exp, scale=neAF[:, c:c + 1])
            act.activation(A128[:], neAF[:], ACT.Exp, scale=float(P))
            act.activation(kdec[:], neA[:], ACT.Exp, scale=rev[:, 0:1]).then_inc(s["tables"], 1)
            with act.Fori(0, B) as b:
                with act.Fori(0, NT) as i:
                    n = b * NT + i
                    act.activation(xT[:], XA[:, bass.ds(b, 1), bass.ds(1 + i * P, P)].rearrange("p a t -> p (a t)"),
                                   ACT.Copy).then_inc(s["x_kept"], 1)
                    for src, dst, r, k in ((PA, qs, "q_ready", "q_kept"), (PB, ks, "k_ready", "k_kept"),
                                           (PC, vs, "v_ready", "v_kept")):
                        act.wait_ge(s[r], n + 1)
                        act.activation(dst[:], flat(src), ACT.Silu).then_inc(s[k], 1)
                    act.wait_ge(s["k_kept"], n + 1)
                    act.activation(sqa[:], qs[:], ACT.Square).then_inc(s["sqq"], 1)
                    act.activation(sqb[:], ks[:], ACT.Square).then_inc(s["sqk"], 1)
                    act.wait_ge(s["b_ready"], n + 1)
                    act.activation(bt[:], PD[:, 0, 0:HEADS], ACT.Sigmoid).then_inc(s["b_kept"], 1)
                    for src, dst, r, k in ((PA, fs, "f_ready", "f_kept"), (PB, gs, "g_ready", "g_kept")):
                        act.wait_ge(s[r], n + 1)
                        act.activation(dst[:], flat(src), ACT.Sigmoid).then_inc(s[k], 1)
                    act.wait_ge(s["q_turned"], n + 1)
                    act.activation(qT[:], tiles(PC), ACT.Copy).then_inc(s["qT_kept"], 1)
                    act.wait_ge(s["k_turned"], n + 1)
                    act.activation(kT[:], tiles(PD), ACT.Copy).then_inc(s["kT_kept"], 1)
                    act.wait_ge(s["o1_ready"], n + 1)
                    act.activation(sqa[:], o1[:], ACT.Square).then_inc(s["sqo"], 1)
                    act.wait_ge(s["o_turned"], n + 1)
                    act.activation(oT[:], tiles(PC), ACT.Copy).then_inc(s["oT_kept"], 1)
                    act.wait_ge(s["y_kept"], n + 1)

        @block.tensor
        def _(pe):
            pe.wait_ge(s["w_in"], W_IN)
            pe.wait_ge(s["t_chain"], 4)
            pe.wait_ge(s["tables"], 1)
            with pe.Fori(0, B * NT) as n:
                def project(dst, k, bias, done):
                    for a in range(2):
                        r = slice(a * 512, a * 512 + 512)
                        mm = pe.matmul(dst[:, a, :], xT[:], W5[:, k, r], start=True, stop=(bias is None))
                        if bias is not None:
                            mm = pe.matmul(dst[:, a, :], ones[:], brow[:, bias, r], start=False, stop=True)
                    mm.then_inc(s[done], 1)

                def turn(dst, src, done):
                    for c in range(NCH):
                        mm = pe.transpose(tiles(dst)[:, c, :], src[:, c * P:c * P + P], ident[:])
                    mm.then_inc(s[done], 1)

                pe.wait_ge(s["x_kept"], n + 1)
                project(PA, 0, None, "q_ready")
                project(PB, 1, None, "k_ready")
                project(PC, 2, None, "v_ready")
                pe.matmul(PD[:, 0, 0:HEADS], xT[:], wb[:], start=True, stop=True).then_inc(s["b_ready"], 1)
                pe.wait_ge(s["q_kept"], n + 1)
                project(PA, 3, 0, "f_ready")
                pe.wait_ge(s["k_kept"], n + 1)
                project(PB, 4, 1, "g_ready")
                pe.wait_ge(s["v_kept"], n + 1)
                turn(PC, qs, "q_turned")
                pe.wait_ge(s["b_kept"], n + 1)
                turn(PD, ks, "k_turned")
                pe.wait_ge(s["qT_kept"], n + 1)
                pe.wait_ge(s["kT_kept"], n + 1)
                pe.wait_ge(s["qd_ready"], n + 1)
                for a, bank in ((0, PC), (1, PD)):
                    r = slice(a * D1, a * D1 + D1)
                    for j in range(2):
                        for c in range(4 * j, 4 * j + 4):
                            mm = pe.matmul(tiles(bank)[:, c, :], kT[r, c, :], qT[r, c, :], start=True, stop=True)
                        mm.then_inc(s["s_ready"], 1)
                pe.wait_ge(s["f_kept"], n + 1)
                pe.wait_ge(s["vp_ready"], n + 1)
                for a in range(2):
                    r = slice(a * D1, a * D1 + D1)
                    for j in range(2):
                        pe.wait_ge(s["w_ready"], 4 * n + 2 * a + j + 1)
                        for c in range(4 * j, 4 * j + 4):
                            h = 2 * c + a
                            pe.matmul(PA[:, a, c * D1:c * D1 + D1], Wd[:, a, c, :], vp[:, h * D1:h * D1 + D1],
                                      start=True, stop=False)
                            mm = pe.matmul(PA[:, a, c * D1:c * D1 + D1], qdT[r, c, :], St[r, c, :],
                                           start=False, stop=True)
                mm.then_inc(s["o_ready"], 1)
                pe.wait_ge(s["g_kept"], n + 1)
                pe.wait_ge(s["kp_ready"], n + 1)
                for c in range(NCH):
                    r = slice(c * P, c * P + P)
                    mm = pe.matmul(tiles(PB)[:, c, :], kp[:, r], vp[:, r], start=True, stop=True)
                mm.then_inc(s["st_ready"], 1)
                pe.wait_ge(s["o2_ready"], n + 1)
                turn(PC, o1, "o_turned")
                pe.wait_ge(s["oT_kept"], n + 1)
                for c in range(NCH):
                    mm = pe.matmul(PD[:, 0, 0:C], oT[:, c, :], wo[:, c, :], start=(c == 0), stop=(c == NCH - 1))
                mm.then_inc(s["y_ready"], 1)
                pe.wait_ge(s["st_kept"], n + 1)

        @block.vector
        def _(dve):
            dve.wait_ge(s["w_in"], W_IN)
            dve.wait_ge(s["t_exp"], 2)
            dve.tensor_scalar(neA[:], neA[:], 1e30, -1.0, ALU.min, ALU.mult).then_inc(s["t_chain"], 1)
            dve.tensor_scalar(neAF[:], neAF[:], 1e30, -1.0, ALU.min, ALU.mult).then_inc(s["t_chain"], 1)
            dve.tensor_scalar(brow[:, 0, :], brow[:, 0, :], -1.0, None, ALU.mult).then_inc(s["t_chain"], 1)
            dve.wait_ge(s["t_exp"], 2 + HEADS)
            dec = Dec[:].rearrange("p a c t -> p (a c) t")
            dve.tensor_tensor(dec, dec, before[:].unsqueeze(1).broadcast_to([P, HEADS, P]), ALU.mult)\
               .then_inc(s["t_chain"], 1)
            dve.wait_ge(s["t_chain"], 4)
            dve.wait_ge(s["tables"], 1)
            with dve.Fori(0, B) as b:
                dve.memset(St[:], 0.0).then_inc(s["st_zeroed"], 1)
                dve.wait_ge(s["st_zeroed"], b + 1)
                dve.sem_inc(s["passed"], 1)
                with dve.Fori(0, NT) as i:
                    n = b * NT + i
                    ch = Chain(dve, s["v_chain"])
                    dve.wait_ge(s["sqq"], n + 1)
                    ch.mark(dve.tensor_reduce(ss[:, 0:HEADS], heads(sqa[:]), AX_X, ALU.add))
                    dve.wait_ge(s["sqk"], n + 1)
                    ch.do(dve.tensor_reduce(ss[:, HEADS:2 * HEADS], heads(sqb[:]), AX_X, ALU.add))
                    ch.do(dve.tensor_scalar(ss[:], ss[:], L2_TINY, None, ALU.max))
                    rsqrt(dve, ch, rr[:], ss[:], tn[:])
                    dve.wait_ge(s["b_kept"], n + 1)
                    dve.tensor_tensor(bv[:], bt[:], rr[:, HEADS:2 * HEADS], ALU.mult).then_inc(s["r_ready"], 1)
                    dve.wait_ge(s["r_ready"], n + 1)
                    dve.wait_ge(s["v_kept"], n + 1)
                    dve.tensor_tensor(heads(vp[:]), heads(vs[:]), wide(bv[:]), ALU.mult).then_inc(s["vp_ready"], 1)
                    dve.wait_ge(s["q_turned"], n + 1)
                    dve.wait_ge(s["qT_kept"], n + 1)
                    dve.tensor_tensor(qdT[:], tiles(PC), decT[:], ALU.mult).then_inc(s["qd_ready"], 1)
                    for q in range(4):
                        a, j = q // 2, q % 2
                        dve.wait_ge(s["s_ready"], 4 * n + q + 1)
                        dve.tensor_tensor(Wd[:, a, 4 * j:4 * j + 4, :], tiles((PC, PD)[a])[:, 4 * j:4 * j + 4, :],
                                          Dec[:, a, 4 * j:4 * j + 4, :], ALU.mult).then_inc(s["w_ready"], 1)
                    dve.wait_ge(s["o_ready"], n + 1)
                    dve.wait_ge(s["gq_ready"], n + 1)
                    dve.tensor_tensor(feat4(o1[:]), o_feat, feat4(fs[:]), ALU.mult).then_inc(s["o1_ready"], 1)
                    ch.do(dve.tensor_tensor(StA[:], St[:], A128[:].unsqueeze(2).broadcast_to([P, NCH, D1]), ALU.mult))
                    dve.wait_ge(s["st_ready"], n + 1)
                    ch.mark(dve.tensor_tensor(St[0:D1], StA[0:D1], tiles(PB)[0:D1, :, 0:D1], ALU.add))
                    dve.tensor_tensor(St[D1:P], StA[D1:P], tiles(PB)[D1:P, :, D1:P], ALU.add).then_inc(s["st_kept"], 1)
                    dve.wait_ge(s["sqo"], n + 1)
                    ch.do(dve.tensor_reduce(ss[:, 0:HEADS], heads(sqa[:]), AX_X, ALU.add))
                    ch.do(dve.tensor_scalar(ss[:, 0:HEADS], ss[:, 0:HEADS], 1.0 / D1, RMS_EPS, ALU.mult, ALU.add))
                    rsqrt(dve, ch, bv[:], ss[:, 0:HEADS], tn[:, 0:HEADS])
                    ch.do(dve.tensor_tensor(heads(o1[:]), heads(o1[:]), wide(bv[:]), ALU.mult))
                    dve.wait_ge(s["gw_ready"], n + 1)
                    dve.tensor_tensor(o1[:], o1[:], gs[:], ALU.mult).then_inc(s["o2_ready"], 1)
                    dve.wait_ge(s["y_ready"], n + 1)
                    dve.tensor_tensor(one(X, n), PD[:, 0, 0:C], one(X, n), ALU.add).then_inc(s["y_kept"], 1)
                    dve.wait_ge(s["st_kept"], n + 1)
                    ch.close()


def l1_ffn_phase(nc, io, keep):
    ident, identb, XA, XB = keep["ident"], keep["identb"], keep["XA"], keep["XB"]
    with ExitStack() as ctx:
        sem = lambda n: ctx.enter_context(nc.semaphore(n))
        sb = lambda n, s, d=F32: ctx.enter_context(nc.sbuf_tensor(n, s, d))
        ps = lambda n, s, d=F32: ctx.enter_context(nc.psum_tensor(n, s, d))

        Wqkv = sb("Wqkv", [P, 3 * INNER])
        Wo = sb("Wo", [P, NCH, C])
        qsc, ksc = sb("qsc", [P, D1]), sb("ksc", [P, D1])
        rot = {k: sb(k, [P, NT, D1]) for k in ("cos_q", "sin_q", "cos_k", "sin_k")}
        tab = {k: sb("t_" + k, [P, NT, D1]) for k in rot}
        mask = sb("mask", [P, NT, 2 * KEYS], BF16)
        stays = sb("stays", [P, NT])
        W1 = sb("W1", [P, 2 * FFN])
        W2 = sb("W2", [P, 3, C])
        lng, lnb, b2 = sb("lng", [P, 1]), sb("lnb", [P, 1]), sb("b2", [P, 1])
        b1 = sb("b1", [P, 6])
        warm = sb("warm", [P, 1])
        xs = sb("xs", [P, P])
        q0, k0 = sb("q0", [P, INNER]), sb("k0", [P, INNER])
        t2q, t2k = sb("t2q", [P, INNER]), sb("t2k", [P, INNER])
        sqa, sqb = sb("sqa", [P, INNER]), sb("sqb", [P, INNER])
        qr, kr = sb("qr", [P, INNER]), sb("kr", [P, INNER])
        ss, rr, tn = sb("ss", [P, 2 * HEADS]), sb("rr", [P, 2 * HEADS]), sb("tn", [P, 2 * HEADS])
        rq8 = sb("rq8", [P, HEADS])
        qT = sb("qT", [P, NCH, P])
        kT = sb("kT", [P, NCH, KEYS])
        V, VL = sb("V", [P, 2, INNER]), sb("VL", [WINDOW, 2, INNER])
        mx, nb, den, rden = (sb(n, [P, HEADS]) for n in ("mx", "nb", "den", "rden"))
        Pr = sb("Pr", [P, 2, 4, KEYS])
        PT, PL = sb("PTs", [P, 2, 4, P]), sb("PLs", [WINDOW, 2, 4, WINDOW])
        on, oT = sb("on", [P, INNER]), sb("oT", [P, NCH, P])
        xf = sb("xf", [P, FTOK])
        st, mv = sb("st", [P, 4, 6]), sb("mv", [P, 4, 2])
        ve, rs, tv = sb("ve", [P, 4]), sb("rs", [P, 4]), sb("tv", [P, 4])
        xn, xnT = sb("xn", [P, 4, P]), sb("xnT", [P, FTOK])
        G, H = sb("G", [P, 3, FTOK]), sb("H", [P, 3, FTOK])

        PS, PO, PR = ps("PS", [P, 2, 512]), ps("PO", [P, 2, 512]), ps("PR", [P, 2, 512])
        PT1, PM = ps("PT1", [P, 512]), ps("PM", [P, 512])
        flat = lambda t: t[:].rearrange("p a k -> p (a k)")
        tiles = lambda t: t[:].rearrange("p a (c t) -> p (a c) t", t=P)
        heads = lambda t: t.rearrange("p (h d) -> p h d", d=D1)
        halves = lambda t: t.rearrange("p (h a j) -> p h a j", a=2, j=D1 // 2)
        wide = lambda t: t.unsqueeze(2).broadcast_to([P, HEADS, D1])
        yA = PM[:, P:2 * P]
        turned_p = PT1[:].rearrange("p (h t) -> p h t", t=P)
        turned_l = PM[0:WINDOW, 0:4 * WINDOW].rearrange("p (h t) -> p h t", t=WINDOW)
        fbank = [PS[:, 0, :], PS[:, 1, :], PO[:, 0, :], PO[:, 1, :], PR[:, 0, :], PR[:, 1, :]]
        fturn, fturn2, fout = PT1[:], PM[:], fbank[3]
        hh = D1 // 2

        names = ["consts", "passed", "tabs_ready", "warmed", "aw_in", "fw_in", "first", "v_chain", "f_chain", "xs_ready", "q_ready", "k_ready",
                 "v_ready", "q0_kept", "k0_kept", "q_squared", "k_squared", "q_cos", "q_sin", "k_cos", "k_sin", "qr_ready", "ks_ready", "kr_ready", "v_kept",
                 "q_turned", "k_turned", "qT_kept", "kT_kept", "tail_kept", "s_ready", "nb_ready", "exp_done", "p_turned", "p_kept",
                 "o_ready", "on_ready", "o_turned", "oT_kept", "y_ready", "xb_kept", "xf_ready", "xf_turned",
                 "xn_ready", "xn_turned", "xnT_kept", "hg_ready", "g_ready", "h_ready", "yf_ready", "xa_kept"]
        s = {n: sem("f_" + n) for n in names}
        AW, FW = 16 * 4, 16 * 13
        TILES, BLOCKS = B * NT, B * T // FTOK
        block = ctx.enter_context(nc.Block())

        @block.sync
        def _(sp):
            for k in rot:
                sp.dma_start(rot[k][:], io[k]).then_inc(s["consts"], 16)
            sp.dma_start(mask[:], io["mask"]).then_inc(s["consts"], 16)
            sp.dma_start(stays[:], io["stays"]).then_inc(s["consts"], 16)

            def at(name, l):
                a = io["L1_ffn_" + name]
                a = a[bass.ds(l, 1)]
                return a.rearrange("a m n -> (a m) n") if len(a.shape) == 3 else a

            def attn_weights(l):
                load = lambda dst, src: sp.dma_start(dst, src).then_inc(s["aw_in"], 16)
                load(Wqkv[:], at("Wqkv", l))
                load(Wo[:], at("Wo", l).rearrange("(c p) n -> p c n", p=P))
                load(qsc[:], at("q_scale", l).broadcast_to([P, D1]))
                load(ksc[:], at("k_scale", l).broadcast_to([P, D1]))

            def ffn_weights(l):
                load = lambda dst, src: sp.dma_start(dst, src).then_inc(s["fw_in"], 16)
                load(W1[:], at("W1", l))
                for k, (f, m) in enumerate(FCH):
                    load(W2[0:m, k, :], at("W2", l)[f:f + m, :])
                with nc.allow_non_contiguous_dma(reason="a column of channels"):
                    col = lambda name, f, m: at(name, l)[:, f:f + m].rearrange("a m -> m a")
                    load(lng[:], col("ln_g", 0, C))
                    load(lnb[:], col("ln_b", 0, C))
                    load(b2[:], col("b2", 0, C))
                    for k, (f, m) in enumerate(FCH):
                        load(b1[0:m, k:k + 1], col("b1", f, m))
                        load(b1[0:m, 3 + k:4 + k], col("b1", FFN + f, m))

            attn_weights(0)
            ffn_weights(0)
            with sp.Fori(0, DEPTH - 1) as l:
                sp.wait_ge(s["xb_kept"], (l + 1) * TILES)
                attn_weights(l + 1)
                sp.wait_ge(s["xa_kept"], (l + 1) * BLOCKS + 1)
                ffn_weights(l + 1)

        @block.gpsimd
        def _(pool):
            pool.memset(kT[:], 0.0).then_inc(s["first"], 1)
            pool.memset(VL[:], 0.0).then_inc(s["first"], 1)
            pool.wait_ge(s["first"], 2)

            def shifted(dst, src, b, i, m, done, n):
                h = C // 2
                for k, (r, first) in enumerate(((slice(0, h), 1), (slice(h, C), 0))):
                    pool.tensor_copy(dst[r, :], src[r, bass.ds(b, 1), bass.ds(first + i * m, m)]
                                     .rearrange("p a t -> p (a t)")).then_inc(s[done], 1)
                    pool.wait_ge(s[done], 2 * n + k + 1)
                    pool.sem_inc(s["passed"], 1)

            with pool.Fori(0, DEPTH) as l:
                pool.wait_ge(s["xa_kept"], l * BLOCKS + 1)
                pool.sem_inc(s["passed"], 1)
                pool.wait_ge(s["tabs_ready"], l + 1)
                pool.sem_inc(s["passed"], 1)
                with pool.Fori(0, TILES) as t:
                    n = l * TILES + t
                    shifted(xs, XA, t // NT, t % NT, P, "xs_ready", n)
                    pool.wait_ge(s["q0_kept"], 2 * n + 2)
                    pool.sem_inc(s["passed"], 1)
                    pool.tensor_tensor(heads(qr[:]), heads(q0[:]), tab["cos_q"][:, bass.ds(t % NT, 1), :]
                                       .broadcast_to([P, HEADS, D1]), ALU.mult).then_inc(s["q_cos"], 1)
                    pool.wait_ge(s["q_cos"], n + 1)
                    pool.sem_inc(s["passed"], 1)
                    pool.wait_ge(s["q_sin"], n + 1)
                    pool.sem_inc(s["passed"], 1)
                    pool.tensor_tensor(qr[:], qr[:], t2q[:], ALU.add).then_inc(s["qr_ready"], 1)
                    pool.wait_ge(s["k0_kept"], 2 * n + 2)
                    pool.sem_inc(s["passed"], 1)
                    pool.tensor_tensor(heads(kr[:]), heads(k0[:]), tab["cos_k"][:, bass.ds(t % NT, 1), :]
                                       .broadcast_to([P, HEADS, D1]), ALU.mult).then_inc(s["k_cos"], 1)
                    pool.wait_ge(s["k_cos"], n + 1)
                    pool.sem_inc(s["passed"], 1)
                    pool.wait_ge(s["k_sin"], n + 1)
                    pool.sem_inc(s["passed"], 1)
                    pool.tensor_tensor(kr[:], kr[:], t2k[:], ALU.add).then_inc(s["ks_ready"], 1)
                    pool.wait_ge(s["v_ready"], 2 * n + 2)
                    pool.sem_inc(s["passed"], 1)
                    pool.wait_ge(s["ks_ready"], n + 1)
                    pool.sem_inc(s["passed"], 1)
                pool.wait_ge(s["xb_kept"], (l + 1) * TILES)
                pool.sem_inc(s["passed"], 1)
                with pool.Fori(0, B) as b:
                    with pool.Fori(0, T // FTOK) as i:
                        m = l * BLOCKS + b * (T // FTOK) + i
                        shifted(xf, XB, b, i, FTOK, "xf_ready", m)
                        pool.wait_ge(s["xf_turned"], m + 1)
                        pool.sem_inc(s["passed"], 1)

        @block.scalar
        def _(act):
            act.wait_ge(s["first"], 2)
            act.wait_ge(s["consts"], 16 * 6)
            with act.Fori(0, DEPTH) as l:
                act.activation(warm[:, 0:1], stays[:, 0:1], ACT.Exp).then_inc(s["warmed"], 1)
                act.wait_ge(s["warmed"], 2 * l + 1)

                def keep(a, dst, ready, done):
                    for k in range(2):
                        act.wait_ge(s[ready], 2 * a + k + 1)
                        act.activation(dst[:, 512 * k:512 * k + 512], PR[:, k, :], ACT.Copy).then_inc(s[done], 1)

                def keep_turned(n, dst, ready, done):
                    for k in range(2):
                        act.wait_ge(s[ready], 2 * n + k + 1)
                        act.activation(dst[:, 4 * k:4 * k + 4], PR[:, k, :].rearrange("p (c t) -> p c t", t=P),
                                       ACT.Copy).then_inc(s[done], 1)

                def square(a, src, kept, dst, done):
                    act.wait_ge(s[kept], 2 * a + 2)
                    act.activation(dst[:], src[:], ACT.Square).then_inc(s[done], 1)

                def exps(n, g):
                    act.wait_ge(s["nb_ready"], 4 * n + g + 1)
                    if g >= 2:
                        act.wait_ge(s["p_turned"], 4 * n + g - 1)
                    for j in range(4):
                        h = 4 * g + j
                        ins = act.activation(Pr[:, g % 2, j, :], PS[:, j % 2, (j // 2) * KEYS:(j // 2 + 1) * KEYS],
                                             ACT.Exp, bias=nb[:, h:h + 1], scale=rq8[:, h:h + 1],
                                             accum_out=den[:, h:h + 1])
                    ins.then_inc(s["exp_done"], 1)

                def tile(n, t, e, ahead, behind):
                    exps(n, 0)
                    if ahead:
                        if behind:
                            act.wait_ge(s["ks_ready"], n + 1)
                        keep(n + 1, q0, "q_ready", "q0_kept")
                        square(n + 1, q0, "q0_kept", sqa, "q_squared")
                    exps(n, 1)
                    if ahead:
                        keep(n + 1, k0, "k_ready", "k0_kept")
                        square(n + 1, k0, "k0_kept", sqb, "k_squared")
                    if behind:
                        keep_turned(n - 1, oT, "o_turned", "oT_kept")
                    exps(n, 2)
                    if ahead:
                        keep(n + 1, V[:, 1 - e, :], "v_ready", "v_kept")
                    if behind:
                        act.wait_ge(s["o_ready"], n)
                    act.activation(VL[:, e, :], V[P - WINDOW:P, e, :], ACT.Copy).then_inc(s["tail_kept"], 1)
                    if ahead:
                        keep_turned(n + 1, qT, "q_turned", "qT_kept")
                    exps(n, 3)
                    act.activation(kT[:, :, 0:WINDOW], kT[:, :, P:KEYS], ACT.Copy, scale=stays[:, bass.ds(t % NT, 1)])\
                       .then_inc(s["tail_kept"], 1)
                    act.wait_ge(s["tail_kept"], 2 * n + 2)
                    if ahead:
                        keep_turned(n + 1, kT[:, :, WINDOW:KEYS], "k_turned", "kT_kept")

                first, last = l * TILES, l * TILES + (TILES - 1)
                keep(first, q0, "q_ready", "q0_kept")
                square(first, q0, "q0_kept", sqa, "q_squared")
                keep(first, k0, "k_ready", "k0_kept")
                square(first, k0, "k0_kept", sqb, "k_squared")
                keep(first, V[:, 0, :], "v_ready", "v_kept")
                keep_turned(first, qT, "q_turned", "qT_kept")
                keep_turned(first, kT[:, :, WINDOW:KEYS], "k_turned", "kT_kept")
                tile(first, 0, 0, True, False)
                with act.Fori(0, TILES // 2 - 1) as t:
                    tile(l * TILES + 2 * t + 1, 2 * t + 1, 1, True, True)
                    tile(l * TILES + 2 * t + 2, 2 * t + 2, 0, True, True)
                tile(last, TILES - 1, 1, False, True)
                keep_turned(last, oT, "o_turned", "oT_kept")
                act.activation(warm[:, 0:1], stays[:, 0:1], ACT.Gelu).then_inc(s["warmed"], 1)
                act.wait_ge(s["warmed"], 2 * l + 2)
                act.wait_ge(s["fw_in"], (l + 1) * FW)

                def keep_xn(m):
                    act.wait_ge(s["xn_turned"], m + 1)
                    act.activation(xnT[:], fturn2, ACT.Identity, bias=lnb[:, 0:1], scale=lng[:, 0:1])\
                       .then_inc(s["xnT_kept"], 1)

                def gates(m, others):
                    for k, (f, w) in enumerate(FCH):
                        act.wait_ge(s["hg_ready"], 6 * m + k + 1)
                        if others:
                            act.wait_ge(s["h_ready"], 3 * m + k - 2)
                        act.activation(G[0:w, k, :], fbank[k][0:w, :], ACT.Gelu, bias=b1[0:w, 3 + k:4 + k])\
                           .then_inc(s["g_ready"], 1)

                keep_xn(l * BLOCKS)
                gates(l * BLOCKS, False)
                with act.Fori(1, BLOCKS) as t:
                    keep_xn(l * BLOCKS + t)
                    gates(l * BLOCKS + t, True)

        @block.tensor
        def _(pe):
            pe.wait_ge(s["consts"], 16 * 6)
            pe.wait_ge(s["first"], 2)

            with pe.Fori(0, DEPTH) as l:
                pe.wait_ge(s["aw_in"], (l + 1) * AW)
                pe.sem_inc(s["passed"], 1)

                def project(a, k, done, free):
                    for h in range(2):
                        if free:
                            pe.wait_ge(s[free[0]], 2 * free[1] + h + 1)
                        f = k * INNER + h * 512
                        pe.matmul(PR[:, h, :], xs[:], Wqkv[:, f:f + 512], start=True, stop=True)\
                            .then_inc(s[done], 1)

                def turn(src, done, free):
                    for h in range(2):
                        pe.wait_ge(s[free[0]], 2 * free[1] + h + 1)
                        for c in range(4 * h, 4 * h + 4):
                            mm = pe.transpose(PR[:, h, (c % 4) * P:(c % 4) * P + P], src[:, c * P:c * P + P], ident[:])
                        mm.then_inc(s[done], 1)

                def scores(n, i, g):
                    for a in range(2):
                        pe.matmul(PS[:, a, 0:2 * KEYS], identb[:],
                                  mask[:, bass.ds(i, 1), :].rearrange("p a k -> p (a k)"), start=True, stop=False)
                    for k in range(2):
                        c = 2 * g + k
                        for a in range(2):
                            r = slice(a * D1, a * D1 + D1)
                            mm = pe.matmul(PS[:, a, k * KEYS:k * KEYS + KEYS], qT[r, c, :], kT[r, c, :],
                                           start=False, stop=(k == 1))
                    mm.then_inc(s["s_ready"], 1)

                def turn_p(n, g):
                    for j in range(4):
                        pe.transpose(turned_p[:, j, :], Pr[:, g % 2, j, WINDOW:KEYS], ident[:])
                    for j in range(4):
                        mm = pe.transpose(turned_l[:, j, :], Pr[0:WINDOW, g % 2, j, 0:WINDOW],
                                          ident[0:WINDOW, 0:WINDOW])
                    mm.then_inc(s["p_turned"], 1)

                def values(n, e, g):
                    pe.wait_ge(s["p_kept"], 4 * n + g + 1)
                    for j in range(4):
                        f = slice((4 * g + j) * D1, (4 * g + j) * D1 + D1)
                        o = PO[:].rearrange("p a k -> p (a k)")
                        pe.matmul(o[:, f], PT[:, g % 2, j, :], V[:, e, f], start=True, stop=True)
                        mm = pe.matmul(o[0:WINDOW, f], PL[:, g % 2, j, :], VL[:, 1 - e, f],
                                       start=False, stop=True, skip_group_check=True)
                    if g == 3:
                        mm.then_inc(s["o_ready"], 1)

                def turn_o(n, free):
                    pe.wait_ge(s["on_ready"], n + 1)
                    turn(on, "o_turned", free)

                def output(n):
                    pe.wait_ge(s["oT_kept"], 2 * n + 2)
                    for c in range(NCH):
                        mm = pe.matmul(yA, Wo[:, c, :], oT[:, c, :], start=(c == 0), stop=(c == NCH - 1))
                    mm.then_inc(s["y_ready"], 1)

                def tile(n, i, e, ahead, behind):
                    pe.wait_ge(s["qT_kept"], 2 * n + 2)
                    pe.wait_ge(s["kT_kept"], 2 * n + 2)
                    scores(n, i, 0)
                    if behind:
                        values(n - 1, 1 - e, 3)
                    if ahead:
                        pe.wait_ge(s["xs_ready"], 2 * (n + 1) + 2)
                        project(n + 1, 0, "q_ready", ("kT_kept", n))
                    pe.wait_ge(s["exp_done"], 4 * n + 1)
                    scores(n, i, 1)
                    turn_p(n, 0)
                    if ahead:
                        project(n + 1, 1, "k_ready", ("q0_kept", n + 1))
                    pe.wait_ge(s["v_kept"], 2 * n + 2)
                    if behind:
                        pe.wait_ge(s["on_ready"], n)
                    values(n, e, 0)
                    pe.wait_ge(s["exp_done"], 4 * n + 2)
                    scores(n, i, 2)
                    if behind:
                        turn_o(n - 1, ("k0_kept", n + 1) if ahead else ("kT_kept", n))
                    turn_p(n, 1)
                    if ahead:
                        project(n + 1, 2, "v_ready", ("oT_kept", n - 1) if behind else ("k0_kept", n + 1))
                    pe.wait_ge(s["exp_done"], 4 * n + 3)
                    scores(n, i, 3)
                    if ahead:
                        pe.wait_ge(s["qr_ready"], n + 2)
                        turn(qr, "q_turned", ("v_kept", n + 1))
                    if behind:
                        pe.wait_ge(s["p_kept"], 4 * n + 2)
                        output(n - 1)
                    values(n, e, 1)
                    if behind:
                        pe.wait_ge(s["xb_kept"], n)
                    turn_p(n, 2)
                    if ahead:
                        pe.wait_ge(s["kr_ready"], n + 2)
                        turn(kr, "k_turned", ("qT_kept", n + 1))
                    values(n, e, 2)
                    pe.wait_ge(s["exp_done"], 4 * n + 4)
                    turn_p(n, 3)

                first, last = l * TILES, l * TILES + (TILES - 1)
                pe.wait_ge(s["xs_ready"], 2 * first + 2)
                project(first, 0, "q_ready", None)
                project(first, 1, "k_ready", ("q0_kept", first))
                project(first, 2, "v_ready", ("k0_kept", first))
                pe.wait_ge(s["qr_ready"], first + 1)
                turn(qr, "q_turned", ("v_kept", first))
                pe.wait_ge(s["kr_ready"], first + 1)
                turn(kr, "k_turned", ("qT_kept", first))
                tile(first, 0, 0, True, False)
                with pe.Fori(0, TILES // 2 - 1) as t:
                    tile(l * TILES + 2 * t + 1, (2 * t + 1) % NT, 1, True, True)
                    tile(l * TILES + 2 * t + 2, (2 * t + 2) % NT, 0, True, True)
                tile(last, NT - 1, 1, False, True)
                values(last, 1, 3)
                turn_o(last, ("oT_kept", last - 1))
                output(last)
                pe.wait_ge(s["fw_in"], (l + 1) * FW)
                pe.sem_inc(s["passed"], 1)
                pe.wait_ge(s["xb_kept"], (l + 1) * TILES)
                pe.sem_inc(s["passed"], 1)

                def turn_xf(m):
                    pe.wait_ge(s["xf_ready"], 2 * m + 2)
                    for c in range(4):
                        mm = pe.transpose(fturn[:, c * P:c * P + P], xf[:, c * P:c * P + P], ident[:])
                    mm.then_inc(s["xf_turned"], 1)

                def turn_xn(m):
                    pe.wait_ge(s["xn_ready"], m + 1)
                    for c in range(4):
                        mm = pe.transpose(fturn2[:, c * P:c * P + P], xn[:, c, :], ident[:])
                    mm.then_inc(s["xn_turned"], 1)

                def widen(m):
                    pe.wait_ge(s["xnT_kept"], m + 1)
                    for k in range(6):
                        if k == 3:
                            pe.wait_ge(s["xa_kept"], m + 1)
                        f, w = FCH[k % 3]
                        f += FFN if k < 3 else 0
                        pe.matmul(fbank[k][0:w, :], W1[:, f:f + w], xnT[:], start=True, stop=True)\
                          .then_inc(s["hg_ready"], 1)

                def narrow(m):
                    for k, (f, w) in enumerate(FCH):
                        pe.wait_ge(s["h_ready"], 3 * m + k + 1)
                        mm = pe.matmul(fout, W2[0:w, k, :], H[0:w, k, :], start=(k == 0), stop=(k == 2))
                    mm.then_inc(s["yf_ready"], 1)

                turn_xf(l * BLOCKS)
                turn_xn(l * BLOCKS)
                with pe.Fori(0, BLOCKS - 1) as t:
                    m = l * BLOCKS + t
                    turn_xf(m + 1)
                    widen(m)
                    turn_xn(m + 1)
                    narrow(m)
                widen(l * BLOCKS + BLOCKS - 1)
                narrow(l * BLOCKS + BLOCKS - 1)

        @block.vector
        def _(dve):
            dve.wait_ge(s["consts"], 16 * 6)
            dve.sem_inc(s["xa_kept"], 1)
            with dve.Fori(0, DEPTH) as l:
                dve.wait_ge(s["aw_in"], (l + 1) * AW)
                dve.sem_inc(s["passed"], 1)
                ch = Chain(dve, s["v_chain"])
                for k, sc in (("q", qsc), ("k", ksc)):
                    ch.mark(dve.tensor_tensor(tab["cos_" + k][:], rot["cos_" + k][:],
                                              sc[:].unsqueeze(1).broadcast_to([P, NT, D1]), ALU.mult))
                    for a in range(2):
                        r, o = slice(a * hh, a * hh + hh), slice((1 - a) * hh, (1 - a) * hh + hh)
                        ch.mark(dve.tensor_tensor(tab["sin_" + k][:, :, r], rot["sin_" + k][:, :, r],
                                                  sc[:, o].unsqueeze(1).broadcast_to([P, NT, hh]), ALU.mult))
                ch.close()
                dve.sem_inc(s["tabs_ready"], 1)

                def rotate(i, k, src, dst):
                    for e in range(2):
                        sn = tab["sin_" + k][:, bass.ds(i, 1), e * hh:e * hh + hh].broadcast_to([P, HEADS, hh])
                        ins = dve.tensor_tensor(halves(dst[:])[:, :, e, :], halves(src[:])[:, :, 1 - e, :], sn, ALU.mult)
                    return ins

                def rotate_q(a, i):
                    dve.wait_ge(s["q0_kept"], 2 * a + 2)
                    rotate(i, "q", q0, t2q).then_inc(s["q_sin"], 1)

                def rotate_k(a, i):
                    dve.wait_ge(s["k0_kept"], 2 * a + 2)
                    rotate(i, "k", k0, t2k).then_inc(s["k_sin"], 1)

                def norm_q(a, ch):
                    dve.wait_ge(s["q_squared"], a + 1)
                    ch.mark(dve.tensor_reduce(ss[:, 0:HEADS], heads(sqa[:]), AX_X, ALU.add))

                def norm_k(a, ch):
                    dve.wait_ge(s["k_squared"], a + 1)
                    ch.mark(dve.tensor_reduce(ss[:, HEADS:2 * HEADS], heads(sqb[:]), AX_X, ALU.add))

                def norms(ch):
                    ch.after()
                    ch.do(dve.tensor_scalar(ss[:], ss[:], L2_TINY, None, ALU.max))
                    rsqrt_start(dve, ch, rr[:], ss[:])

                def scale_k(a):
                    dve.wait_ge(s["ks_ready"], a + 1)
                    dve.tensor_tensor(heads(kr[:]), heads(kr[:]), wide(rr[:, HEADS:2 * HEADS]), ALU.mult)\
                        .then_inc(s["kr_ready"], 1)

                def keep_scales(ch):
                    ch.do(dve.tensor_scalar(rq8[:], rr[:, 0:HEADS], QK_SCALE, None, ALU.mult))

                def maxima(n, g, ch):
                    dve.wait_ge(s["s_ready"], 4 * n + g + 1)
                    q = slice(4 * g, 4 * g + 4)
                    ch.do(dve.tensor_reduce(mx[:, q].rearrange("p (c a) -> p a c", a=2),
                                            PS[:, :, 0:2 * KEYS].rearrange("p a (c j) -> p a c j", j=KEYS),
                                            AX_X, ALU.max))
                    dve.scalar_tensor_tensor(out=nb[:, q], in0=mx[:, q], scalar=-1.0, in1=rq8[:, q],
                                             op0=ALU.mult, op1=ALU.mult).then_inc(s["nb_ready"], 1)

                def keep_p(n, g, ch):
                    dve.wait_ge(s["p_turned"], 4 * n + g + 1)
                    ch.mark(dve.tensor_copy(PL[:, g % 2], turned_l))
                    ch.after()
                    dve.tensor_copy(PT[:, g % 2], turned_p).then_inc(s["p_kept"], 1)

                def divide(n):
                    dve.wait_ge(s["o_ready"], n + 1)
                    dve.tensor_tensor(heads(on[:]), PO[:].rearrange("p a (h d) -> p (a h) d", d=D1), wide(rden[:]),
                                      ALU.mult).then_inc(s["on_ready"], 1)

                def output(n, t):
                    dve.wait_ge(s["y_ready"], n + 1)
                    here = lambda x: x[:, bass.ds(t // NT, 1), bass.ds(1 + (t % NT) * P, P)].rearrange("p a t -> p (a t)")
                    dve.tensor_tensor(here(XB), yA, here(XA), ALU.add).then_inc(s["xb_kept"], 1)

                def tile(n, t, ahead, behind):
                    ch = Chain(dve, s["v_chain"])
                    maxima(n, 0, ch)
                    i = (t + 1) % NT
                    if behind:
                        divide(n - 1)
                    maxima(n, 1, ch)
                    keep_p(n, 0, ch)
                    if ahead:
                        rotate_q(n + 1, i)
                    if ahead:
                        norm_q(n + 1, ch)
                        rotate_k(n + 1, i)
                    maxima(n, 2, ch)
                    if ahead:
                        norm_k(n + 1, ch)
                    keep_p(n, 1, ch)
                    if ahead:
                        norms(ch)
                        newton(dve, ch, rr[:], ss[:], tn[:], 2)
                    maxima(n, 3, ch)
                    if ahead:
                        newton(dve, ch, rr[:], ss[:], tn[:], 1)
                        scale_k(n + 1)
                    if behind:
                        output(n - 1, t - 1)
                    keep_p(n, 2, ch)
                    keep_p(n, 3, ch)
                    if ahead:
                        keep_scales(ch)
                    ch.do(dve.reciprocal(rden[:], den[:]))

                first, last = l * TILES, l * TILES + (TILES - 1)
                rotate_q(first, 0)
                rotate_k(first, 0)
                ch = Chain(dve, s["v_chain"])
                norm_q(first, ch)
                norm_k(first, ch)
                norms(ch)
                newton(dve, ch, rr[:], ss[:], tn[:], 3)
                scale_k(first)
                keep_scales(ch)
                tile(first, 0, True, False)
                with dve.Fori(0, TILES // 2 - 1) as t:
                    for k in range(1, 3):
                        tile(l * TILES + 2 * t + k, 2 * t + k, True, True)
                tile(last, TILES - 1, False, True)
                divide(last)
                output(last, TILES - 1)
                dve.wait_ge(s["fw_in"], (l + 1) * FW)
                dve.sem_inc(s["passed"], 1)

                def norm(m, ch, others):
                    dve.wait_ge(s["xf_turned"], m + 1)
                    for c in range(4):
                        ch.mark(dve.bn_stats(st[:, c, :], fturn[:, c * P:c * P + P]))
                    ch.after()
                    for c in range(4):
                        ch.mark(dve.bn_aggr(mv[:, c, :], st[:, c, :]))
                    ch.after()
                    ch.do(dve.tensor_scalar(ve[:].unsqueeze(2), mv[:, :, 1:2], LN_EPS, None, ALU.add))
                    rsqrt(dve, ch, rs[:], ve[:], tv[:])
                    if others:
                        dve.wait_ge(s["xn_turned"], m)
                    for c in range(4):
                        ins = dve.tensor_scalar(xn[:, c, :], fturn[:, c * P:c * P + P], mv[:, c, 0:1],
                                                rs[:, c:c + 1], ALU.subtract, ALU.mult)
                    ins.then_inc(s["xn_ready"], 1)

                def gated(m, others):
                    for k, (f, w) in enumerate(FCH):
                        dve.wait_ge(s["hg_ready"], 6 * m + k + 4)
                        dve.wait_ge(s["g_ready"], 3 * m + k + 1)
                        if others:
                            dve.wait_ge(s["yf_ready"], m)
                        dve.scalar_tensor_tensor(out=H[0:w, k, :], in0=fbank[3 + k][0:w, :], scalar=b1[0:w, k:k + 1],
                                                 in1=G[0:w, k, :], op0=ALU.add, op1=ALU.mult)\
                           .then_inc(s["h_ready"], 1)

                def add(m, t):
                    dve.wait_ge(s["yf_ready"], m + 1)
                    each = T // FTOK
                    here = lambda x: x[:, bass.ds(t // each, 1), bass.ds(1 + (t % each) * FTOK, FTOK)]\
                        .rearrange("p a t -> p (a t)")
                    dve.scalar_tensor_tensor(out=here(XA), in0=fout, scalar=b2[:, 0:1], in1=here(XB),
                                             op0=ALU.add, op1=ALU.add).then_inc(s["xa_kept"], 1)

                first, last = l * BLOCKS, l * BLOCKS + (BLOCKS - 1)
                ch = Chain(dve, s["f_chain"])
                norm(first, ch, False)
                norm(first + 1, ch, True)
                gated(first, False)
                add(first, 0)
                ch.close()
                with dve.Fori(1, BLOCKS - 1) as t:
                    ch = Chain(dve, s["f_chain"])
                    norm(l * BLOCKS + t + 1, ch, True)
                    gated(l * BLOCKS + t, True)
                    add(l * BLOCKS + t, t)
                    ch.close()
                gated(last, True)
                add(last, BLOCKS - 1)


def store_phase(nc, io, keep):
    ident, X, XA = keep["ident"], keep["X"], keep["XA"]
    with ExitStack() as ctx:
        sem = lambda n: ctx.enter_context(nc.semaphore(n))
        tile = ctx.enter_context(nc.sbuf_tensor("tile", [P, 2, 4, P], F32))
        turned = ctx.enter_context(nc.psum_tensor("turned", [P, 2, 512], F32))
        copied, ready, added, stored = (sem(n) for n in ("z_copied", "z_ready", "z_added", "z_stored"))
        block = ctx.enter_context(nc.Block())
        QUADS = B * NT // 4

        @block.scalar
        def _(act):
            for q in range(QUADS):
                if q >= 2:
                    act.wait_ge(ready, q - 1)
                b, t = q // 2, 1 + (q % 2) * 4 * P
                act.activation(tile[:, q % 2].rearrange("p c t -> p (c t)"), XA[:, b, t:t + 4 * P], ACT.Copy)\
                   .then_inc(copied, 1)

        @block.tensor
        def _(pe):
            for q in range(QUADS):
                pe.wait_ge(copied, q + 1)
                if q >= 2:
                    pe.wait_ge(added, q - 1)
                for c in range(4):
                    mm = pe.transpose(turned[:, q % 2, c * P:c * P + P], tile[:, q % 2, c, :], ident[:])
                mm.then_inc(ready, 1)

        @block.vector
        def _(dve):
            for q in range(QUADS):
                dve.wait_ge(ready, q + 1)
                here = X[:, 4 * q:4 * q + 4, :].rearrange("p n c -> p (n c)")
                dve.tensor_tensor(here, turned[:, q % 2, :], here, ALU.add).then_inc(added, 1)

        @block.sync
        def _(sp):
            for q in range(QUADS):
                sp.wait_ge(added, q + 1)
                t = (q % 2) * 4 * P
                sp.dma_start(io["out"][q // 2, t:t + 4 * P].rearrange("(n p) c -> p n c", p=P),
                             X[:, 4 * q:4 * q + 4, :]).then_inc(stored, 16)
            sp.wait_ge(stored, 16 * QUADS)


PHASES = [load_phase, l0_phase, l1_attn_phase, l1_ffn_phase, store_phase]


def build(nc, io):
    with ExitStack() as ctx:
        keep = {
            "ident": ctx.enter_context(nc.sbuf_tensor("ident", [P, P], F32)),
            "identb": ctx.enter_context(nc.sbuf_tensor("identb", [P, P], BF16)),
            "X": ctx.enter_context(nc.sbuf_tensor("X", [P, B * NT, C], F32)),
            "XA": ctx.enter_context(nc.sbuf_tensor("XA", [P, B, 1 + T], F32)),
            "XB": ctx.enter_context(nc.sbuf_tensor("XB", [P, B, 1 + T], F32)),
        }
        for phase in PHASES:
            phase(nc, io, keep)


def constants():
    import numpy as np

    f = np.float32
    half = D0 // 2
    theta = f(10000.0) ** (-np.arange(half, dtype=f) / f(half))
    freqs = np.arange(T, dtype=f)[:, None] * theta[None, :]
    tile = lambda a: np.ascontiguousarray(a.reshape(NT, P, -1).transpose(1, 0, 2))
    out = {"cos0": tile(np.cos(freqs).astype(f)), "sin0": tile(np.sin(freqs).astype(f))}
    hf = np.arange(0, D1, 2, dtype=f)
    inv = (f(1.0) / f(10000.0) ** (hf / f(D1))).astype(f)
    fr = np.arange(T, dtype=f)[:, None] * inv[None, :]
    fr = np.concatenate([fr, fr], -1)
    base = ((hf + f(0.4 * D1)) / f(1.4 * D1)).astype(f)
    power = (np.arange(T, dtype=f) - f(T // 2)) / f(WINDOW // 2)
    sc = (base[None, :] ** power[:, None]).astype(f)
    sc = np.concatenate([sc, sc], -1)
    sign = np.where(np.arange(D1) < D1 // 2, f(-1), f(1))[None, :]
    cos, sin = np.cos(fr).astype(f), np.sin(fr).astype(f) * sign
    for name, s in (("q", sc), ("k", (f(1.0) / sc).astype(f))):
        out["cos_" + name] = tile((cos * s).astype(f))
        out["sin_" + name] = tile((sin * s).astype(f))
    t = np.arange(P, dtype=f)
    out["dist"] = np.maximum(t[None, :] - 1 - t[:, None], 0)
    out["before"] = (t[:, None] < t[None, :]).astype(f)
    out["trow"] = np.tile(t[None, :], (P, 1))
    out["trow1"] = np.ones((1, P), f)
    j, i = np.arange(KEYS)[None, :], np.arange(P)[:, None]
    seen = (j >= i) & (j <= i + WINDOW)
    first = seen & (j >= WINDOW)
    m = np.stack([first] + [seen] * (NT - 1), 1)
    m = np.where(m, f(0), f(MASKED))
    out["mask"] = np.concatenate([m, m], 2).astype(mybir.dt.np(BF16))
    out["stays"] = np.tile((np.arange(NT) < NT - 1).astype(f), (P, 1))
    out["rev"] = (P - 1 - t)[:, None]
    return out


def kernel(**inputs):
    import numpy as _np
    import concourse.bacc as _bacc
    from concourse import mybir as _mybir
    from concourse.bass_utils import run_bass_kernel_spmd as _run

    nc = _bacc.Bacc("TRN2", target_bir_lowering=False, num_devices=1)
    g = {k: _np.asarray(v) for k, v in inputs.items()}
    laid = {
        "x": g["L0_attn_x"],
        "wqkv0": _np.concatenate([g["L0_attn_Wq"].T, g["L0_attn_Wk"].T, g["L0_attn_Wv"].T], 1),
        "woT0": g["L0_attn_Wo"].T,
        "w_ffn0": g["L0_ffn_weight"],
    }
    for k, v in g.items():
        if k.startswith(("L0_attn_b", "L0_ffn_bias", "L1_")):
            laid[k] = v
    laid.update(constants())
    arrays, io = {}, {}
    for name, a in laid.items():
        if False:
            continue
        a = _np.ascontiguousarray(a)
        arrays[f"in_{name}_dram"] = a
        io[name] = nc.dram_tensor(f"in_{name}_dram", a.shape, _mybir.dt.from_np(a.dtype), kind="ExternalInput").ap()
    io["out"] = nc.dram_tensor("out_dram", (B, T, C), F32, kind="ExternalOutput").ap()
    build(nc, io)
    r = _run(nc, [arrays], core_ids=[0])
    return r.results[0]["out_dram"]
```

```python
from contextlib import ExitStack

import concourse.bass as bass
from concourse import mybir

F32 = mybir.dt.float32
BF16 = mybir.dt.bfloat16
I32 = mybir.dt.int32
ALU = mybir.AluOpType
ACT = mybir.ActivationFunctionType
AX_X = mybir.AxisListType.X

P = 128
B, T, C = 4, 1024, 128
NT = T // P
HEADS = 16
LN_EPS = 1e-5

D0 = C // HEADS
SLOT = 64
NPART = 6
SHIFT_AT = NPART * D0
SCALE0 = float(D0) ** -0.5
FP6_MAX, FP6_TINY = 7.5, 1e-30
ROUND = 1.5 * 2.0 ** 23

D1 = 64
INNER = HEADS * D1
NCH = INNER // P
RMS_EPS = 1e-5
L2_TINY = 1e-24

DEPTH = 6
WINDOW = 32
KEYS = WINDOW + P
QK_SCALE = 8.0
FFN = int(C * 4 * 2 / 3)
FCH = [(0, 128), (128, 128), (256, FFN - 256)]
FTOK = 512
MASKED = -1e30




class Chain:

    def __init__(self, eng, sem):
        self.eng, self.sem, self.n = eng, sem, 0
        eng.sem_clear(sem)

    def mark(self, ins):
        self.n += 1
        ins.then_inc(self.sem, 1)
        return self.n

    def after(self, n=None):
        self.eng.wait_ge(self.sem, self.n if n is None else n)

    def do(self, ins):
        self.mark(ins)
        self.after()

    def close(self):
        self.after()


def rsqrt_start(dve, ch, y, x):
    ch.do(dve.tensor_scalar(y.bitcast(I32), x.bitcast(I32), 1, None, ALU.logical_shift_right))
    ch.do(dve.tensor_scalar(y.bitcast(I32), y.bitcast(I32), -1.0, 1597463007.0, ALU.mult, ALU.add))


def newton(dve, ch, y, x, tmp, steps):
    for _ in range(steps):
        ch.do(dve.tensor_tensor(tmp, y, y, ALU.mult))
        ch.do(dve.scalar_tensor_tensor(out=tmp, in0=tmp, scalar=-0.5, in1=x, op0=ALU.mult, op1=ALU.mult))
        ch.do(dve.scalar_tensor_tensor(out=y, in0=tmp, scalar=1.5, in1=y, op0=ALU.add, op1=ALU.mult))


def rsqrt(dve, ch, y, x, tmp):
    rsqrt_start(dve, ch, y, x)
    newton(dve, ch, y, x, tmp, 3)


def one(t, n):
    return t[:, bass.ds(n, 1), :].rearrange("p a m -> p (a m)")


def load_phase(nc, io, keep):
    with ExitStack() as ctx:
        sem = lambda n: ctx.enter_context(nc.semaphore(n))
        loaded, ident_zero, ident_set, zeroed = sem("ld_x"), sem("ld_id0"), sem("ld_id"), sem("ld_zero")
        block = ctx.enter_context(nc.Block())
        ident, identb, X, XA, XB = keep["ident"], keep["identb"], keep["X"], keep["XA"], keep["XB"]

        @block.sync
        def _(sp):
            for b in range(B):
                sp.dma_start(X[:, NT * b:NT * b + NT, :],
                             io["x"][b].rearrange("(n p) c -> p n c", p=P)).then_inc(loaded, 16)
            sp.wait_ge(loaded, 16 * B)

        @block.gpsimd
        def _(pool):
            pool.memset(ident[:], 0.0).then_inc(ident_zero, 1)
            pool.memset(identb[:], 0.0).then_inc(ident_zero, 1)
            pool.wait_ge(ident_zero, 2)
            for m in (ident, identb):
                pool.affine_select(out=m[:], in_=m[:], compare_op=ALU.not_equal, fill=1.0, base=0,
                                   pattern=[[-1, P]], channel_multiplier=1).then_inc(ident_set, 1)
            pool.wait_ge(ident_set, 2)

        @block.vector
        def _(dve):
            dve.memset(XA[:, :, 0:1], 0.0).then_inc(zeroed, 1)
            dve.memset(XB[:, :, 0:1], 0.0).then_inc(zeroed, 1)
            dve.wait_ge(zeroed, 2)


def quantize(pool, ch, u, scale, out, a, g):
    ch.do(pool.tensor_tensor(a, u, u, ALU.mult))
    ch.do(pool.tensor_scalar(g, a, 4.0, -4.0, ALU.is_ge, ALU.mult))
    ch.do(pool.tensor_scalar(a, a, 16.0, -2.0, ALU.is_ge, ALU.mult))
    ch.do(pool.tensor_tensor(g, g, a, ALU.add))
    ch.do(pool.tensor_scalar(g, g, 8.0, None, ALU.add))
    ch.do(pool.tensor_tensor(u, u, g, ALU.mult))
    ch.do(pool.tensor_scalar(a, u, ROUND, -ROUND, ALU.add, ALU.add))
    ch.do(pool.tensor_tensor(u, a, u, ALU.subtract))
    ch.do(pool.tensor_scalar(u, u, 0.5, None, ALU.is_ge))
    ch.do(pool.tensor_tensor(a, a, u, ALU.subtract))
    ch.do(pool.tensor_scalar(u, g, -14.0, None, ALU.add))
    ch.do(pool.tensor_tensor(u, u, g, ALU.mult))
    ch.do(pool.tensor_scalar(u, u, 56.0, 1.0 / 64.0, ALU.add, ALU.mult))
    ch.do(pool.tensor_tensor(a, a, u, ALU.mult))
    return pool.tensor_tensor(out, a, scale, ALU.mult)


def block_scales(dve, ch, x, mx, inv, u):
    ch.do(dve.tensor_reduce(mx, x.rearrange("p (k j) -> p k j", j=32), AX_X, ALU.max,
                            apply_absolute_value=True))
    ch.do(dve.tensor_scalar(mx, mx, 1.0 / FP6_MAX, FP6_TINY, ALU.mult, ALU.max))
    ch.do(dve.reciprocal(inv, mx))
    return dve.tensor_tensor(u.rearrange("p (k j) -> p k j", j=32), x.rearrange("p (k j) -> p k j", j=32),
                             wide(inv), ALU.mult)


def blocks(t):
    return t.rearrange("p (k j) -> p k j", j=32)


def wide(mx):
    return mx.unsqueeze(2).broadcast_to([P, C // 32, 32])


def l0_phase(nc, io, keep):
    ident, identb, X, XA = keep["ident"], keep["identb"], keep["X"], keep["XA"]
    with ExitStack() as ctx:
        sem = lambda n: ctx.enter_context(nc.semaphore(n))
        sb = lambda n, s, d=F32: ctx.enter_context(nc.sbuf_tensor(n, s, d))
        ps = lambda n, s, d=F32: ctx.enter_context(nc.psum_tensor(n, s, d))

        wqkv = sb("wqkv0", [P, 3 * C])
        bqkv = sb("bqkv0", [P, 3 * C])
        wo = sb("wo0", [P, C])
        bsum = sb("bsum", [P, C])
        fbias = sb("fbias", [P, C])
        wraw = sb("wraw", [P, C])
        wdq = sb("wdq", [P, C])
        wdT = sb("wdT", [P, C])
        cos = sb("cos0", [P, NT, 4])
        sin = sb("sin0", [P, NT, 4])
        nsin = sb("nsin0", [P, NT, 4])
        st = sb("st0", [P, 6])
        mv = sb("mv0", [P, 2])
        ve, rs, nt_ = sb("ve0", [P, 1]), sb("rs0", [P, 1]), sb("nt0", [P, 1])
        xn = sb("xn0", [P, C])
        u, ua, ug = sb("u0", [P, C]), sb("ua0", [P, C]), sb("ug0", [P, C])
        mx6, inv6 = sb("mx6", [P, C // 32]), sb("inv6", [P, C // 32])
        xnT = sb("xnT0", [P, C])
        qkv = sb("qkv0", [P, 3 * C])
        t1, t2 = sb("ropea", [P, 2 * C]), sb("ropeb", [P, 2 * C])
        hi, mid, lo = sb("hi", [P, 2 * C], BF16), sb("mid", [P, 2 * C], BF16), sb("lo", [P, 2 * C], BF16)
        Ktok = sb("Ktok", [P, HEADS, SLOT], BF16)
        Qtok = sb("Qtok", [P, NT, HEADS, SLOT], BF16)
        Qs = sb("Qs", [P, HEADS, SLOT], BF16)
        kT = sb("kT0", [P, NCH, T], BF16)
        qTm = sb("qTm", [P, NCH, P], BF16)
        qTe = sb("qTe", [P, NCH, P], BF16)
        Vaug = sb("Vaug", [P, NT, HEADS, D0 + 1])
        XD = sb("XD", [P, NT, C])
        mxh = sb("mxh", [P, HEADS, 2])
        mx = sb("mx0", [P, HEADS])
        m1 = sb("m1", [P, HEADS])
        PT = sb("PT0", [P, 4, NT, P])
        oS = sb("oS", [P, 4, P])
        rden = sb("rden0", [P, HEADS])
        att = sb("att0", [P, C])
        attT = sb("attT0", [P, C])
        xds = sb("xds", [P, C])
        xdT = sb("xdT", [P, C])
        x1 = sb("x1", [P, C])
        xn2 = sb("xn2", [P, C])

        pS = ps("pS", [P, 2, 512])
        pE = ps("pE", [P, 2, NT, P])
        pE2 = pE[:, 0].rearrange("p (a c) t -> p a (c t)", a=2)
        pM = ps("pM", [P, 512])
        pTb = pM[:].bitcast(BF16).rearrange("p (c t) -> p c t", t=P)
        pO = ps("pO", [P, 4, P])
        oh = pM[:].rearrange("p (h d) -> p h d", d=32)
        pP = pS[:, 0, 0:3 * C]
        pX = pS[:, 1, 0:P]
        pA, pX2, pY, pN = (pM[:, k * P:k * P + P] for k in range(4))

        names = ["w_in", "passed", "w_over", "w_quant", "w_turned", "w_kept", "p_chain", "v_chain",
                 "xn_ready", "u_ready", "xd_kept", "xn_turned", "xn_kept", "qkv_ready", "parts_ready",
                 "k_slots", "q_slots", "k_turned", "k_kept", "preset", "b_chain", "q_copied", "q_turned",
                 "q_kept", "s_ready", "max_done", "qe_copied", "qe_turned", "qe_kept", "e_ready", "exp_done",
                 "o_cleared", "o_ready", "o_kept", "o_back", "att_ready", "xd_copied", "out_turned",
                 "out_kept", "y_ready", "xn2_ready", "xn2_turned", "xn2_kept"]
        s = {n: sem("l0_" + n) for n in names}
        block = ctx.enter_context(nc.Block())

        def rounds(eng):
            return eng.Fori(0, B)

        PAIRS = HEADS // 2
        SCORED = (0, 2, 4, 6, 8, 11, 14, 16, 16)

        @block.sync
        def _(sp):
            for dst, src in ((wqkv, "wqkv0"), (wo, "woT0"), (wraw, "w_ffn0"), (cos, "cos0"), (sin, "sin0")):
                sp.dma_start(dst[:], io[src]).then_inc(s["w_in"], 16)
            for k, n in enumerate(("L0_attn_bq", "L0_attn_bk", "L0_attn_bv")):
                sp.dma_start(bqkv[:, k * C:k * C + C], io[n].partition_broadcast(P)).then_inc(s["w_in"], 16)
            sp.dma_start(bsum[:], io["L0_attn_bo"].partition_broadcast(P)).then_inc(s["w_in"], 16)
            sp.dma_start(fbias[:], io["L0_ffn_bias"].partition_broadcast(P)).then_inc(s["w_in"], 16)

        W_IN = 16 * 10

        @block.gpsimd
        def _(pool):
            pool.memset(Ktok[:], 0.0).then_inc(s["preset"], 1)
            pool.memset(Qtok[:], 0.0).then_inc(s["preset"], 1)
            pool.memset(Vaug[:], 1.0).then_inc(s["preset"], 1)
            pool.wait_ge(s["preset"], 3)
            pool.memset(Ktok[:, :, SHIFT_AT:SHIFT_AT + 3], 1.0).then_inc(s["preset"], 1)
            pool.wait_ge(s["preset"], 4)
            pool.wait_ge(s["w_over"], 1)
            ch = Chain(pool, s["p_chain"])
            quantize(pool, ch, blocks(u[:]), wide(mx6[:]), blocks(wdq[:]), blocks(ua[:]), blocks(ug[:]))\
                .then_inc(s["w_quant"], 1)
            with rounds(pool) as b:
                with pool.Fori(0, NT) as i:
                    n = b * NT + i
                    ch = Chain(pool, s["p_chain"])
                    pool.wait_ge(s["u_ready"], n + 1)
                    pool.sem_inc(s["passed"], 1)
                    quantize(pool, ch, blocks(u[:]), wide(mx6[:]),
                             XD[:, bass.ds(i, 1), :].rearrange("p a (k j) -> p (a k) j", j=32),
                             blocks(ua[:]), blocks(ug[:])).then_inc(s["xd_kept"], 1)
                    ch.close()
                pool.wait_ge(s["xd_kept"], (b + 1) * NT)
                pool.sem_inc(s["passed"], 1)
                with pool.Fori(0, NT) as i:
                    n = b * NT + i
                    pool.tensor_copy(xds[:], one(XD, i)).then_inc(s["xd_copied"], 1)
                    pool.wait_ge(s["out_turned"], n + 1)
                    pool.sem_inc(s["passed"], 1)

        @block.scalar
        def _(act):
            act.wait_ge(s["w_turned"], 1)
            act.activation(wdT[:], pX, ACT.Copy).then_inc(s["w_kept"], 1)
            with rounds(act) as b:
                def keep_xn(n):
                    act.wait_ge(s["xn_turned"], n + 1)
                    act.activation(xnT[:], pX, ACT.Copy).then_inc(s["xn_kept"], 1)

                def slots(n, i):
                    act.wait_ge(s["parts_ready"], n + 1)
                    hh = lambda t, a: t[:, a * C:a * C + C].rearrange("p (h d) -> p h d", h=HEADS)
                    qd = Qtok[:, bass.ds(i, 1), :, :].rearrange("p a h d -> p (a h) d")

                    def put(t, k, src, a, m):
                        dst = t[:, :, a * D0:(a + m) * D0]
                        sr = hh(src, k)
                        if m > 1:
                            dst = dst.rearrange("p h (m d) -> p h m d", m=m)
                            sr = sr.unsqueeze(2).broadcast_to([P, HEADS, m, D0])
                        return act.activation(dst, sr, ACT.Copy)
                    put(Ktok, 1, hi, 0, 1)
                    put(Ktok, 1, hi, 3, 2)
                    put(Ktok, 1, mid, 1, 1)
                    put(Ktok, 1, mid, 5, 1)
                    put(Ktok, 1, lo, 2, 1).then_inc(s["k_slots"], 1)
                    put(qd, 0, hi, 0, 3)
                    put(qd, 0, mid, 3, 1)
                    put(qd, 0, mid, 5, 1)
                    put(qd, 0, lo, 4, 1).then_inc(s["q_slots"], 1)

                def keep_k(n, i):
                    act.wait_ge(s["k_turned"], n + 1)
                    act.activation(kT[:, :, bass.ds(i * P, P)], pTb, ACT.Copy).then_inc(s["k_kept"], 1)

                keep_xn(b * NT)
                with act.Fori(0, NT - 1) as i:
                    n = b * NT + i
                    slots(n, i)
                    keep_xn(n + 1)
                    keep_k(n, i)
                slots(b * NT + NT - 1, NT - 1)
                keep_k(b * NT + NT - 1, NT - 1)

                def keep_q(n):
                    act.wait_ge(s["q_turned"], n + 1)
                    act.activation(qTm[:], pTb, ACT.Copy).then_inc(s["q_kept"], 1)

                def keep_qe(n):
                    act.wait_ge(s["qe_turned"], n + 1)
                    act.activation(qTe[:], pTb, ACT.Copy).then_inc(s["qe_kept"], 1)

                def keep_o(n):
                    act.wait_ge(s["o_ready"], (n + 1) * PAIRS)
                    act.activation(oS[:].rearrange("p g t -> p (g t)"), pO[:].rearrange("p g t -> p (g t)"),
                                   ACT.Copy).then_inc(s["o_kept"], 1)

                def keep_out(n):
                    act.wait_ge(s["out_turned"], n + 1)
                    act.activation(attT[:], pA, ACT.Copy).then_inc(s["out_kept"], 1)
                    act.activation(xdT[:], pX2, ACT.Copy).then_inc(s["out_kept"], 1)

                def keep_xn2(n, i):
                    act.wait_ge(s["xn2_turned"], n + 1)
                    act.activation(XA[:, bass.ds(b, 1), bass.ds(1 + i * P, P)].rearrange("p a t -> p (a t)"),
                                   pN, ACT.Copy).then_inc(s["xn2_kept"], 1)

                def tile(n, i, ahead, behind):
                    if behind:
                        keep_o(n - 1)
                    for h in range(HEADS):
                        act.wait_ge(s["e_ready"], n * HEADS + h + 1)
                        if h >= 4:
                            act.wait_ge(s["o_ready"], n * PAIRS + h // 2 - 1)
                        act.activation(PT[:, h % 4], pE[:, h % 2], ACT.Exp, scale=SCALE0)\
                           .then_inc(s["exp_done"], 1)
                        if ahead and h == 0:
                            keep_q(n + 1)
                        if behind and h == 6:
                            keep_out(n - 1)
                        if behind and h == 14:
                            keep_xn2(n - 1, i - 1)
                    if ahead:
                        keep_qe(n + 1)

                first, last = b * NT, b * NT + NT - 1
                keep_q(first)
                keep_qe(first)
                tile(first, 0, True, False)
                with act.Fori(1, NT - 1) as i:
                    tile(b * NT + i, i, True, True)
                tile(last, NT - 1, False, True)
                keep_o(last)
                keep_out(last)
                keep_xn2(last, NT - 1)

        @block.tensor
        def _(pe):
            pe.wait_ge(s["w_quant"], 1)
            pe.transpose(pX, wdq[:], ident[:]).then_inc(s["w_turned"], 1)
            pe.wait_ge(s["w_in"], W_IN)
            pe.wait_ge(s["w_kept"], 1)
            pe.wait_ge(s["o_cleared"], 1)
            with rounds(pe) as b:
                def project_qkv(n):
                    pe.wait_ge(s["xn_ready"], n + 1)
                    pe.transpose(pX, xn[:], ident[:]).then_inc(s["xn_turned"], 1)
                    pe.wait_ge(s["xn_kept"], n + 1)
                    pe.matmul(pP, xnT[:], wqkv[:], start=True, stop=True).then_inc(s["qkv_ready"], 1)

                def turn_k(n):
                    pe.wait_ge(s["k_slots"], n + 1)
                    for c in range(NCH):
                        mm = pe.transpose(pTb[:, c, :], Ktok[:, 2 * c:2 * c + 2, :].rearrange("p h d -> p (h d)"),
                                          identb[:])
                    mm.then_inc(s["k_turned"], 1)

                project_qkv(b * NT)
                with pe.Fori(0, NT - 1) as i:
                    turn_k(b * NT + i)
                    pe.wait_ge(s["parts_ready"], b * NT + i + 1)
                    project_qkv(b * NT + i + 1)
                    pe.wait_ge(s["k_kept"], b * NT + i + 1)
                turn_k(b * NT + NT - 1)
                pe.wait_ge(s["k_kept"], (b + 1) * NT)

                def turn_q(n, done, turned):
                    pe.wait_ge(s[done], n + 1)
                    for c in range(NCH):
                        mm = pe.transpose(pTb[:, c, :], Qs[:, 2 * c:2 * c + 2, :].rearrange("p h d -> p (h d)"),
                                          identb[:])
                    mm.then_inc(s[turned], 1)

                def head_rows(h):
                    return slice(SLOT * (h % 2), SLOT * (h % 2) + SLOT)

                def scores(n, h, bank=pS[:], banks=1):
                    r = head_rows(h)
                    if h == 0:
                        pe.wait_ge(s["q_kept"], n + 1)
                    for a in range(2):
                        if h >= banks:
                            pe.wait_ge(s["max_done"], 2 * (n * HEADS + h - banks) + a + 1)
                        pe.matmul(bank[:, a, :], qTm[r, h // 2, :], kT[r, h // 2, a * 512:a * 512 + 512],
                                  start=True, stop=True).then_inc(s["s_ready"], 1)

                def exponents(n, h):
                    r = head_rows(h)
                    if h == 0:
                        pe.wait_ge(s["qe_kept"], n + 1)
                    if h >= 2:
                        pe.wait_ge(s["exp_done"], n * HEADS + h - 1)
                    for j in range(NT):
                        mm = pe.matmul(pE[:, h % 2, j, :], kT[r, h // 2, j * P:j * P + P], qTe[r, h // 2, :],
                                       start=True, stop=True)
                    mm.then_inc(s["e_ready"], 1)

                def values(n, p, js):
                    if js[0] == 0:
                        pe.wait_ge(s["exp_done"], n * HEADS + 2 * p + 2)
                    for j in js:
                        for h in (2 * p, 2 * p + 1):
                            r = 32 * (h % 4)
                            mm = pe.matmul(pO[r:r + D0 + 1, h // 4, :], Vaug[:, j, h, :], PT[:, h % 4, j, :],
                                           start=(j == 0), stop=(j == NT - 1), skip_group_check=True)
                    if js[-1] == NT - 1:
                        mm.then_inc(s["o_ready"], 1)

                def turn_o(n):
                    pe.wait_ge(s["o_kept"], n + 1)
                    for g in range(4):
                        mm = pe.transpose(pM[:, g * P:g * P + P], oS[:, g, :], ident[:])
                    mm.then_inc(s["o_back"], 1)

                def turn_out(n):
                    pe.wait_ge(s["att_ready"], n + 1)
                    pe.transpose(pA, att[:], ident[:])
                    pe.wait_ge(s["xd_copied"], n + 1)
                    pe.transpose(pX2, xds[:], ident[:]).then_inc(s["out_turned"], 1)

                def project(n):
                    pe.wait_ge(s["out_kept"], 2 * n + 2)
                    pe.matmul(pY, attT[:], wo[:], start=True, stop=False)
                    pe.matmul(pY, xdT[:], wdT[:], start=False, stop=True).then_inc(s["y_ready"], 1)

                def turn_xn2(n):
                    pe.wait_ge(s["xn2_ready"], n + 1)
                    pe.transpose(pN, xn2[:], ident[:]).then_inc(s["xn2_turned"], 1)

                def tile(n, ahead, behind):
                    exponents(n, 0)
                    if ahead:
                        turn_q(n + 1, "q_copied", "q_turned")
                    exponents(n, 1)
                    if behind:
                        pe.wait_ge(s["o_kept"], n)
                    for p in range(PAIRS):
                        for h in (2 * p + 2, 2 * p + 3):
                            if h < HEADS:
                                exponents(n, h)
                        if behind and p == 1:
                            if ahead:
                                pe.wait_ge(s["q_kept"], n + 2)
                            turn_o(n - 1)
                        if behind and p == 2:
                            turn_out(n - 1)
                        if behind and p == 3:
                            project(n - 1)
                        if behind and p == 6:
                            turn_xn2(n - 1)
                        if ahead and p == 7:
                            if behind:
                                pe.wait_ge(s["xn2_kept"], n)
                            turn_q(n + 1, "qe_copied", "qe_turned")
                        g, m = SCORED[p], SCORED[p + 1] - SCORED[p]
                        for k, js in enumerate(((0, 1, 2), (3, 4, 5), (6, 7))):
                            if ahead and k in ((), (2,), (0, 2), (0, 1, 2))[m]:
                                scores(n + 1, g)
                                g += 1
                            values(n, p, js)

                first, last = b * NT, b * NT + NT - 1
                turn_q(first, "q_copied", "q_turned")
                for h in range(HEADS):
                    scores(first, h, (pS[:], pE2)[h % 2], 2)
                turn_q(first, "qe_copied", "qe_turned")
                tile(first, True, False)
                with pe.Fori(1, NT - 1) as i:
                    tile(b * NT + i, True, True)
                tile(last, False, True)
                turn_o(last)
                turn_out(last)
                project(last)
                turn_xn2(last)
                pe.wait_ge(s["xn2_kept"], (b + 1) * NT)
                pe.sem_inc(s["passed"], 1)

        def statistics(dve, ch, x):
            ch.do(dve.bn_stats(st[:], x))
            ch.do(dve.bn_aggr(mv[:], st[:]))
            ch.do(dve.tensor_scalar(ve[:], mv[:, 1:2], LN_EPS, None, ALU.add))
            rsqrt_start(dve, ch, rs[:], ve[:])

        def normalized(dve, x, out):
            return dve.tensor_scalar(out, x, mv[:, 0:1], rs[:, 0:1], ALU.subtract, ALU.mult)

        @block.vector
        def _(dve):
            dve.wait_ge(s["w_in"], W_IN)
            ch = Chain(dve, s["v_chain"])
            ch.mark(dve.tensor_tensor(bsum[:], bsum[:], fbias[:], ALU.add))
            block_scales(dve, ch, wraw[:], mx6[:], inv6[:], u[:]).then_inc(s["w_over"], 1)
            ch.do(dve.tensor_scalar(nsin[:], sin[:], -1.0, None, ALU.mult))
            ch.close()
            dve.wait_ge(s["w_quant"], 1)
            dve.memset(pO[:].rearrange("p g t -> p (g t)"), 0.0).then_inc(s["o_cleared"], 1)
            dve.wait_ge(s["o_cleared"], 1)
            with rounds(dve) as b:
                def norm(n, ch, others):
                    statistics(dve, ch, one(X, n))
                    newton(dve, ch, rs[:], ve[:], nt_[:], 3)
                    normalized(dve, one(X, n), xn[:]).then_inc(s["xn_ready"], 1)
                    dve.wait_ge(s["xn_ready"], n + 1)
                    if others:
                        dve.wait_ge(s["xd_kept"], n)
                    block_scales(dve, ch, xn[:], mx6[:], inv6[:], u[:]).then_inc(s["u_ready"], 1)

                def parts(n, i, ch, others):
                    dve.wait_ge(s["qkv_ready"], n + 1)
                    ch.do(dve.tensor_tensor(qkv[:], pP, bqkv[:], ALU.add))
                    v4 = lambda t: t[:, 0:2 * C].rearrange("p (h a j) -> p h a j", a=2, j=D0 // 2)
                    cb = cos[:, bass.ds(i, 1), :].unsqueeze(2).broadcast_to([P, 2 * HEADS, 2, D0 // 2])
                    sn = nsin[:, bass.ds(i, 1), :].broadcast_to([P, 2 * HEADS, D0 // 2])
                    sp_ = sin[:, bass.ds(i, 1), :].broadcast_to([P, 2 * HEADS, D0 // 2])
                    ch.mark(dve.tensor_tensor(v4(t1), v4(qkv), cb, ALU.mult))
                    ch.mark(dve.tensor_tensor(v4(t2)[:, :, 0, :], v4(qkv)[:, :, 1, :], sn, ALU.mult))
                    ch.do(dve.tensor_tensor(v4(t2)[:, :, 1, :], v4(qkv)[:, :, 0, :], sp_, ALU.mult))
                    ch.do(dve.tensor_tensor(t1[:], t1[:], t2[:], ALU.add))
                    if others:
                        dve.wait_ge(s["q_slots"], n)
                    ch.do(dve.tensor_copy(hi[:], t1[:]))
                    ch.do(dve.tensor_tensor(t1[:], t1[:], hi[:], ALU.subtract))
                    ch.do(dve.tensor_copy(mid[:], t1[:]))
                    ch.do(dve.tensor_tensor(t1[:], t1[:], mid[:], ALU.subtract))
                    dve.tensor_copy(lo[:], t1[:]).then_inc(s["parts_ready"], 1)
                    ch.mark(dve.tensor_copy(Vaug[:, bass.ds(i, 1), :, 0:D0].rearrange("p a h d -> p (a h) d"),
                                            qkv[:, 2 * C:3 * C].rearrange("p (h d) -> p h d", h=HEADS)))

                ch = Chain(dve, s["v_chain"])
                norm(b * NT, ch, False)
                parts(b * NT, 0, ch, False)
                norm(b * NT + 1, ch, True)
                ch.close()
                with dve.Fori(1, NT - 1) as i:
                    ch = Chain(dve, s["v_chain"])
                    parts(b * NT + i, i, ch, True)
                    norm(b * NT + i + 1, ch, True)
                    dve.wait_ge(s["parts_ready"], b * NT + i + 1)
                    dve.wait_ge(s["u_ready"], b * NT + i + 2)
                    dve.sem_inc(s["passed"], 1)
                    ch.close()
                ch = Chain(dve, s["v_chain"])
                parts(b * NT + NT - 1, NT - 1, ch, True)
                dve.wait_ge(s["xd_kept"], (b + 1) * NT)
                dve.wait_ge(s["q_slots"], (b + 1) * NT)
                dve.sem_inc(s["passed"], 1)
                ch.close()

                def copy_q(n, i):
                    qi = Qtok[:, bass.ds(i, 1), :, :].rearrange("p a h d -> p (a h d)")
                    dve.tensor_copy(Qs[:].rearrange("p h d -> p (h d)"), qi).then_inc(s["q_copied"], 1)

                def maximum(n, h, bank):
                    for a in range(2):
                        dve.wait_ge(s["s_ready"], 2 * (n * HEADS + h) + a + 1)
                        dve.tensor_reduce(mxh[:, h, a:a + 1], bank[:, a, :], AX_X, ALU.max).then_inc(s["max_done"], 1)

                def add_maxima(n, ch):
                    at = lambda k: Qs[:, :, SHIFT_AT + k:SHIFT_AT + k + 1].rearrange("p h d -> p (h d)")
                    dve.wait_ge(s["max_done"], 2 * (n + 1) * HEADS)
                    dve.wait_ge(s["q_turned"], n + 1)
                    ch.do(dve.tensor_reduce(mx[:], mxh[:], AX_X, ALU.max))
                    ch.do(dve.tensor_scalar(m1[:], mx[:], -1.0, None, ALU.mult))
                    ch.do(dve.tensor_copy(at(0), m1[:]))
                    ch.do(dve.tensor_tensor(m1[:], m1[:], at(0), ALU.subtract))
                    ch.do(dve.tensor_copy(at(1), m1[:]))
                    ch.do(dve.tensor_tensor(m1[:], m1[:], at(1), ALU.subtract))
                    dve.tensor_copy(at(2), m1[:]).then_inc(s["qe_copied"], 1)

                def divide(n, ch):
                    dve.wait_ge(s["o_back"], n + 1)
                    ch.do(dve.reciprocal(rden[:], oh[:, :, D0:D0 + 1].rearrange("p h d -> p (h d)")))
                    dve.tensor_tensor(att[:].rearrange("p (h d) -> p h d", h=HEADS), oh[:, :, 0:D0],
                                      rden[:].unsqueeze(2).broadcast_to([P, HEADS, D0]), ALU.mult)\
                       .then_inc(s["att_ready"], 1)

                def residual(n, ch):
                    dve.wait_ge(s["y_ready"], n + 1)
                    ch.do(dve.tensor_tensor(x1[:], pY, bsum[:], ALU.add))
                    ch.do(dve.tensor_tensor(x1[:], x1[:], one(X, n), ALU.add))
                    ch.do(dve.tensor_copy(one(X, n), x1[:]))

                def tile(n, i, ahead, behind):
                    ch = Chain(dve, s["b_chain"])
                    if ahead:
                        dve.wait_ge(s["qe_turned"], n + 1)
                        copy_q(n + 1, i + 1)
                    for h in range(HEADS):
                        if ahead:
                            maximum(n + 1, h, pS[:])
                        if behind and h == 1:
                            divide(n - 1, ch)
                        if behind and h == 7:
                            residual(n - 1, ch)
                        if behind and h == 8:
                            statistics(dve, ch, x1[:])
                        if behind and h == 9:
                            newton(dve, ch, rs[:], ve[:], nt_[:], 2)
                        if behind and h == 10:
                            newton(dve, ch, rs[:], ve[:], nt_[:], 1)
                            normalized(dve, x1[:], xn2[:]).then_inc(s["xn2_ready"], 1)
                    if ahead:
                        add_maxima(n + 1, ch)
                    if behind:
                        dve.wait_ge(s["xn2_turned"], n)
                        dve.sem_inc(s["passed"], 1)
                        ch.close()

                first, last = b * NT, b * NT + NT - 1
                ch = Chain(dve, s["b_chain"])
                copy_q(first, 0)
                for h in range(HEADS):
                    maximum(first, h, (pS[:], pE2)[h % 2])
                add_maxima(first, ch)
                ch.close()
                tile(first, 0, True, False)
                with dve.Fori(1, NT - 1) as i:
                    tile(b * NT + i, i, True, True)
                tile(last, NT - 1, False, True)
                ch = Chain(dve, s["b_chain"])
                divide(last, ch)
                residual(last, ch)
                statistics(dve, ch, x1[:])
                newton(dve, ch, rs[:], ve[:], nt_[:], 3)
                normalized(dve, x1[:], xn2[:]).then_inc(s["xn2_ready"], 1)
                ch.close()
                dve.wait_ge(s["xn2_turned"], (b + 1) * NT)
                dve.sem_inc(s["passed"], 1)

def l1_attn_phase(nc, io, keep):
    ident, X, XA = keep["ident"], keep["X"], keep["XA"]
    with ExitStack() as ctx:
        sem = lambda n: ctx.enter_context(nc.semaphore(n))
        sb = lambda n, s, d=F32: ctx.enter_context(nc.sbuf_tensor(n, s, d))
        ps = lambda n, s, d=F32: ctx.enter_context(nc.psum_tensor(n, s, d))

        W5 = sb("W5", [P, 5, INNER])
        wb = sb("wb", [P, HEADS])
        wo = sb("wo1", [P, NCH, C])
        brow, btmp = sb("brow1", [96, 2, INNER]), sb("btmp1", [96, 2, INNER], BF16)
        bparts = sb("bparts1", [96, 2, INNER], BF16)
        ones = sb("ones1", [96, P], BF16)
        alog, neA = sb("alog", [P, HEADS]), sb("neA", [P, HEADS])
        alogF, neAF = sb("alogF", [P, NCH]), sb("neAF", [P, NCH])
        dist, before = sb("dist", [P, P]), sb("before", [P, P])
        trow, rev = sb("trow", [P, P]), sb("rev", [P, 1])
        nw = sb("nw", [P, D1])
        Dec = sb("Dec", [P, 2, NCH, P])
        decT = sb("decT", [P, NCH, P])
        A128 = sb("A128", [P, NCH])
        kdec = sb("kdec", [P, HEADS])
        xT = sb("xT1", [P, P])
        qs, ks, vs = sb("qs1", [P, INNER]), sb("ks1", [P, INNER]), sb("vs1", [P, INNER])
        fs, gs = sb("fs1", [P, INNER]), sb("gs1", [P, INNER])
        sqa, sqb, sqo = (sb(n, [P, INNER]) for n in ("sqa1", "sqb1", "sqo1"))
        stays = sb("stays1", [P, NT])
        bt, bv = sb("bt1", [P, HEADS]), sb("bv1", [P, HEADS])
        so, ro = sb("so1", [P, HEADS]), sb("ro1", [P, HEADS])
        ss, rr, tn = sb("ss1", [P, 2 * HEADS]), sb("rr1", [P, 2 * HEADS]), sb("tn1", [P, 2 * HEADS])
        qT, kT, qdT = sb("qT1", [P, NCH, P]), sb("kT1", [P, NCH, P]), sb("qdT1", [P, NCH, P])
        vp, kp = sb("vp1", [P, INNER]), sb("kp1", [P, INNER])
        Wd = sb("Wd1", [P, 2, NCH, P])
        St, StA = sb("St", [P, NCH, D1]), sb("StA", [P, NCH, D1])
        o1, oT = sb("o1", [P, INNER]), sb("oT1", [P, NCH, P])

        PA, PB = ps("PA1", [P, 2, 512]), ps("PB1", [P, 2, 512])
        PC, PD = ps("PC1", [P, 2, 512]), ps("PD1", [P, 2, 512])
        tiles = lambda t: t[:].rearrange("p a (c t) -> p (a c) t", t=P)
        heads = lambda t: t.rearrange("p (h d) -> p h d", d=D1)
        wide = lambda t: t.unsqueeze(2).broadcast_to([P, HEADS, D1])
        o_feat = PA[:].rearrange("p a (c d) -> p c a d", d=D1)
        feat4 = lambda t: t.rearrange("p (c a d) -> p c a d", a=2, d=D1)

        names = ["w_in", "passed", "bias_ready", "t_chain", "t_exp", "v_chain", "x_kept", "q_ready",
                 "k_ready", "v_ready", "b_ready", "f_ready", "g_ready", "q_kept", "k_kept", "v_kept",
                 "b_kept", "f_kept", "g_kept", "sqq", "sqk", "r_ready", "q_turned", "k_turned", "qT_kept",
                 "kT_kept", "qd_ready", "vp_ready", "kp_ready", "gq_ready", "gw_ready", "s_ready", "w_ready",
                 "o_ready", "st_ready", "st_kept", "o1_ready", "sqo", "o2_ready", "o_turned", "oT_kept",
                 "y_ready", "y_kept", "tables", "st_zeroed"]
        s = {n: sem("l1_" + n) for n in names}
        W_IN = 16 * 18
        TILES = B * NT
        block = ctx.enter_context(nc.Block())

        @block.sync
        def _(sp):
            load = lambda dst, src: sp.dma_start(dst, src).then_inc(s["w_in"], 16)
            for k, n in enumerate(("Wq", "Wk", "Wv", "Wf", "Wg")):
                load(W5[:, k, :], io["L1_attn_" + n])
            load(wb[:], io["L1_attn_Wb"])
            load(wo[:], io["L1_attn_Wo"].rearrange("(c p) n -> p c n", p=P))
            load(brow[:, 0, :], io["L1_attn_dt_bias"].partition_broadcast(96))
            load(brow[:, 1, :], io["L1_attn_bg"].partition_broadcast(96))
            load(alog[:], io["L1_attn_A_log"].partition_broadcast(P))
            pairs = io["L1_attn_A_log"].rearrange("(c a) -> a c", a=2)
            with nc.allow_non_contiguous_dma(reason="8 values"):
                load(alogF[0:D1, :], pairs[0].partition_broadcast(D1))
                load(alogF[D1:P, :], pairs[1].partition_broadcast(D1))
            load(nw[:], io["L1_attn_norm_w"].partition_broadcast(P))
            load(dist[:], io["dist"])
            load(before[:], io["before"])
            load(trow[:], io["trow"])
            load(rev[:], io["rev"])
            load(stays[:], io["stays"])

        @block.gpsimd
        def _(pool):
            pool.wait_ge(s["w_in"], W_IN)

            def tile(n, others):
                pool.wait_ge(s["k_kept"], 2 * n + 2)
                pool.sem_inc(s["passed"], 1)
                if others:
                    pool.wait_ge(s["st_ready"], n)
                    pool.sem_inc(s["passed"], 1)
                pool.tensor_tensor(heads(kp[:]), heads(ks[:]), wide(kdec[:]), ALU.mult).then_inc(s["kp_ready"], 1)
                pool.wait_ge(s["f_kept"], 2 * n + 2)
                pool.sem_inc(s["passed"], 1)
                pool.wait_ge(s["r_ready"], n + 1)
                pool.sem_inc(s["passed"], 1)
                pool.tensor_tensor(heads(fs[:]), heads(fs[:]), wide(rr[:, 0:HEADS]), ALU.mult)\
                    .then_inc(s["gq_ready"], 1)
                pool.wait_ge(s["g_kept"], 2 * n + 2)
                pool.sem_inc(s["passed"], 1)
                pool.tensor_tensor(heads(gs[:]), heads(gs[:]), nw[:].unsqueeze(1).broadcast_to([P, HEADS, D1]),
                                   ALU.mult).then_inc(s["gw_ready"], 1)

            tile(0, False)
            with pool.Fori(1, TILES) as n:
                tile(n, True)

        @block.scalar
        def _(act):
            act.wait_ge(s["w_in"], W_IN)
            act.activation(neA[:], alog[:], ACT.Exp).then_inc(s["t_exp"], 1)
            act.activation(neAF[:], alogF[:], ACT.Exp).then_inc(s["t_exp"], 1)
            act.wait_ge(s["t_chain"], 2)
            for h in range(HEADS):
                act.activation(Dec[:, h % 2, h // 2, :], dist[:], ACT.Exp, scale=neA[:, h:h + 1])\
                   .then_inc(s["t_exp"], 1)
            for c in range(NCH):
                act.activation(decT[:, c, :], trow[:], ACT.Exp, scale=neAF[:, c:c + 1])
            act.activation(A128[:], neAF[:], ACT.Exp, scale=float(P))
            act.activation(kdec[:], neA[:], ACT.Exp, scale=rev[:, 0:1]).then_inc(s["tables"], 1)

            def take_x(n, others):
                if others:
                    act.wait_ge(s["g_ready"], 2 * n)
                act.activation(xT[:], XA[:, bass.ds(n // NT, 1), bass.ds(1 + (n % NT) * P, P)]
                               .rearrange("p a t -> p (a t)"), ACT.Copy).then_inc(s["x_kept"], 1)

            def keep(n, dst, ready, kept, func):
                for a in range(2):
                    act.wait_ge(s[ready], 2 * n + a + 1)
                    act.activation(dst[:, a * 512:a * 512 + 512], PB[:, a, :], func).then_inc(s[kept], 1)

            def keep_turned(n, dst, src, ready, kept):
                act.wait_ge(s[ready], n + 1)
                act.activation(dst[:], tiles(src), ACT.Copy).then_inc(s[kept], 1)

            def squares(n, others):
                if others:
                    act.wait_ge(s["r_ready"], n)
                act.wait_ge(s["q_kept"], 2 * n + 2)
                act.activation(sqa[:], qs[:], ACT.Square).then_inc(s["sqq"], 1)
                act.wait_ge(s["k_kept"], 2 * n + 2)
                act.activation(sqb[:], ks[:], ACT.Square).then_inc(s["sqk"], 1)

            def gates(n, others):
                act.wait_ge(s["b_ready"], n + 1)
                act.activation(bt[:], PD[:, 1, 0:HEADS], ACT.Sigmoid).then_inc(s["b_kept"], 1)
                keep(n, fs, "f_ready", "f_kept", ACT.Sigmoid)
                if others:
                    act.wait_ge(s["o2_ready"], n)
                keep(n, gs, "g_ready", "g_kept", ACT.Sigmoid)

            def tile(n, ahead, behind):
                if ahead:
                    take_x(n + 1, True)
                keep_turned(n, qT, PC, "q_turned", "qT_kept")
                keep_turned(n, kT, PD, "k_turned", "kT_kept")
                if behind:
                    keep_turned(n - 1, oT, PA, "o_turned", "oT_kept")
                if ahead:
                    keep(n + 1, qs, "q_ready", "q_kept", ACT.Silu)
                    act.wait_ge(s["kp_ready"], n + 1)
                    keep(n + 1, ks, "k_ready", "k_kept", ACT.Silu)
                    squares(n + 1, True)
                    act.wait_ge(s["vp_ready"], n + 1)
                    keep(n + 1, vs, "v_ready", "v_kept", ACT.Silu)
                act.wait_ge(s["o1_ready"], n + 1)
                act.activation(sqo[:], o1[:], ACT.Square).then_inc(s["sqo"], 1)
                if ahead:
                    gates(n + 1, True)

            take_x(0, False)
            keep(0, qs, "q_ready", "q_kept", ACT.Silu)
            keep(0, ks, "k_ready", "k_kept", ACT.Silu)
            keep(0, vs, "v_ready", "v_kept", ACT.Silu)
            squares(0, False)
            gates(0, False)
            tile(0, True, False)
            with act.Fori(0, TILES // 2 - 1) as t:
                for k in range(1, 3):
                    tile(2 * t + k, True, True)
            tile(TILES - 1, False, True)
            keep_turned(TILES - 1, oT, PA, "o_turned", "oT_kept")

        @block.tensor
        def _(pe):
            pe.wait_ge(s["w_in"], W_IN)
            pe.wait_ge(s["t_chain"], 4)
            pe.wait_ge(s["bias_ready"], 1)
            pe.wait_ge(s["tables"], 1)

            def project(n, k, bias, done, free, parts=(0, 1)):
                for a in parts:
                    if free:
                        pe.wait_ge(s[free[0]], 2 * free[1] + a + 1)
                    r = slice(a * 512, a * 512 + 512)
                    mm = pe.matmul(PB[:, a, :], xT[:], W5[:, k, r], start=True, stop=(bias is None))
                    if bias is not None:
                        mm = pe.matmul(PB[:, a, :], ones[:], bparts[:, bias, r], start=False, stop=True)
                    mm.then_inc(s[done], 1)

            def turn(dst, src, done):
                for c in range(NCH):
                    mm = pe.transpose(tiles(dst)[:, c, :], src[:, c * P:c * P + P], ident[:])
                mm.then_inc(s[done], 1)

            def scores(n):
                pe.wait_ge(s["qT_kept"], n + 1)
                pe.wait_ge(s["kT_kept"], n + 1)
                pe.wait_ge(s["qd_ready"], n + 1)
                for j in range(2):
                    for c in range(4 * j, 4 * j + 4):
                        for a, bank in ((0, PC), (1, PD)):
                            r = slice(a * D1, a * D1 + D1)
                            mm = pe.matmul(tiles(bank)[:, c, :], kT[r, c, :], qT[r, c, :], start=True, stop=True)
                    mm.then_inc(s["s_ready"], 1)

            def output(n, c):
                for a in range(2):
                    r = slice(a * D1, a * D1 + D1)
                    h = 2 * c + a
                    pe.matmul(PA[:, a, c * D1:c * D1 + D1], Wd[:, a, c, :], vp[:, h * D1:h * D1 + D1],
                              start=True, stop=False)
                    mm = pe.matmul(PA[:, a, c * D1:c * D1 + D1], qdT[r, c, :], St[r, c, :],
                                   start=False, stop=True)
                if c == NCH - 1:
                    mm.then_inc(s["o_ready"], 1)

            def increment(n):
                pe.wait_ge(s["kp_ready"], n + 1)
                for c in range(NCH):
                    r = slice(c * P, c * P + P)
                    mm = pe.matmul(tiles(PC)[:, c, :], kp[:, r], vp[:, r], start=True, stop=True)
                mm.then_inc(s["st_ready"], 1)

            def turn_o(n):
                pe.wait_ge(s["o2_ready"], n + 1)
                turn(PA, o1, "o_turned")

            def out(n, c):
                mm = pe.matmul(PD[:, 0, 0:C], oT[:, c, :], wo[:, c, :], start=(c == 0), stop=(c == NCH - 1))
                if c == NCH - 1:
                    mm.then_inc(s["y_ready"], 1)

            def beta(n):
                pe.matmul(PD[:, 1, 0:HEADS], xT[:], wb[:], start=True, stop=True).then_inc(s["b_ready"], 1)

            def tile(n, ahead, behind):
                pe.wait_ge(s["k_kept"], 2 * n + 2)
                if behind:
                    pe.wait_ge(s["st_kept"], n)
                turn(PC, qs, "q_turned")
                pe.wait_ge(s["b_kept"], n + 1)
                if behind > 1:
                    pe.wait_ge(s["y_kept"], n - 1)
                turn(PD, ks, "k_turned")
                if behind:
                    turn_o(n - 1)
                if ahead:
                    pe.wait_ge(s["x_kept"], n + 2)
                    project(n + 1, 0, None, "q_ready", ("g_kept", n))
                scores(n)
                if ahead:
                    project(n + 1, 1, None, "k_ready", ("q_kept", n + 1))
                if behind:
                    pe.wait_ge(s["oT_kept"], n)
                pe.wait_ge(s["vp_ready"], n + 1)
                for c in range(NCH):
                    if c % 4 == 0:
                        pe.wait_ge(s["w_ready"], 2 * n + c // 4 + 1)
                    output(n, c)
                    if behind:
                        out(n - 1, c)
                    if ahead and c % 4 == 1:
                        project(n + 1, 2, None, "v_ready", ("k_kept", n + 1), (c // 4,))
                increment(n)
                if ahead:
                    beta(n + 1)
                    project(n + 1, 3, 0, "f_ready", ("v_kept", n + 1))
                    project(n + 1, 4, 1, "g_ready", ("f_kept", n + 1))

            pe.wait_ge(s["x_kept"], 1)
            project(0, 0, None, "q_ready", None)
            project(0, 1, None, "k_ready", ("q_kept", 0))
            project(0, 2, None, "v_ready", ("k_kept", 0))
            beta(0)
            project(0, 3, 0, "f_ready", ("v_kept", 0))
            project(0, 4, 1, "g_ready", ("f_kept", 0))
            tile(0, True, 0)
            tile(1, True, 1)
            with pe.Fori(0, TILES // 2 - 2) as t:
                for k in range(2, 4):
                    tile(2 * t + k, True, 2)
            tile(TILES - 2, True, 2)
            tile(TILES - 1, False, 2)
            turn_o(TILES - 1)
            pe.wait_ge(s["oT_kept"], TILES)
            for c in range(NCH):
                out(TILES - 1, c)

        @block.vector
        def _(dve):
            dve.wait_ge(s["w_in"], W_IN)
            dve.wait_ge(s["t_exp"], 2)
            dve.tensor_scalar(neA[:], neA[:], 1e30, -1.0, ALU.min, ALU.mult).then_inc(s["t_chain"], 1)
            dve.tensor_scalar(neAF[:], neAF[:], 1e30, -1.0, ALU.min, ALU.mult).then_inc(s["t_chain"], 1)
            dve.tensor_scalar(brow[:, 0, :], brow[:, 0, :], -1.0, None, ALU.mult).then_inc(s["t_chain"], 1)
            ch = Chain(dve, s["v_chain"])
            ch.mark(dve.memset(ones[:], 1.0))
            ch.do(dve.memset(bparts[:], 0.0))
            dve.wait_ge(s["t_chain"], 3)
            for r in (0, 32, 64):
                ch.do(dve.tensor_copy(btmp[:], brow[:]))
                ch.mark(dve.tensor_copy(bparts[r:r + 1], btmp[r:r + 1]))
                ch.do(dve.tensor_tensor(brow[:], brow[:], btmp[:], ALU.subtract))
            ch.close()
            dve.sem_inc(s["bias_ready"], 1)
            dve.wait_ge(s["t_exp"], 2 + HEADS)
            dec = Dec[:].rearrange("p a c t -> p (a c) t")
            dve.tensor_tensor(dec, dec, before[:].unsqueeze(1).broadcast_to([P, HEADS, P]), ALU.mult)\
               .then_inc(s["t_chain"], 1)
            dve.wait_ge(s["t_chain"], 4)
            dve.wait_ge(s["tables"], 1)
            dve.memset(St[:], 0.0).then_inc(s["st_zeroed"], 1)
            dve.wait_ge(s["st_zeroed"], 1)

            def sums(n, ch):
                dve.wait_ge(s["sqq"], n + 1)
                ch.mark(dve.tensor_reduce(ss[:, 0:HEADS], heads(sqa[:]), AX_X, ALU.add))
                dve.wait_ge(s["sqk"], n + 1)
                ch.do(dve.tensor_reduce(ss[:, HEADS:2 * HEADS], heads(sqb[:]), AX_X, ALU.add))
                ch.do(dve.tensor_scalar(ss[:], ss[:], L2_TINY, None, ALU.max))
                rsqrt_start(dve, ch, rr[:], ss[:])

            def norms(n, ch):
                newton(dve, ch, rr[:], ss[:], tn[:], 3)
                dve.wait_ge(s["b_kept"], n + 1)
                dve.tensor_tensor(bv[:], bt[:], rr[:, HEADS:2 * HEADS], ALU.mult).then_inc(s["r_ready"], 1)
                dve.wait_ge(s["r_ready"], n + 1)
                dve.wait_ge(s["v_kept"], 2 * n + 2)
                dve.tensor_tensor(heads(vp[:]), heads(vs[:]), wide(bv[:]), ALU.mult).then_inc(s["vp_ready"], 1)

            def add_y(n):
                dve.wait_ge(s["y_ready"], n + 1)
                dve.tensor_tensor(one(X, n), PD[:, 0, 0:C], one(X, n), ALU.add).then_inc(s["y_kept"], 1)

            def tile(n, i, ahead, behind):
                ch = Chain(dve, s["v_chain"])
                goes_on = stays[:, bass.ds((i + NT - 1) % NT, 1)]
                dve.wait_ge(s["q_turned"], n + 1)
                dve.wait_ge(s["qT_kept"], n + 1)
                dve.scalar_tensor_tensor(out=qdT[:], in0=tiles(PC), scalar=goes_on, in1=decT[:],
                                         op0=ALU.mult, op1=ALU.mult).then_inc(s["qd_ready"], 1)
                norms(n, ch)
                for j in range(2):
                    q = slice(4 * j, 4 * j + 4)
                    dve.wait_ge(s["s_ready"], 2 * n + j + 1)
                    for a in range(2):
                        ins = dve.tensor_tensor(Wd[:, a, q, :], tiles((PC, PD)[a])[:, q, :], Dec[:, a, q, :], ALU.mult)
                    ins.then_inc(s["w_ready"], 1)
                ch.mark(dve.scalar_tensor_tensor(out=StA[:], in0=St[:], scalar=goes_on,
                                                 in1=A128[:].unsqueeze(2).broadcast_to([P, NCH, D1]),
                                                 op0=ALU.mult, op1=ALU.mult))
                dve.wait_ge(s["o_ready"], n + 1)
                dve.wait_ge(s["gq_ready"], n + 1)
                dve.tensor_tensor(feat4(o1[:]), o_feat, feat4(fs[:]), ALU.mult).then_inc(s["o1_ready"], 1)
                if behind:
                    add_y(n - 1)
                ch.after()
                dve.wait_ge(s["st_ready"], n + 1)
                dve.tensor_tensor(St[0:D1], StA[0:D1], tiles(PC)[0:D1, :, 0:D1], ALU.add)
                dve.tensor_tensor(St[D1:P], StA[D1:P], tiles(PC)[D1:P, :, D1:P], ALU.add).then_inc(s["st_kept"], 1)
                dve.wait_ge(s["sqo"], n + 1)
                ch.do(dve.tensor_reduce(so[:], heads(sqo[:]), AX_X, ALU.add))
                ch.do(dve.tensor_scalar(so[:], so[:], 1.0 / D1, RMS_EPS, ALU.mult, ALU.add))
                rsqrt(dve, ch, ro[:], so[:], tn[:, 0:HEADS])
                ch.do(dve.tensor_tensor(heads(o1[:]), heads(o1[:]), wide(ro[:]), ALU.mult))
                dve.wait_ge(s["gw_ready"], n + 1)
                dve.tensor_tensor(o1[:], o1[:], gs[:], ALU.mult).then_inc(s["o2_ready"], 1)
                if ahead:
                    sums(n + 1, ch)
                dve.wait_ge(s["st_kept"], n + 1)
                dve.sem_inc(s["passed"], 1)
                ch.close()

            ch = Chain(dve, s["v_chain"])
            sums(0, ch)
            ch.close()
            tile(0, 0, True, False)
            with dve.Fori(0, TILES // 2 - 1) as t:
                for k in range(1, 3):
                    tile(2 * t + k, 2 * t + k, True, True)
            tile(TILES - 1, TILES - 1, False, True)
            add_y(TILES - 1)


def l1_ffn_phase(nc, io, keep):
    ident, identb, XA, XB = keep["ident"], keep["identb"], keep["XA"], keep["XB"]
    with ExitStack() as ctx:
        sem = lambda n: ctx.enter_context(nc.semaphore(n))
        sb = lambda n, s, d=F32: ctx.enter_context(nc.sbuf_tensor(n, s, d))
        ps = lambda n, s, d=F32: ctx.enter_context(nc.psum_tensor(n, s, d))

        Wqkv = sb("Wqkv", [P, 3 * INNER])
        Wo = sb("Wo", [P, NCH, C])
        qsc, ksc = sb("qsc", [P, D1]), sb("ksc", [P, D1])
        rot = {k: sb(k, [P, NT, D1]) for k in ("cos_q", "sin_q", "cos_k", "sin_k")}
        tab = {k: sb("t_" + k, [P, NT, D1]) for k in rot}
        mask = sb("mask", [P, NT, 2 * KEYS], BF16)
        stays = sb("stays", [P, NT])
        W1 = sb("W1", [P, 2 * FFN])
        W2 = sb("W2", [P, 3, C])
        lng, lnb, b2 = sb("lng", [P, 1]), sb("lnb", [P, 1]), sb("b2", [P, 1])
        b1 = sb("b1", [P, 6])
        warm = sb("warm", [P, 1])
        xs = sb("xs", [P, P])
        q0, k0 = sb("q0", [P, INNER]), sb("k0", [P, INNER])
        t2q, t2k = sb("t2q", [P, INNER]), sb("t2k", [P, INNER])
        sqa, sqb = sb("sqa", [P, INNER]), sb("sqb", [P, INNER])
        qr, kr = sb("qr", [P, INNER]), sb("kr", [P, INNER])
        ss, rr, tn = sb("ss", [P, 2 * HEADS]), sb("rr", [P, 2 * HEADS]), sb("tn", [P, 2 * HEADS])
        rq8 = sb("rq8", [P, HEADS])
        qT = sb("qT", [P, NCH, P])
        kT = sb("kT", [P, NCH, KEYS])
        V, VL = sb("V", [P, 2, INNER]), sb("VL", [WINDOW, 2, INNER])
        mx, nb, den, rden = (sb(n, [P, HEADS]) for n in ("mx", "nb", "den", "rden"))
        Pr = sb("Pr", [P, 2, 4, KEYS])
        PT, PL = sb("PTs", [P, 2, 4, P]), sb("PLs", [WINDOW, 2, 4, WINDOW])
        on, oT = sb("on", [P, INNER]), sb("oT", [P, NCH, P])
        xf = sb("xf", [P, FTOK])
        st, mv = sb("st", [P, 4, 6]), sb("mv", [P, 4, 2])
        ve, rs, tv = sb("ve", [P, 4]), sb("rs", [P, 4]), sb("tv", [P, 4])
        xn, xnT = sb("xn", [P, 4, P]), sb("xnT", [P, FTOK])
        G, H = sb("G", [P, 3, FTOK]), sb("H", [P, 3, FTOK])

        PS, PO, PR = ps("PS", [P, 2, 512]), ps("PO", [P, 2, 512]), ps("PR", [P, 2, 512])
        PT1, PM = ps("PT1", [P, 512]), ps("PM", [P, 512])
        tiles = lambda t: t[:].rearrange("p a (c t) -> p (a c) t", t=P)
        heads = lambda t: t.rearrange("p (h d) -> p h d", d=D1)
        halves = lambda t: t.rearrange("p (h a j) -> p h a j", a=2, j=D1 // 2)
        wide = lambda t: t.unsqueeze(2).broadcast_to([P, HEADS, D1])
        yA = PM[:, P:2 * P]
        turned_p = PT1[:].rearrange("p (h t) -> p h t", t=P)
        turned_l = PM[0:WINDOW, 0:4 * WINDOW].rearrange("p (h t) -> p h t", t=WINDOW)
        fbank = [PS[:, 0, :], PS[:, 1, :], PO[:, 0, :], PO[:, 1, :], PR[:, 0, :], PR[:, 1, :]]
        fturn, fturn2, fout = PT1[:], PM[:], fbank[3]
        hh = D1 // 2

        names = ["consts", "passed", "tabs_ready", "warmed", "aw_in", "fw_in", "first", "v_chain", "f_chain",
                 "xs_ready", "q_ready", "k_ready", "v_ready", "q0_kept", "k0_kept", "q_squared", "k_squared",
                 "q_cos", "q_sin", "k_cos", "k_sin", "qr_ready", "ks_ready", "kr_ready", "v_kept",
                 "q_turned", "k_turned", "qT_kept", "kT_kept", "tail_kept", "s_ready", "nb_ready",
                 "exp_done", "p_turned", "p_kept", "o_ready", "on_ready", "o_turned", "oT_kept", "y_ready",
                 "xb_kept", "xf_ready", "xf_turned", "xn_ready", "xn_turned", "xnT_kept", "hg_ready",
                 "g_ready", "h_ready", "yf_ready", "xa_kept"]
        s = {n: sem("f_" + n) for n in names}
        AW, FW = 16 * 4, 16 * 13
        TILES, BLOCKS = B * NT, B * T // FTOK
        block = ctx.enter_context(nc.Block())

        @block.sync
        def _(sp):
            for k in rot:
                sp.dma_start(rot[k][:], io[k]).then_inc(s["consts"], 16)
            sp.dma_start(mask[:], io["mask"]).then_inc(s["consts"], 16)
            sp.dma_start(stays[:], io["stays"]).then_inc(s["consts"], 16)

            def at(name, l):
                a = io["L1_ffn_" + name]
                a = a[bass.ds(l, 1)]
                return a.rearrange("a m n -> (a m) n") if len(a.shape) == 3 else a

            def attn_weights(l):
                load = lambda dst, src: sp.dma_start(dst, src).then_inc(s["aw_in"], 16)
                load(Wqkv[:], at("Wqkv", l))
                load(Wo[:], at("Wo", l).rearrange("(c p) n -> p c n", p=P))
                load(qsc[:], at("q_scale", l).broadcast_to([P, D1]))
                load(ksc[:], at("k_scale", l).broadcast_to([P, D1]))

            def ffn_weights(l):
                load = lambda dst, src: sp.dma_start(dst, src).then_inc(s["fw_in"], 16)
                load(W1[:], at("W1", l))
                for k, (f, m) in enumerate(FCH):
                    load(W2[0:m, k, :], at("W2", l)[f:f + m, :])
                with nc.allow_non_contiguous_dma(reason="a column of channels"):
                    col = lambda name, f, m: at(name, l)[:, f:f + m].rearrange("a m -> m a")
                    load(lng[:], col("ln_g", 0, C))
                    load(lnb[:], col("ln_b", 0, C))
                    load(b2[:], col("b2", 0, C))
                    for k, (f, m) in enumerate(FCH):
                        load(b1[0:m, k:k + 1], col("b1", f, m))
                        load(b1[0:m, 3 + k:4 + k], col("b1", FFN + f, m))

            attn_weights(0)
            ffn_weights(0)
            with sp.Fori(0, DEPTH - 1) as l:
                sp.wait_ge(s["xb_kept"], (l + 1) * TILES)
                attn_weights(l + 1)
                sp.wait_ge(s["xa_kept"], (l + 1) * BLOCKS + 1)
                ffn_weights(l + 1)

        @block.gpsimd
        def _(pool):
            pool.memset(kT[:], 0.0).then_inc(s["first"], 1)
            pool.memset(VL[:], 0.0).then_inc(s["first"], 1)
            pool.wait_ge(s["first"], 2)

            def shifted(dst, src, b, i, m, done, n):
                h = C // 2
                for k, (r, first) in enumerate(((slice(0, h), 1), (slice(h, C), 0))):
                    pool.tensor_copy(dst[r, :], src[r, bass.ds(b, 1), bass.ds(first + i * m, m)]
                                     .rearrange("p a t -> p (a t)")).then_inc(s[done], 1)
                    pool.wait_ge(s[done], 2 * n + k + 1)
                    pool.sem_inc(s["passed"], 1)

            with pool.Fori(0, DEPTH) as l:
                pool.wait_ge(s["xa_kept"], l * BLOCKS + 1)
                pool.sem_inc(s["passed"], 1)
                pool.wait_ge(s["tabs_ready"], l + 1)
                pool.sem_inc(s["passed"], 1)
                with pool.Fori(0, TILES) as t:
                    n = l * TILES + t
                    shifted(xs, XA, t // NT, t % NT, P, "xs_ready", n)
                    pool.wait_ge(s["q0_kept"], 2 * n + 2)
                    pool.sem_inc(s["passed"], 1)
                    pool.tensor_tensor(heads(qr[:]), heads(q0[:]), tab["cos_q"][:, bass.ds(t % NT, 1), :]
                                       .broadcast_to([P, HEADS, D1]), ALU.mult).then_inc(s["q_cos"], 1)
                    pool.wait_ge(s["q_cos"], n + 1)
                    pool.sem_inc(s["passed"], 1)
                    pool.wait_ge(s["q_sin"], n + 1)
                    pool.sem_inc(s["passed"], 1)
                    pool.tensor_tensor(qr[:], qr[:], t2q[:], ALU.add).then_inc(s["qr_ready"], 1)
                    pool.wait_ge(s["k0_kept"], 2 * n + 2)
                    pool.sem_inc(s["passed"], 1)
                    pool.tensor_tensor(heads(kr[:]), heads(k0[:]), tab["cos_k"][:, bass.ds(t % NT, 1), :]
                                       .broadcast_to([P, HEADS, D1]), ALU.mult).then_inc(s["k_cos"], 1)
                    pool.wait_ge(s["k_cos"], n + 1)
                    pool.sem_inc(s["passed"], 1)
                    pool.wait_ge(s["k_sin"], n + 1)
                    pool.sem_inc(s["passed"], 1)
                    pool.tensor_tensor(kr[:], kr[:], t2k[:], ALU.add).then_inc(s["ks_ready"], 1)
                    pool.wait_ge(s["v_ready"], 2 * n + 2)
                    pool.sem_inc(s["passed"], 1)
                    pool.wait_ge(s["ks_ready"], n + 1)
                    pool.sem_inc(s["passed"], 1)
                pool.wait_ge(s["xb_kept"], (l + 1) * TILES)
                pool.sem_inc(s["passed"], 1)
                with pool.Fori(0, B) as b:
                    with pool.Fori(0, T // FTOK) as i:
                        m = l * BLOCKS + b * (T // FTOK) + i
                        shifted(xf, XB, b, i, FTOK, "xf_ready", m)
                        pool.wait_ge(s["xf_turned"], m + 1)
                        pool.sem_inc(s["passed"], 1)

        @block.scalar
        def _(act):
            act.wait_ge(s["first"], 2)
            act.wait_ge(s["consts"], 16 * 6)
            with act.Fori(0, DEPTH) as l:
                act.activation(warm[:, 0:1], stays[:, 0:1], ACT.Exp).then_inc(s["warmed"], 1)
                act.wait_ge(s["warmed"], 2 * l + 1)

                def keep(a, dst, ready, done):
                    for k in range(2):
                        act.wait_ge(s[ready], 2 * a + k + 1)
                        act.activation(dst[:, 512 * k:512 * k + 512], PR[:, k, :], ACT.Copy).then_inc(s[done], 1)

                def keep_turned(n, dst, ready, done):
                    for k in range(2):
                        act.wait_ge(s[ready], 2 * n + k + 1)
                        act.activation(dst[:, 4 * k:4 * k + 4], PR[:, k, :].rearrange("p (c t) -> p c t", t=P),
                                       ACT.Copy).then_inc(s[done], 1)

                def square(a, src, kept, dst, done):
                    act.wait_ge(s[kept], 2 * a + 2)
                    act.activation(dst[:], src[:], ACT.Square).then_inc(s[done], 1)

                def exps(n, g):
                    act.wait_ge(s["nb_ready"], 4 * n + g + 1)
                    if g >= 2:
                        act.wait_ge(s["p_turned"], 4 * n + g - 1)
                    for j in range(4):
                        h = 4 * g + j
                        ins = act.activation(Pr[:, g % 2, j, :], PS[:, j % 2, (j // 2) * KEYS:(j // 2 + 1) * KEYS],
                                             ACT.Exp, bias=nb[:, h:h + 1], scale=rq8[:, h:h + 1],
                                             accum_out=den[:, h:h + 1])
                    ins.then_inc(s["exp_done"], 1)

                def tile(n, t, e, ahead, behind):
                    exps(n, 0)
                    if ahead:
                        if behind:
                            act.wait_ge(s["ks_ready"], n + 1)
                        keep(n + 1, q0, "q_ready", "q0_kept")
                        square(n + 1, q0, "q0_kept", sqa, "q_squared")
                    exps(n, 1)
                    if ahead:
                        keep(n + 1, k0, "k_ready", "k0_kept")
                        square(n + 1, k0, "k0_kept", sqb, "k_squared")
                    if behind:
                        keep_turned(n - 1, oT, "o_turned", "oT_kept")
                    exps(n, 2)
                    if ahead:
                        keep(n + 1, V[:, 1 - e, :], "v_ready", "v_kept")
                    if behind:
                        act.wait_ge(s["o_ready"], n)
                    act.activation(VL[:, e, :], V[P - WINDOW:P, e, :], ACT.Copy).then_inc(s["tail_kept"], 1)
                    if ahead:
                        keep_turned(n + 1, qT, "q_turned", "qT_kept")
                    exps(n, 3)
                    act.activation(kT[:, :, 0:WINDOW], kT[:, :, P:KEYS], ACT.Copy, scale=stays[:, bass.ds(t % NT, 1)])\
                       .then_inc(s["tail_kept"], 1)
                    act.wait_ge(s["tail_kept"], 2 * n + 2)
                    if ahead:
                        keep_turned(n + 1, kT[:, :, WINDOW:KEYS], "k_turned", "kT_kept")

                first, last = l * TILES, l * TILES + (TILES - 1)
                keep(first, q0, "q_ready", "q0_kept")
                square(first, q0, "q0_kept", sqa, "q_squared")
                keep(first, k0, "k_ready", "k0_kept")
                square(first, k0, "k0_kept", sqb, "k_squared")
                keep(first, V[:, 0, :], "v_ready", "v_kept")
                keep_turned(first, qT, "q_turned", "qT_kept")
                keep_turned(first, kT[:, :, WINDOW:KEYS], "k_turned", "kT_kept")
                tile(first, 0, 0, True, False)
                with act.Fori(0, TILES // 2 - 1) as t:
                    tile(l * TILES + 2 * t + 1, 2 * t + 1, 1, True, True)
                    tile(l * TILES + 2 * t + 2, 2 * t + 2, 0, True, True)
                tile(last, TILES - 1, 1, False, True)
                keep_turned(last, oT, "o_turned", "oT_kept")
                act.activation(warm[:, 0:1], stays[:, 0:1], ACT.Gelu).then_inc(s["warmed"], 1)
                act.wait_ge(s["warmed"], 2 * l + 2)
                act.wait_ge(s["fw_in"], (l + 1) * FW)

                def keep_xn(m):
                    act.wait_ge(s["xn_turned"], m + 1)
                    act.activation(xnT[:], fturn2, ACT.Identity, bias=lnb[:, 0:1], scale=lng[:, 0:1])\
                       .then_inc(s["xnT_kept"], 1)

                def gates(m, others):
                    for k, (f, w) in enumerate(FCH):
                        act.wait_ge(s["hg_ready"], 6 * m + k + 1)
                        if others:
                            act.wait_ge(s["h_ready"], 3 * m + k - 2)
                        act.activation(G[0:w, k, :], fbank[k][0:w, :], ACT.Gelu, bias=b1[0:w, 3 + k:4 + k])\
                           .then_inc(s["g_ready"], 1)

                keep_xn(l * BLOCKS)
                gates(l * BLOCKS, False)
                with act.Fori(1, BLOCKS) as t:
                    keep_xn(l * BLOCKS + t)
                    gates(l * BLOCKS + t, True)

        @block.tensor
        def _(pe):
            pe.wait_ge(s["consts"], 16 * 6)
            pe.wait_ge(s["first"], 2)

            with pe.Fori(0, DEPTH) as l:
                pe.wait_ge(s["aw_in"], (l + 1) * AW)
                pe.sem_inc(s["passed"], 1)

                def project(a, k, done, free):
                    for h in range(2):
                        if free:
                            pe.wait_ge(s[free[0]], 2 * free[1] + h + 1)
                        f = k * INNER + h * 512
                        pe.matmul(PR[:, h, :], xs[:], Wqkv[:, f:f + 512], start=True, stop=True)\
                            .then_inc(s[done], 1)

                def turn(src, done, free):
                    for h in range(2):
                        pe.wait_ge(s[free[0]], 2 * free[1] + h + 1)
                        for c in range(4 * h, 4 * h + 4):
                            mm = pe.transpose(PR[:, h, (c % 4) * P:(c % 4) * P + P], src[:, c * P:c * P + P], ident[:])
                        mm.then_inc(s[done], 1)

                def scores(n, i, g):
                    for a in range(2):
                        pe.matmul(PS[:, a, 0:2 * KEYS], identb[:],
                                  mask[:, bass.ds(i, 1), :].rearrange("p a k -> p (a k)"), start=True, stop=False)
                    for k in range(2):
                        c = 2 * g + k
                        for a in range(2):
                            r = slice(a * D1, a * D1 + D1)
                            mm = pe.matmul(PS[:, a, k * KEYS:k * KEYS + KEYS], qT[r, c, :], kT[r, c, :],
                                           start=False, stop=(k == 1))
                    mm.then_inc(s["s_ready"], 1)

                def turn_p(n, g):
                    for j in range(4):
                        pe.transpose(turned_p[:, j, :], Pr[:, g % 2, j, WINDOW:KEYS], ident[:])
                    for j in range(4):
                        mm = pe.transpose(turned_l[:, j, :], Pr[0:WINDOW, g % 2, j, 0:WINDOW],
                                          ident[0:WINDOW, 0:WINDOW])
                    mm.then_inc(s["p_turned"], 1)

                def values(n, e, g):
                    pe.wait_ge(s["p_kept"], 4 * n + g + 1)
                    for j in range(4):
                        f = slice((4 * g + j) * D1, (4 * g + j) * D1 + D1)
                        o = PO[:].rearrange("p a k -> p (a k)")
                        pe.matmul(o[:, f], PT[:, g % 2, j, :], V[:, e, f], start=True, stop=True)
                        mm = pe.matmul(o[0:WINDOW, f], PL[:, g % 2, j, :], VL[:, 1 - e, f],
                                       start=False, stop=True, skip_group_check=True)
                    if g == 3:
                        mm.then_inc(s["o_ready"], 1)

                def turn_o(n, free):
                    pe.wait_ge(s["on_ready"], n + 1)
                    turn(on, "o_turned", free)

                def output(n):
                    pe.wait_ge(s["oT_kept"], 2 * n + 2)
                    for c in range(NCH):
                        mm = pe.matmul(yA, Wo[:, c, :], oT[:, c, :], start=(c == 0), stop=(c == NCH - 1))
                    mm.then_inc(s["y_ready"], 1)

                def tile(n, i, e, ahead, behind):
                    pe.wait_ge(s["qT_kept"], 2 * n + 2)
                    pe.wait_ge(s["kT_kept"], 2 * n + 2)
                    scores(n, i, 0)
                    if behind:
                        values(n - 1, 1 - e, 3)
                    if ahead:
                        pe.wait_ge(s["xs_ready"], 2 * (n + 1) + 2)
                        project(n + 1, 0, "q_ready", ("kT_kept", n))
                    pe.wait_ge(s["exp_done"], 4 * n + 1)
                    scores(n, i, 1)
                    turn_p(n, 0)
                    if ahead:
                        project(n + 1, 1, "k_ready", ("q0_kept", n + 1))
                    pe.wait_ge(s["v_kept"], 2 * n + 2)
                    if behind:
                        pe.wait_ge(s["on_ready"], n)
                    values(n, e, 0)
                    pe.wait_ge(s["exp_done"], 4 * n + 2)
                    scores(n, i, 2)
                    if behind:
                        turn_o(n - 1, ("k0_kept", n + 1) if ahead else ("kT_kept", n))
                    turn_p(n, 1)
                    if ahead:
                        project(n + 1, 2, "v_ready", ("oT_kept", n - 1) if behind else ("k0_kept", n + 1))
                    pe.wait_ge(s["exp_done"], 4 * n + 3)
                    scores(n, i, 3)
                    if ahead:
                        pe.wait_ge(s["qr_ready"], n + 2)
                        turn(qr, "q_turned", ("v_kept", n + 1))
                    if behind:
                        pe.wait_ge(s["p_kept"], 4 * n + 2)
                        output(n - 1)
                    values(n, e, 1)
                    if behind:
                        pe.wait_ge(s["xb_kept"], n)
                    turn_p(n, 2)
                    if ahead:
                        pe.wait_ge(s["kr_ready"], n + 2)
                        turn(kr, "k_turned", ("qT_kept", n + 1))
                    values(n, e, 2)
                    pe.wait_ge(s["exp_done"], 4 * n + 4)
                    turn_p(n, 3)

                first, last = l * TILES, l * TILES + (TILES - 1)
                pe.wait_ge(s["xs_ready"], 2 * first + 2)
                project(first, 0, "q_ready", None)
                project(first, 1, "k_ready", ("q0_kept", first))
                project(first, 2, "v_ready", ("k0_kept", first))
                pe.wait_ge(s["qr_ready"], first + 1)
                turn(qr, "q_turned", ("v_kept", first))
                pe.wait_ge(s["kr_ready"], first + 1)
                turn(kr, "k_turned", ("qT_kept", first))
                tile(first, 0, 0, True, False)
                with pe.Fori(0, TILES // 2 - 1) as t:
                    tile(l * TILES + 2 * t + 1, (2 * t + 1) % NT, 1, True, True)
                    tile(l * TILES + 2 * t + 2, (2 * t + 2) % NT, 0, True, True)
                tile(last, NT - 1, 1, False, True)
                values(last, 1, 3)
                turn_o(last, ("oT_kept", last - 1))
                output(last)
                pe.wait_ge(s["fw_in"], (l + 1) * FW)
                pe.sem_inc(s["passed"], 1)
                pe.wait_ge(s["xb_kept"], (l + 1) * TILES)
                pe.sem_inc(s["passed"], 1)

                def turn_xf(m):
                    pe.wait_ge(s["xf_ready"], 2 * m + 2)
                    for c in range(4):
                        mm = pe.transpose(fturn[:, c * P:c * P + P], xf[:, c * P:c * P + P], ident[:])
                    mm.then_inc(s["xf_turned"], 1)

                def turn_xn(m):
                    pe.wait_ge(s["xn_ready"], m + 1)
                    for c in range(4):
                        mm = pe.transpose(fturn2[:, c * P:c * P + P], xn[:, c, :], ident[:])
                    mm.then_inc(s["xn_turned"], 1)

                def widen(m):
                    pe.wait_ge(s["xnT_kept"], m + 1)
                    for k in range(6):
                        if k == 3:
                            pe.wait_ge(s["xa_kept"], m + 1)
                        f, w = FCH[k % 3]
                        f += FFN if k < 3 else 0
                        pe.matmul(fbank[k][0:w, :], W1[:, f:f + w], xnT[:], start=True, stop=True)\
                          .then_inc(s["hg_ready"], 1)

                def narrow(m):
                    for k, (f, w) in enumerate(FCH):
                        pe.wait_ge(s["h_ready"], 3 * m + k + 1)
                        mm = pe.matmul(fout, W2[0:w, k, :], H[0:w, k, :], start=(k == 0), stop=(k == 2))
                    mm.then_inc(s["yf_ready"], 1)

                turn_xf(l * BLOCKS)
                turn_xn(l * BLOCKS)
                with pe.Fori(0, BLOCKS - 1) as t:
                    m = l * BLOCKS + t
                    turn_xf(m + 1)
                    widen(m)
                    turn_xn(m + 1)
                    narrow(m)
                widen(l * BLOCKS + BLOCKS - 1)
                narrow(l * BLOCKS + BLOCKS - 1)

        @block.vector
        def _(dve):
            dve.wait_ge(s["consts"], 16 * 6)
            dve.sem_inc(s["xa_kept"], 1)
            with dve.Fori(0, DEPTH) as l:
                dve.wait_ge(s["aw_in"], (l + 1) * AW)
                dve.sem_inc(s["passed"], 1)
                ch = Chain(dve, s["v_chain"])
                for k, sc in (("q", qsc), ("k", ksc)):
                    ch.mark(dve.tensor_tensor(tab["cos_" + k][:], rot["cos_" + k][:],
                                              sc[:].unsqueeze(1).broadcast_to([P, NT, D1]), ALU.mult))
                    for a in range(2):
                        r, o = slice(a * hh, a * hh + hh), slice((1 - a) * hh, (1 - a) * hh + hh)
                        ch.mark(dve.tensor_tensor(tab["sin_" + k][:, :, r], rot["sin_" + k][:, :, r],
                                                  sc[:, o].unsqueeze(1).broadcast_to([P, NT, hh]), ALU.mult))
                ch.close()
                dve.sem_inc(s["tabs_ready"], 1)

                def rotate(i, k, src, dst):
                    for e in range(2):
                        sn = tab["sin_" + k][:, bass.ds(i, 1), e * hh:e * hh + hh].broadcast_to([P, HEADS, hh])
                        ins = dve.tensor_tensor(halves(dst[:])[:, :, e, :], halves(src[:])[:, :, 1 - e, :], sn, ALU.mult)
                    return ins

                def rotate_q(a, i):
                    dve.wait_ge(s["q0_kept"], 2 * a + 2)
                    rotate(i, "q", q0, t2q).then_inc(s["q_sin"], 1)

                def rotate_k(a, i):
                    dve.wait_ge(s["k0_kept"], 2 * a + 2)
                    rotate(i, "k", k0, t2k).then_inc(s["k_sin"], 1)

                def norm_q(a, ch):
                    dve.wait_ge(s["q_squared"], a + 1)
                    ch.mark(dve.tensor_reduce(ss[:, 0:HEADS], heads(sqa[:]), AX_X, ALU.add))

                def norm_k(a, ch):
                    dve.wait_ge(s["k_squared"], a + 1)
                    ch.mark(dve.tensor_reduce(ss[:, HEADS:2 * HEADS], heads(sqb[:]), AX_X, ALU.add))

                def norms(ch):
                    ch.after()
                    ch.do(dve.tensor_scalar(ss[:], ss[:], L2_TINY, None, ALU.max))
                    rsqrt_start(dve, ch, rr[:], ss[:])

                def scale_k(a):
                    dve.wait_ge(s["ks_ready"], a + 1)
                    dve.tensor_tensor(heads(kr[:]), heads(kr[:]), wide(rr[:, HEADS:2 * HEADS]), ALU.mult)\
                        .then_inc(s["kr_ready"], 1)

                def keep_scales(ch):
                    ch.do(dve.tensor_scalar(rq8[:], rr[:, 0:HEADS], QK_SCALE, None, ALU.mult))

                def maxima(n, g, ch):
                    dve.wait_ge(s["s_ready"], 4 * n + g + 1)
                    q = slice(4 * g, 4 * g + 4)
                    ch.do(dve.tensor_reduce(mx[:, q].rearrange("p (c a) -> p a c", a=2),
                                            PS[:, :, 0:2 * KEYS].rearrange("p a (c j) -> p a c j", j=KEYS),
                                            AX_X, ALU.max))
                    dve.scalar_tensor_tensor(out=nb[:, q], in0=mx[:, q], scalar=-1.0, in1=rq8[:, q],
                                             op0=ALU.mult, op1=ALU.mult).then_inc(s["nb_ready"], 1)

                def keep_p(n, g, ch):
                    dve.wait_ge(s["p_turned"], 4 * n + g + 1)
                    ch.mark(dve.tensor_copy(PL[:, g % 2], turned_l))
                    ch.after()
                    dve.tensor_copy(PT[:, g % 2], turned_p).then_inc(s["p_kept"], 1)

                def divide(n):
                    dve.wait_ge(s["o_ready"], n + 1)
                    dve.tensor_tensor(heads(on[:]), PO[:].rearrange("p a (h d) -> p (a h) d", d=D1), wide(rden[:]),
                                      ALU.mult).then_inc(s["on_ready"], 1)

                def output(n, t):
                    dve.wait_ge(s["y_ready"], n + 1)
                    here = lambda x: x[:, bass.ds(t // NT, 1), bass.ds(1 + (t % NT) * P, P)].rearrange("p a t -> p (a t)")
                    dve.tensor_tensor(here(XB), yA, here(XA), ALU.add).then_inc(s["xb_kept"], 1)

                def tile(n, t, ahead, behind):
                    ch = Chain(dve, s["v_chain"])
                    maxima(n, 0, ch)
                    i = (t + 1) % NT
                    if behind:
                        divide(n - 1)
                    maxima(n, 1, ch)
                    keep_p(n, 0, ch)
                    if ahead:
                        rotate_q(n + 1, i)
                    if ahead:
                        norm_q(n + 1, ch)
                        rotate_k(n + 1, i)
                    maxima(n, 2, ch)
                    if ahead:
                        norm_k(n + 1, ch)
                    keep_p(n, 1, ch)
                    if ahead:
                        norms(ch)
                        newton(dve, ch, rr[:], ss[:], tn[:], 2)
                    maxima(n, 3, ch)
                    if ahead:
                        newton(dve, ch, rr[:], ss[:], tn[:], 1)
                        scale_k(n + 1)
                    if behind:
                        output(n - 1, t - 1)
                    keep_p(n, 2, ch)
                    keep_p(n, 3, ch)
                    if ahead:
                        keep_scales(ch)
                    ch.do(dve.reciprocal(rden[:], den[:]))

                first, last = l * TILES, l * TILES + (TILES - 1)
                rotate_q(first, 0)
                rotate_k(first, 0)
                ch = Chain(dve, s["v_chain"])
                norm_q(first, ch)
                norm_k(first, ch)
                norms(ch)
                newton(dve, ch, rr[:], ss[:], tn[:], 3)
                scale_k(first)
                keep_scales(ch)
                tile(first, 0, True, False)
                with dve.Fori(0, TILES // 2 - 1) as t:
                    for k in range(1, 3):
                        tile(l * TILES + 2 * t + k, 2 * t + k, True, True)
                tile(last, TILES - 1, False, True)
                divide(last)
                output(last, TILES - 1)
                dve.wait_ge(s["fw_in"], (l + 1) * FW)
                dve.sem_inc(s["passed"], 1)

                def norm(m, ch, others):
                    dve.wait_ge(s["xf_turned"], m + 1)
                    for c in range(4):
                        ch.mark(dve.bn_stats(st[:, c, :], fturn[:, c * P:c * P + P]))
                    ch.after()
                    for c in range(4):
                        ch.mark(dve.bn_aggr(mv[:, c, :], st[:, c, :]))
                    ch.after()
                    ch.do(dve.tensor_scalar(ve[:].unsqueeze(2), mv[:, :, 1:2], LN_EPS, None, ALU.add))
                    rsqrt(dve, ch, rs[:], ve[:], tv[:])
                    if others:
                        dve.wait_ge(s["xn_turned"], m)
                    for c in range(4):
                        ins = dve.tensor_scalar(xn[:, c, :], fturn[:, c * P:c * P + P], mv[:, c, 0:1],
                                                rs[:, c:c + 1], ALU.subtract, ALU.mult)
                    ins.then_inc(s["xn_ready"], 1)

                def gated(m, others):
                    for k, (f, w) in enumerate(FCH):
                        dve.wait_ge(s["hg_ready"], 6 * m + k + 4)
                        dve.wait_ge(s["g_ready"], 3 * m + k + 1)
                        if others:
                            dve.wait_ge(s["yf_ready"], m)
                        dve.scalar_tensor_tensor(out=H[0:w, k, :], in0=fbank[3 + k][0:w, :], scalar=b1[0:w, k:k + 1],
                                                 in1=G[0:w, k, :], op0=ALU.add, op1=ALU.mult)\
                           .then_inc(s["h_ready"], 1)

                def add(m, t):
                    dve.wait_ge(s["yf_ready"], m + 1)
                    each = T // FTOK
                    here = lambda x: x[:, bass.ds(t // each, 1), bass.ds(1 + (t % each) * FTOK, FTOK)]\
                        .rearrange("p a t -> p (a t)")
                    dve.scalar_tensor_tensor(out=here(XA), in0=fout, scalar=b2[:, 0:1], in1=here(XB),
                                             op0=ALU.add, op1=ALU.add).then_inc(s["xa_kept"], 1)

                first, last = l * BLOCKS, l * BLOCKS + (BLOCKS - 1)
                ch = Chain(dve, s["f_chain"])
                norm(first, ch, False)
                norm(first + 1, ch, True)
                gated(first, False)
                add(first, 0)
                ch.close()
                with dve.Fori(1, BLOCKS - 1) as t:
                    ch = Chain(dve, s["f_chain"])
                    norm(l * BLOCKS + t + 1, ch, True)
                    gated(l * BLOCKS + t, True)
                    add(l * BLOCKS + t, t)
                    ch.close()
                gated(last, True)
                add(last, BLOCKS - 1)


def store_phase(nc, io, keep):
    ident, X, XA = keep["ident"], keep["X"], keep["XA"]
    with ExitStack() as ctx:
        sem = lambda n: ctx.enter_context(nc.semaphore(n))
        tile = ctx.enter_context(nc.sbuf_tensor("tile", [P, 2, 4, P], F32))
        turned = ctx.enter_context(nc.psum_tensor("turned", [P, 2, 512], F32))
        copied, ready, added, stored = (sem(n) for n in ("z_copied", "z_ready", "z_added", "z_stored"))
        block = ctx.enter_context(nc.Block())
        QUADS = B * NT // 4

        @block.scalar
        def _(act):
            for q in range(QUADS):
                if q >= 2:
                    act.wait_ge(ready, q - 1)
                b, t = q // 2, 1 + (q % 2) * 4 * P
                act.activation(tile[:, q % 2].rearrange("p c t -> p (c t)"), XA[:, b, t:t + 4 * P], ACT.Copy)\
                   .then_inc(copied, 1)

        @block.tensor
        def _(pe):
            for q in range(QUADS):
                pe.wait_ge(copied, q + 1)
                if q >= 2:
                    pe.wait_ge(added, q - 1)
                for c in range(4):
                    mm = pe.transpose(turned[:, q % 2, c * P:c * P + P], tile[:, q % 2, c, :], ident[:])
                mm.then_inc(ready, 1)

        @block.vector
        def _(dve):
            for q in range(QUADS):
                dve.wait_ge(ready, q + 1)
                here = X[:, 4 * q:4 * q + 4, :].rearrange("p n c -> p (n c)")
                dve.tensor_tensor(here, turned[:, q % 2, :], here, ALU.add).then_inc(added, 1)

        @block.sync
        def _(sp):
            for q in range(QUADS):
                sp.wait_ge(added, q + 1)
                t = (q % 2) * 4 * P
                sp.dma_start(io["out"][q // 2, t:t + 4 * P].rearrange("(n p) c -> p n c", p=P),
                             X[:, 4 * q:4 * q + 4, :]).then_inc(stored, 16)
            sp.wait_ge(stored, 16 * QUADS)


PHASES = [load_phase, l0_phase, l1_attn_phase, l1_ffn_phase, store_phase]


def build(nc, io):
    with ExitStack() as ctx:
        keep = {
            "ident": ctx.enter_context(nc.sbuf_tensor("ident", [P, P], F32)),
            "identb": ctx.enter_context(nc.sbuf_tensor("identb", [P, P], BF16)),
            "X": ctx.enter_context(nc.sbuf_tensor("X", [P, B * NT, C], F32)),
            "XA": ctx.enter_context(nc.sbuf_tensor("XA", [P, B, 1 + T], F32)),
            "XB": ctx.enter_context(nc.sbuf_tensor("XB", [P, B, 1 + T], F32)),
        }
        for phase in PHASES:
            phase(nc, io, keep)


def constants():
    import numpy as np

    f = np.float32
    half = D0 // 2
    theta = f(10000.0) ** (-np.arange(half, dtype=f) / f(half))
    freqs = np.arange(T, dtype=f)[:, None] * theta[None, :]
    tile = lambda a: np.ascontiguousarray(a.reshape(NT, P, -1).transpose(1, 0, 2))
    out = {"cos0": tile(np.cos(freqs).astype(f)), "sin0": tile(np.sin(freqs).astype(f))}
    hf = np.arange(0, D1, 2, dtype=f)
    inv = (f(1.0) / f(10000.0) ** (hf / f(D1))).astype(f)
    fr = np.arange(T, dtype=f)[:, None] * inv[None, :]
    fr = np.concatenate([fr, fr], -1)
    base = ((hf + f(0.4 * D1)) / f(1.4 * D1)).astype(f)
    power = (np.arange(T, dtype=f) - f(T // 2)) / f(WINDOW // 2)
    sc = (base[None, :] ** power[:, None]).astype(f)
    sc = np.concatenate([sc, sc], -1)
    sign = np.where(np.arange(D1) < D1 // 2, f(-1), f(1))[None, :]
    cos, sin = np.cos(fr).astype(f), np.sin(fr).astype(f) * sign
    for name, s in (("q", sc), ("k", (f(1.0) / sc).astype(f))):
        out["cos_" + name] = tile((cos * s).astype(f))
        out["sin_" + name] = tile((sin * s).astype(f))
    t = np.arange(P, dtype=f)
    out["dist"] = np.maximum(t[None, :] - 1 - t[:, None], 0)
    out["before"] = (t[:, None] < t[None, :]).astype(f)
    out["trow"] = np.tile(t[None, :], (P, 1))
    j, i = np.arange(KEYS)[None, :], np.arange(P)[:, None]
    seen = (j >= i) & (j <= i + WINDOW)
    first = seen & (j >= WINDOW)
    m = np.stack([first] + [seen] * (NT - 1), 1)
    m = np.where(m, f(0), f(MASKED))
    out["mask"] = np.concatenate([m, m], 2).astype(mybir.dt.np(BF16))
    out["stays"] = np.tile((np.arange(NT) < NT - 1).astype(f), (P, 1))
    out["rev"] = (P - 1 - t)[:, None]
    return out


def kernel(**inputs):
    import numpy as _np
    import concourse.bacc as _bacc
    from concourse import mybir as _mybir
    from concourse.bass_utils import run_bass_kernel_spmd as _run

    nc = _bacc.Bacc("TRN2", target_bir_lowering=False, num_devices=1)
    g = {k: _np.asarray(v) for k, v in inputs.items()}
    laid = {
        "x": g["L0_attn_x"],
        "wqkv0": _np.concatenate([g["L0_attn_Wq"].T, g["L0_attn_Wk"].T, g["L0_attn_Wv"].T], 1),
        "woT0": g["L0_attn_Wo"].T,
        "w_ffn0": g["L0_ffn_weight"],
    }
    for k, v in g.items():
        if k.startswith(("L0_attn_b", "L0_ffn_bias", "L1_")):
            laid[k] = v
    laid.update(constants())
    arrays, io = {}, {}
    for name, a in laid.items():
        a = _np.ascontiguousarray(a)
        arrays[f"in_{name}_dram"] = a
        io[name] = nc.dram_tensor(f"in_{name}_dram", a.shape, _mybir.dt.from_np(a.dtype), kind="ExternalInput").ap()
    io["out"] = nc.dram_tensor("out_dram", (B, T, C), F32, kind="ExternalOutput").ap()
    build(nc, io)
    r = _run(nc, [arrays], core_ids=[0])
    return r.results[0]["out_dram"]
```
